# Optimizing a Trainium2 kernel written in Bass

```python
import numpy as np
import jax
import jax.numpy as jnp

def _softmax(x, axis=-1):
    return jax.nn.softmax(x, axis=axis)

def _gelu(x):
    return jax.nn.gelu(x, approximate=True)

def _silu(x):
    return jax.nn.silu(x)

def _sigmoid(x):
    return jax.nn.sigmoid(x)

def _layernorm(x, axis=-1, eps=1e-05):
    m = jnp.mean(x, axis=axis, keepdims=True)
    v = jnp.var(x, axis=axis, keepdims=True)
    return (x - m) / jnp.sqrt(v + eps)

def _scatter_add(tgt, idx, src, axis=0):
    return tgt.at[idx].add(src)

def _segment_sum(src, seg, n):
    return jax.ops.segment_sum(src, seg, n)
kernel_name = 'mk_xattn_ffn_d2_seqx_r8_f69663'

def setup_inputs(seed: int=0):
    np.random.seed(seed)
    _w = jnp.asarray

    def _rec_inputs():
        import jax
        import jax.numpy as jnp
        _rk = jax.random.key(seed)
        x = -0.0005146 + 1 * jax.random.normal(jax.random.fold_in(_rk, 1), (16, 128, 128), jnp.float32)
        _lenS = 128 - jax.random.randint(jax.random.fold_in(_rk, 7), (16,), 0, max(1, 128 // 4) + 1, jnp.int32)
        _lenS2 = 77 - jax.random.randint(jax.random.fold_in(_rk, 8), (16,), 0, max(1, 77 // 4) + 1, jnp.int32)
        _ctx_768P = jax.random.normal(jax.random.fold_in(_rk, 11), (16, 16, 96), jnp.float32)
        _ctx_768c = jax.random.dirichlet(jax.random.fold_in(_rk, 511), 0.3 * jnp.ones((16,), jnp.float32), (16, 77))
        _ctx_768t = jnp.einsum('bsk,bkd->bsd', _ctx_768c, _ctx_768P)
        _ctx_768t = _ctx_768t * jax.lax.rsqrt(jnp.mean(jnp.square(_ctx_768t)) + 1e-12) * 0.953939
        ctx_768 = -0.00040386 + 0.999972 * (_ctx_768t + 0.3 * jax.random.normal(jax.random.fold_in(_rk, 611), (16, 77, 96), jnp.float32))
        _validS = jnp.arange(128)[None, :] < _lenS[:, None]
        _validS2 = jnp.arange(77)[None, :] < _lenS2[:, None]
        _causal = jnp.tril(jnp.ones((128, 128), dtype=bool))
        mask_BxS2_bk0 = jnp.logical_not(jnp.broadcast_to(_validS2[:, :], (16, 77)))
        mask_BxS_bk0 = jnp.logical_not(jnp.broadcast_to(_validS[:, :], (16, 128)))
        return (x, ctx_768, mask_BxS2_bk0, mask_BxS_bk0)
    x, ctx_768, mask_BxS2_bk0, mask_BxS_bk0 = _rec_inputs()

    def _L0_xattn_setup():
        import jax, jax.numpy as jnp
        import numpy as np
        DIM_IN, DIM_LAT, DIM_HEAD = (96, 128, 64)
        INNER = max(DIM_LAT, DIM_IN)
        HEADS = INNER // DIM_HEAD
        SCALE = DIM_HEAD ** (-0.5)
        RMS_EPS = 1e-08
        LN_EPS = 1e-05

        def layernorm(x, g, b):
            mu = jnp.mean(x, axis=-1, keepdims=True)
            var = jnp.mean((x - mu) ** 2, axis=-1, keepdims=True)
            return (x - mu) * jax.lax.rsqrt(var + LN_EPS) * g + b

        def rmsnorm(x, gamma):
            norm = jnp.sqrt(jnp.sum(x * x, axis=-1, keepdims=True)) * x.shape[-1] ** (-0.5)
            return x / jnp.maximum(norm, RMS_EPS) * gamma
        key = jax.random.key(seed)
        ks = jax.random.split(key, 12)
        b, n, m = (4, 512, 64)
        x = jax.random.normal(ks[0], (b, n, DIM_IN), jnp.float32)
        latents = jax.random.normal(ks[1], (b, m, DIM_LAT), jnp.float32)
        mask = jax.random.randint(ks[2], (b, n), 0, 2).astype(bool)
        s = lambda k, sh, fan: jax.random.normal(k, sh, jnp.float32) * fan ** (-0.5)
        return {'x': x, 'latents': latents, 'mask': mask, 'ln_x_g': jnp.ones((DIM_IN,), jnp.float32), 'ln_x_b': jnp.zeros((DIM_IN,), jnp.float32), 'ln_l_g': jnp.ones((DIM_LAT,), jnp.float32), 'ln_l_b': jnp.zeros((DIM_LAT,), jnp.float32), 'qn_g': jnp.ones((DIM_HEAD,), jnp.float32), 'kn_g': jnp.ones((DIM_HEAD,), jnp.float32), 'Wq': s(ks[3], (INNER, DIM_LAT), DIM_LAT), 'Wkv': s(ks[4], (2 * INNER, DIM_IN), DIM_IN), 'Wlkv': s(ks[5], (2 * INNER, DIM_LAT), DIM_LAT), 'Wo': s(ks[6], (DIM_LAT, INNER), INNER), 'bo': jnp.zeros((DIM_LAT,), jnp.float32)}
    _L0_xattn_all = _L0_xattn_setup()
    _L0_xattn_in = {k: v for k, v in _L0_xattn_all.items() if k in ('ln_x_g', 'ln_x_b', 'ln_l_g', 'ln_l_b', 'qn_g', 'kn_g', 'Wq', 'Wkv', 'Wlkv', 'Wo', 'bo')}
    del _L0_xattn_all

    def _L0_ffn_setup():
        import jax, jax.numpy as jnp
        import numpy as np
        E = 16
        F_C = 2.0
        D = 128
        I = 4 * D
        IS = 2 * D
        B, S = (4, 128)
        key = jax.random.key(seed)
        ks = jax.random.split(key, 8)
        w = 0.02
        return {'hidden_states': jax.random.normal(ks[0], (B, S, D), dtype=jnp.float32), 'gate_w': jax.random.normal(ks[1], (E, D), dtype=jnp.float32) * w, 'Wg': jax.random.normal(ks[2], (E, I, D), dtype=jnp.float32) * w, 'Wu': jax.random.normal(ks[3], (E, I, D), dtype=jnp.float32) * w, 'Wd': jax.random.normal(ks[4], (E, D, I), dtype=jnp.float32) * w, 'Sg': jax.random.normal(ks[5], (IS, D), dtype=jnp.float32) * w, 'Su': jax.random.normal(ks[6], (IS, D), dtype=jnp.float32) * w, 'Sd': jax.random.normal(ks[7], (D, IS), dtype=jnp.float32) * w}
    _L0_ffn_all = _L0_ffn_setup()
    _L0_ffn_in = {k: v for k, v in _L0_ffn_all.items() if k in ('gate_w', 'Wg', 'Wu', 'Wd', 'Sg', 'Su', 'Sd')}
    del _L0_ffn_all

    def _L1_xattn_setup():
        import jax, jax.numpy as jnp
        import numpy as np
        NUM_HEADS = 16
        key = jax.random.key(seed)
        k1, k2, k3, k4, k5 = jax.random.split(key, 5)
        B, N, C = (4, 256, 128)
        N2, Cy = (128, 96)
        x = jax.random.normal(k1, (B, N, C), dtype=jnp.float32)
        y = jax.random.normal(k2, (B, N2, Cy), dtype=jnp.float32)
        pad_mask = jax.random.randint(k3, (B, N), 0, 2).astype(jnp.bool_)
        Wq = jax.random.normal(k4, (C, C), dtype=jnp.float32) * C ** (-0.5)
        Wkv = jax.random.normal(k5, (2 * C, Cy), dtype=jnp.float32) * Cy ** (-0.5)
        return {'x': x, 'y': y, 'pad_mask': pad_mask, 'Wq': Wq, 'Wkv': Wkv}
    _L1_xattn_all = _L1_xattn_setup()
    _L1_xattn_in = {k: v for k, v in _L1_xattn_all.items() if k in ('Wq', 'Wkv')}
    del _L1_xattn_all

    def _L1_ffn_setup():
        import jax, jax.numpy as jnp
        import numpy as np
        BLOCK = 32
        W_BITS = 4
        ACT_BITS = 16

        def act_qdq(x):
            qmax = 2.0 ** (ACT_BITS - 1) - 1.0
            scale = jnp.maximum(jnp.max(jnp.abs(x)) / qmax, 1e-12)
            return jnp.clip(jnp.round(x / scale), -qmax - 1.0, qmax) * scale

        def fixed_qdq_u16(x):
            scale = 1.0 / 65536.0
            return jnp.clip(jnp.round(x / scale), 0.0, 65535.0) * scale

        def lpbq_dequant(w):
            O, I = w.shape
            qmax = 2.0 ** (W_BITS - 1) - 1.0
            wb = w.reshape(O, I // BLOCK, BLOCK)
            s = jnp.maximum(jnp.max(jnp.abs(wb), axis=-1, keepdims=True) / qmax, 1e-12)
            wq = jnp.clip(jnp.round(wb / s), -qmax - 1.0, qmax) * s
            return wq.reshape(O, I)
        key = jax.random.key(seed)
        k1, k2, k3, k4 = jax.random.split(key, 4)
        B, S, H, I = (2, 512, 128, 384)
        x = jax.random.normal(k1, (B, S, H), jnp.float32)
        w_gate = jax.random.normal(k2, (I, H), jnp.float32) * 0.02
        w_up = jax.random.normal(k3, (I, H), jnp.float32) * 0.02
        w_down = jax.random.normal(k4, (H, I), jnp.float32) * 0.02
        return {'x': x, 'w_gate': w_gate, 'w_up': w_up, 'w_down': w_down}
    _L1_ffn_all = _L1_ffn_setup()
    _L1_ffn_in = {k: v for k, v in _L1_ffn_all.items() if k in ('w_gate', 'w_up', 'w_down')}
    del _L1_ffn_all
    return {'x': x, 'ctx_768': ctx_768, 'mask_BxS2_bk0': mask_BxS2_bk0, 'mask_BxS_bk0': mask_BxS_bk0, 'L0_xattn_ln_x_g': _L0_xattn_in['ln_x_g'], 'L0_xattn_ln_x_b': _L0_xattn_in['ln_x_b'], 'L0_xattn_ln_l_g': _L0_xattn_in['ln_l_g'], 'L0_xattn_ln_l_b': _L0_xattn_in['ln_l_b'], 'L0_xattn_qn_g': _L0_xattn_in['qn_g'], 'L0_xattn_kn_g': _L0_xattn_in['kn_g'], 'L0_xattn_Wq': _L0_xattn_in['Wq'], 'L0_xattn_Wkv': _L0_xattn_in['Wkv'], 'L0_xattn_Wlkv': _L0_xattn_in['Wlkv'], 'L0_xattn_Wo': _L0_xattn_in['Wo'], 'L0_xattn_bo': _L0_xattn_in['bo'], 'L0_ffn_gate_w': _L0_ffn_in['gate_w'], 'L0_ffn_Wg': _L0_ffn_in['Wg'], 'L0_ffn_Wu': _L0_ffn_in['Wu'], 'L0_ffn_Wd': _L0_ffn_in['Wd'], 'L0_ffn_Sg': _L0_ffn_in['Sg'], 'L0_ffn_Su': _L0_ffn_in['Su'], 'L0_ffn_Sd': _L0_ffn_in['Sd'], 'L1_xattn_Wq': _L1_xattn_in['Wq'], 'L1_xattn_Wkv': _L1_xattn_in['Wkv'], 'L1_ffn_w_gate': _L1_ffn_in['w_gate'], 'L1_ffn_w_up': _L1_ffn_in['w_up'], 'L1_ffn_w_down': _L1_ffn_in['w_down']}

def reference(x, ctx_768, mask_BxS2_bk0, mask_BxS_bk0, L0_xattn_ln_x_g, L0_xattn_ln_x_b, L0_xattn_ln_l_g, L0_xattn_ln_l_b, L0_xattn_qn_g, L0_xattn_kn_g, L0_xattn_Wq, L0_xattn_Wkv, L0_xattn_Wlkv, L0_xattn_Wo, L0_xattn_bo, L0_ffn_gate_w, L0_ffn_Wg, L0_ffn_Wu, L0_ffn_Wd, L0_ffn_Sg, L0_ffn_Su, L0_ffn_Sd, L1_xattn_Wq, L1_xattn_Wkv, L1_ffn_w_gate, L1_ffn_w_up, L1_ffn_w_down):
    import jax
    import jax.numpy as jnp

    def _L0_xattn_ref(x, latents, mask, ln_x_g, ln_x_b, ln_l_g, ln_l_b, qn_g, kn_g, Wq, Wkv, Wlkv, Wo, bo):
        import jax, jax.numpy as jnp
        import numpy as np
        DIM_IN, DIM_LAT, DIM_HEAD = (96, 128, 64)
        INNER = max(DIM_LAT, DIM_IN)
        HEADS = INNER // DIM_HEAD
        SCALE = DIM_HEAD ** (-0.5)
        RMS_EPS = 1e-08
        LN_EPS = 1e-05

        def layernorm(x, g, b):
            mu = jnp.mean(x, axis=-1, keepdims=True)
            var = jnp.mean((x - mu) ** 2, axis=-1, keepdims=True)
            return (x - mu) * jax.lax.rsqrt(var + LN_EPS) * g + b

        def rmsnorm(x, gamma):
            norm = jnp.sqrt(jnp.sum(x * x, axis=-1, keepdims=True)) * x.shape[-1] ** (-0.5)
            return x / jnp.maximum(norm, RMS_EPS) * gamma
        b, n, _ = x.shape
        m = latents.shape[1]
        xn = layernorm(x, ln_x_g, ln_x_b)
        ln = layernorm(latents, ln_l_g, ln_l_b)
        q = ln @ Wq.T
        kv = jnp.concatenate([xn @ Wkv.T, ln @ Wlkv.T], axis=1)
        k, v = (kv[..., :INNER], kv[..., INNER:])
        split_heads = lambda t: t.reshape(t.shape[0], t.shape[1], HEADS, DIM_HEAD).transpose(0, 2, 1, 3)
        q, k, v = (split_heads(q), split_heads(k), split_heads(v))
        qn = rmsnorm(q, qn_g) * SCALE
        kn = rmsnorm(k, kn_g)
        attn = jnp.einsum('bhid,bhjd->bhij', qn, kn)
        full_mask = jnp.pad(mask, ((0, 0), (0, m)), constant_values=True)
        attn = jnp.where(full_mask[:, None, None, :], attn, -jnp.finfo(attn.dtype).max)
        attn = jax.nn.softmax(attn, axis=-1)
        out = jnp.einsum('bhij,bhjd->bhid', attn, v)
        out = out.transpose(0, 2, 1, 3).reshape(b, m, INNER)
        return out @ Wo.T + bo

    def _L0_ffn_ref(hidden_states, gate_w, Wg, Wu, Wd, Sg, Su, Sd):
        import jax, jax.numpy as jnp
        import numpy as np
        E = 16
        F_C = 2.0
        D = 128
        I = 4 * D
        IS = 2 * D
        B, S = (4, 128)
        b, s, d = hidden_states.shape
        T = b * s
        C = int(T * F_C / E)
        flat_x = hidden_states.reshape(T, d)
        logits = flat_x @ gate_w.T
        scores = jax.nn.softmax(logits, axis=-1).T
        topk_weight, topk_idx = jax.lax.top_k(scores, C)
        xg = flat_x[topk_idx]
        g = jnp.einsum('ecd,eid->eci', xg, Wg)
        u = jnp.einsum('ecd,eid->eci', xg, Wu)
        h = jax.nn.gelu(g, approximate=False) * u
        eo = jnp.einsum('eci,edi->ecd', h, Wd)
        eo = eo * topk_weight[..., None]
        flat_out = jnp.zeros_like(flat_x).at[topk_idx.reshape(-1)].add(eo.reshape(-1, d))
        out = flat_out.reshape(b, s, d)
        sg = hidden_states @ Sg.T
        su = hidden_states @ Su.T
        shared = jax.nn.gelu(sg, approximate=False) * su @ Sd.T
        return out + shared

    def _L1_xattn_ref(x, y, pad_mask, Wq, Wkv):
        import jax, jax.numpy as jnp
        import numpy as np
        NUM_HEADS = 16
        B, N, C = x.shape
        N2 = y.shape[1]
        H = NUM_HEADS
        d = C // H
        scale = d ** (-0.5)
        q = (x @ Wq.T).reshape(B, N, H, d).transpose(0, 2, 1, 3)
        kv = (y @ Wkv.T).reshape(B, N2, 2, H, d).transpose(2, 0, 3, 1, 4)
        k, v = (kv[0], kv[1])
        attn = jnp.einsum('bhnd,bhmd->bhnm', q * scale, k)
        attn = jnp.where(pad_mask[:, None, :, None], attn, jnp.float32(-1000000000.0))
        attn = jax.nn.softmax(attn, axis=-1)
        out = jnp.einsum('bhnm,bhmd->bhnd', attn, v)
        return out.transpose(0, 2, 1, 3).reshape(B, N, C)

    def _L1_ffn_ref(x, w_gate, w_up, w_down):
        import jax, jax.numpy as jnp
        import numpy as np
        BLOCK = 32
        W_BITS = 4
        ACT_BITS = 16

        def act_qdq(x):
            qmax = 2.0 ** (ACT_BITS - 1) - 1.0
            scale = jnp.maximum(jnp.max(jnp.abs(x)) / qmax, 1e-12)
            return jnp.clip(jnp.round(x / scale), -qmax - 1.0, qmax) * scale

        def fixed_qdq_u16(x):
            scale = 1.0 / 65536.0
            return jnp.clip(jnp.round(x / scale), 0.0, 65535.0) * scale

        def lpbq_dequant(w):
            O, I = w.shape
            qmax = 2.0 ** (W_BITS - 1) - 1.0
            wb = w.reshape(O, I // BLOCK, BLOCK)
            s = jnp.maximum(jnp.max(jnp.abs(wb), axis=-1, keepdims=True) / qmax, 1e-12)
            wq = jnp.clip(jnp.round(wb / s), -qmax - 1.0, qmax) * s
            return wq.reshape(O, I)
        x = act_qdq(x)
        up = act_qdq(x @ lpbq_dequant(w_up).T)
        gate = act_qdq(x @ lpbq_dequant(w_gate).T)
        sig = fixed_qdq_u16(jax.nn.sigmoid(gate))
        gate = act_qdq(gate * sig)
        o = act_qdq(gate * up)
        return o @ lpbq_dequant(w_down).T
    x = x + _L0_xattn_ref(ctx_768, _layernorm(x, axis=-1), mask_BxS2_bk0, L0_xattn_ln_x_g, L0_xattn_ln_x_b, L0_xattn_ln_l_g, L0_xattn_ln_l_b, L0_xattn_qn_g, L0_xattn_kn_g, L0_xattn_Wq, L0_xattn_Wkv, L0_xattn_Wlkv, L0_xattn_Wo, L0_xattn_bo)
    x = x + _L0_ffn_ref(_layernorm(x, axis=-1), L0_ffn_gate_w, L0_ffn_Wg, L0_ffn_Wu, L0_ffn_Wd, L0_ffn_Sg, L0_ffn_Su, L0_ffn_Sd)
    x = x + _L1_xattn_ref(_layernorm(x, axis=-1), ctx_768, mask_BxS_bk0, L1_xattn_Wq, L1_xattn_Wkv)
    x = x + _L1_ffn_ref(_layernorm(x, axis=-1), L1_ffn_w_gate, L1_ffn_w_up, L1_ffn_w_down)
    return x

_drawn_inputs = setup_inputs


def setup_inputs(seed=0):
    import zlib

    import numpy as np

    out = dict(_drawn_inputs(seed))
    spreads = {'L0_xattn_ln_x_g': (1.0, 0.6),
     'L0_xattn_ln_x_b': (0.0, 0.77),
     'L0_xattn_ln_l_g': (1.0, 0.2),
     'L0_xattn_ln_l_b': (0.0, 0.1),
     'L0_xattn_qn_g': (1.0, 0.6),
     'L0_xattn_kn_g': (1.0, 0.6),
     'L0_xattn_bo': (0.0, 0.1)}
    factors = {'L0_ffn_gate_w': 8.0,
     'L0_ffn_Wg': 8.0,
     'L0_ffn_Wu': 8.0,
     'L0_ffn_Wd': 8.0,
     'L0_ffn_Sg': 7.832,
     'L0_ffn_Su': 7.653,
     'L0_ffn_Sd': 7.672,
     'L1_ffn_w_gate': 6.078,
     'L1_ffn_w_up': 5.813,
     'L1_ffn_w_down': 5.877,
     'L1_xattn_Wq': 4.602}
    for name, (base, spread) in spreads.items():
        noise = np.random.default_rng([zlib.crc32(name.encode()), seed]).standard_normal(out[name].shape)
        drawn = base * np.exp(spread * noise) if base else spread * noise
        out[name] = jnp.asarray(drawn.astype(out[name].dtype))
    for name, factor in factors.items():
        out[name] = (out[name] * factor).astype(out[name].dtype)
    return out
```

```python
from contextlib import ExitStack

import concourse.bass as bass
import concourse.mybir as mybir

F32, BF16, F16, I32, U8 = (mybir.dt.float32, mybir.dt.bfloat16, mybir.dt.float16, mybir.dt.int32, mybir.dt.uint8)
ALU = mybir.AluOpType
ACT = mybir.ActivationFunctionType
AX = mybir.AxisListType

NB, T, D = 16, 128, 128
NT = NB * T
CK, CD = 77, 96
H0, DH0 = 2, 64
KEYS0 = CK + T
H1, DH1 = 16, 8
QUAD = 4
NE, CAP, IE = 16, 256, 512
NI = IE // 128
IS = 256
IQ = 384
NQ = IQ // 128
WBLOCK = 32
GROW = D + NE
LN_EPS, RMS_EPS = 1e-5, 1e-8
MASKED = -(2.0 ** 100)
ROUND = 1.5 * 2.0 ** 23
QMAX, WMAX, TINY = 32767.0, 7.0, 1e-12
BITS = 32


def live(b, n):
    return 0 <= b < n if isinstance(b, int) else True


def skewed(eng, n, lag, body, unroll=1):
    for i in range(lag):
        body(i, i % unroll)
    with eng.Fori(lag // unroll, n // unroll) as g:
        for u in range(unroll):
            body(g * unroll + u, u)
    for i in range(n, n + lag):
        body(i, i % unroll)


def build(nc, d, last_phase=9):
    with ExitStack() as ctx:
        def sb(name, shape, dt=F32):
            return ctx.enter_context(nc.sbuf_tensor(name, shape, dt))

        def sem(name):
            return ctx.enter_context(nc.semaphore(name))

        bank = [ctx.enter_context(nc.psum_tensor(f"bank{n}", [128, 512], F32)) for n in range(8)]

        x_all = sb("x_all", [128, NB, D])
        moments = sb("moments", [128, 2 * NB, 2])
        variance = sb("variance", [128, 2 * NB])
        deviation = sb("deviation", [128, 2 * NB])
        rstd = sb("rstd", [128, 2 * NB])
        shift = sb("shift", [128, 2 * NB])
        bn = sb("bn", [128, 2 * NB, 6])
        const = sb("const", [128, d["const"].shape[1]])
        const16 = sb("const16", [128, d["const16"].shape[1]], BF16)
        ident = const[:, 0:128]
        head_of_row = const[:, 128:132]
        bit_value = const[:, 132:132 + BITS]
        token_id = const[:, 164:180]
        first_batch = const[:, 180:436]
        before = const16[:, 0:128]
        ones16 = const16[:, 128:256]
        same_expert = const16[:, 256:384]
        iota1 = const16[:, 384:512]
        bit_int = sb("bit_int", [128, BITS], I32)
        stage = sb("stage", [128, 4096])

        def view(tensor, start, *shape):
            n = 1
            for s in shape:
                n *= s
            flat = tensor[:, start:start + n]
            if len(shape) == 1:
                return flat
            names = "abc"[:len(shape)]
            return flat.rearrange(f"p ({' '.join(names)}) -> p {' '.join(names)}",
                                  **{k: v for k, v in zip(names, shape)})

        loads = sem("loads")
        N_LOADS = [0]

        def load(eng, dst, src):
            eng.dma_start(dst, src).then_inc(loads, 16)
            N_LOADS[0] += 1

        w_token = sb("w_token", [128, 384])
        w_context = sb("w_context", [CD, 256])
        w_out = sb("w_out", [128, 128])
        bias_out = sb("bias_out", [128, 128])
        columns = sb("columns", [128, 8])
        wq1 = sb("wq1", [128, 128])
        wkv1 = sb("wkv1", [CD, 256])
        gate_w = sb("gate_w", [128, NE])
        shared_up = sb("shared_up", [128, 2, IS])
        shared_down = sb("shared_down", [128, 2, 128])
        wq4_in = sb("wq4_in", [128, 3, IQ])
        wq4 = sb("wq4", [128, 3, IQ])
        mask_q8 = sb("mask_q8", [128, NB], U8)
        mask_q = sb("mask_q", [128, NB])
        mask_k8 = sb("mask_k8", [1, NB * CK], U8)
        mask_k = sb("mask_k", [1, NB * CK], BF16)
        sig_all = sb("sig_all", [128, NQ * NT])
        context = sig_all[0:CK, NB * 256:NB * (256 + CD)].rearrange("k (b d) -> k b d", b=NB)
        context_t = sb("context_t", [CD, NB, CK])
        qkv = sb("qkv", [128, NB, 384])
        ctx_kv = sig_all[0:CK, 0:NB * 256].rearrange("k (b n) -> k b n", b=NB)
        keys1 = sb("keys1", [128, NB, CK])
        values1 = sb("values1", [CK, NB, H1, DH1 + 1])
        norms = sb("norms", [128, NB, 6])
        inv_norms = sb("inv_norms", [128, NB, 6])
        w_slots = sb("w_slots", [128, 2, 3, IE])

        memory_set = sem("memory_set")
        bn_done = sem("bn_done")
        var_ready = sem("var_ready")
        dev_ready = sem("dev_ready")
        rstd_ready = sem("rstd_ready")
        shift_ready = sem("shift_ready")
        q4_ready = sem("q4_ready")
        q4_transposed = sem("q4_transposed")
        gain_ready = sem("gain_ready")
        x_loaded = sem("x_loaded")
        ctx_loaded = sem("ctx_loaded")

        vector_chain = sem("vector_chain")
        linked = [0]

        def link(dve, instruction):
            linked[0] += 1
            instruction.then_inc(vector_chain, 1)
            dve.wait_ge(vector_chain, linked[0])

        q4_work = sb("q4_work", [128, 3 * IQ + 72])
        q4s = view(q4_work, 0, 3, IQ)
        q4m = view(q4_work, 1152, 36)
        q4i = view(q4_work, 1188, 36)
        def batched_rstd(k, dve, act, n):
            if dve is not None:
                if n == 2 * NB:
                    nc.vector.tensor_scalar(variance[:, 0:NB], moments[:, 0:NB, 1], 1.0 + LN_EPS, LN_EPS * LN_EPS,
                                            ALU.mult, ALU.add)
                    nc.vector.tensor_scalar(variance[:, NB:2 * NB], moments[:, NB:2 * NB, 1], LN_EPS, None,
                                            ALU.add).then_inc(var_ready, 1)
                else:
                    nc.vector.tensor_scalar(variance[:, 0:n], moments[:, 0:n, 1], LN_EPS, None,
                                            ALU.add).then_inc(var_ready, 1)
                dve.wait_ge(dev_ready, k + 1)
                nc.vector.reciprocal(rstd[:, 0:n], deviation[:, 0:n]).then_inc(rstd_ready, 1)
                dve.wait_ge(rstd_ready, k + 1)
                nc.vector.scalar_tensor_tensor(shift[:, 0:n], moments[:, 0:n, 0], -1.0, rstd[:, 0:n],
                                               ALU.mult, ALU.mult).then_inc(shift_ready, 1)
            if act is not None:
                act.wait_ge(var_ready, k + 1)
                nc.scalar.activation(deviation[:, 0:n], variance[:, 0:n], ACT.Sqrt).then_inc(dev_ready, 1)

        with nc.Block(no_gpsimd_drain=True) as block:
            @block.sync
            def _(sp):
                sp.dma_start(x_all[:, :, :], d["x"].rearrange("b t d -> t b d")).then_inc(x_loaded, 16)
                load(sp, const[:, :], d["const"])
                load(sp, columns[:, :], d["columns"])
                load(sp, w_token[:, :], d["w_token"])
                load(sp, w_context[:, :], d["w_context"])
                load(sp, w_out[:, :], d["w_out"])
                load(sp, bias_out[:, :], d["bias_out"].rearrange("(a n) -> a n", a=1).to_broadcast([128, 128]))
                load(sp, wq4_in[:, 0, :].rearrange("p (c i) -> p c i", c=NQ), d["w_gate"].rearrange("(c p) i -> p c i", p=128))
                load(sp, wq4_in[:, 1, :].rearrange("p (c i) -> p c i", c=NQ), d["w_up"].rearrange("(c p) i -> p c i", p=128))
                load(sp, wq4_in[:, 2, :], d["w_down"])

            @block.scalar
            def _(act):
                act.dma_start(context[:, :, :], d["context"].rearrange("b k d -> k b d")).then_inc(ctx_loaded, 16)
                load(act, const16[:, :], d["const16"])
                load(act, context_t[:, :, :], d["context_t"])
                load(act, bit_int[:, :], d["bit_int"])
                load(act, wq1[:, :], d["wq1"])
                load(act, wkv1[:, :], d["wkv1"])
                load(act, gate_w[:, :], d["gate_w"])
                load(act, shared_up[:, :, :], d["shared_up"])
                load(act, shared_down[:, :, :], d["shared_down"])
                load(act, mask_q8[:, :], d["mask_q"])
                load(act, mask_k8[:, :], d["mask_k"].rearrange("(a n) -> a n", a=1))
                batched_rstd(0, None, act, 2 * NB)

            @block.gpsimd
            def _(pool):
                nc.gpsimd.memset(moments[:, :, :], 1.0).then_inc(memory_set, 1)
                nc.gpsimd.memset(norms[:, :, :], 1.0).then_inc(memory_set, 1)
                nc.gpsimd.memset(values1[:, :, :, DH1:DH1 + 1], 1.0).then_inc(memory_set, 1)

            @block.vector
            def _(dve):
                dve.wait_ge(memory_set, 3)
                dve.wait_ge(x_loaded, 16)
                for b in range(NB):
                    nc.vector.bn_stats(bn[:, b, :], x_all[:, b, :]).then_inc(bn_done, 1)
                dve.wait_ge(ctx_loaded, 16)
                for b in range(NB):
                    nc.vector.bn_stats(bn[0:CK, NB + b, :], context[:, b, :]).then_inc(bn_done, 1)
                dve.wait_ge(bn_done, 2 * NB)
                for b in range(2 * NB):
                    p = 128 if b < NB else CK
                    last = nc.vector.bn_aggr(moments[0:p, b, :], bn[0:p, b, :])
                link(dve, last)
                batched_rstd(0, dve, None, 2 * NB)
                dve.wait_ge(loads, 16 * N_LOADS[0])
                nc.vector.tensor_copy(mask_q[:, :], mask_q8[:, :])
                nc.vector.tensor_scalar(mask_k[:, :], mask_k8[:, :], -1.0, -MASKED, ALU.add, ALU.mult)
                nc.vector.scalar_tensor_tensor(columns[:, 6:7], columns[:, 4:5], DH0 ** -0.5, columns[:, 5:6],
                                               ALU.mult, ALU.mult).then_inc(gain_ready, 1)

        a1_xn_ready = sem("a1_xn_ready")
        a1_cn_ready = sem("a1_cn_ready")
        a1_transposed = sem("a1_transposed")
        a1_lnT_ready = sem("a1_lnT_ready")
        a1_cnT_ready = sem("a1_cnT_ready")
        a1_rawT_ready = sem("a1_rawT_ready")
        a1_projected = sem("a1_projected")
        a1_qkv_ready = sem("a1_qkv_ready")
        a1_keys1_ready = sem("a1_keys1_ready")
        a1_ctx_kv_ready = sem("a1_ctx_kv_ready")
        a1_values1_ready = sem("a1_values1_ready")
        a1_squares_ready = sem("a1_squares_ready")
        a1_ctx_squares_ready = sem("a1_ctx_squares_ready")
        a1_sums_ready = sem("a1_sums_ready")
        a1_norms_ready = sem("a1_norms_ready")

        xn = view(stage, 0, 128)
        cn = view(stage, 128, CD)[0:CK]
        lnT = view(stage, 256, 128)
        cnT = view(stage, 384, CK)[0:CD]
        rawT = view(stage, 464, CK)[0:CD]
        squares = view(stage, 544, 4, DH0)
        ctx_squares = view(stage, 800, 2, DH0)[0:CK]

        with nc.Block(no_gpsimd_drain=True) as block:
            @block.gpsimd
            def _(pool):
                def step(i, u):
                    if live(i, NB):
                        if live(i - 1, NB):
                            pool.wait_ge(a1_projected, i)
                        nc.gpsimd.tensor_copy(rawT, context_t[:, i, :]).then_inc(a1_rawT_ready, 1)
                        pool.wait_ge(a1_xn_ready, i + 1)
                        nc.gpsimd.tensor_tensor(x_all[:, i, :], x_all[:, i, :], bias_out[:, :], ALU.add)
                    b = i - 1
                    if live(b, NB):
                        if live(b - 1, NB):
                            pool.wait_ge(a1_sums_ready, b)
                        pool.wait_ge(a1_qkv_ready, b + 1)
                        qk = qkv[:, b, 0:256].rearrange("p (h e) -> p h e", h=4)
                        nc.gpsimd.tensor_tensor(squares, qk, qk, ALU.mult).then_inc(a1_squares_ready, 1)
                        pool.wait_ge(a1_ctx_kv_ready, b + 1)
                        ck = ctx_kv[:, b, 0:128].rearrange("p (h e) -> p h e", h=2)
                        nc.gpsimd.tensor_tensor(ctx_squares, ck, ck, ALU.mult).then_inc(a1_ctx_squares_ready, 1)

                skewed(pool, NB, 2, step)

            @block.vector
            def _(dve):
                def step(i, u):
                    if live(i, NB):
                        if live(i - 1, NB):
                            dve.wait_ge(a1_transposed, i)
                        nc.vector.tensor_scalar(xn, x_all[:, i, :], rstd[:, bass.ds(i, 1)], shift[:, bass.ds(i, 1)],
                                                ALU.mult, ALU.add).then_inc(a1_xn_ready, 1)
                    b = i - 1
                    if live(b, NB):
                        dve.wait_ge(a1_projected, b + 1)
                        nc.vector.tensor_copy(ctx_kv[:, b, :], bank[2][0:CK, 0:256]).then_inc(a1_ctx_kv_ready, 1)
                        nc.vector.tensor_copy(values1[:, b, :, 0:DH1], bank[2][0:CK, 336:464].rearrange(
                            "p (h e) -> p h e", h=H1)).then_inc(a1_values1_ready, 1)
                    if live(i, NB):
                        dve.wait_ge(a1_transposed, i + 1)
                        nc.vector.tensor_scalar(cnT, bank[3][0:CD, 0:CK], columns[0:CD, 2:3], columns[0:CD, 3:4],
                                                ALU.mult, ALU.add).then_inc(a1_cnT_ready, 1)
                    b = i - 2
                    if live(b, NB):
                        dve.wait_ge(a1_squares_ready, b + 1)
                        nc.vector.tensor_reduce(norms[:, b, 0:4], squares, axis=AX.X, op=ALU.add)
                        dve.wait_ge(a1_ctx_squares_ready, b + 1)
                        nc.vector.tensor_reduce(norms[0:CK, b, 4:6], ctx_squares, axis=AX.X,
                                                op=ALU.add).then_inc(a1_sums_ready, 1)

                skewed(dve, NB, 2, step)
                dve.wait_ge(a1_norms_ready, 1)
                link(dve, nc.vector.tensor_scalar(norms[:, :, :], norms[:, :, :], RMS_EPS, None, ALU.max
                                        ))
                nc.vector.reciprocal(inv_norms[:, :, :], norms[:, :, :])

            @block.scalar
            def _(act):
                def step(i, u):
                    if live(i, NB):
                        if live(i - 1, NB):
                            act.wait_ge(a1_transposed, i)
                        nc.scalar.activation(cn, context[:, i, :], ACT.Identity, bias=shift[0:CK, bass.ds(i + NB, 1)],
                                             scale=rstd[0:CK, bass.ds(i + NB, 1)]).then_inc(a1_cn_ready, 1)
                    b = i - 1
                    if live(b, NB):
                        act.wait_ge(a1_projected, b + 1)
                        nc.scalar.copy(qkv[:, b, :], bank[1][:, 0:384]).then_inc(a1_qkv_ready, 1)
                        nc.scalar.copy(keys1[:, b, :], bank[4][:, 0:CK]).then_inc(a1_keys1_ready, 1)
                    if live(i, NB):
                        act.wait_ge(a1_transposed, i + 1)
                        nc.scalar.activation(lnT, bank[0][:, 0:128], ACT.Identity, bias=columns[:, 1:2],
                                             scale=columns[:, 0:1]).then_inc(a1_lnT_ready, 1)

                skewed(act, NB, 2, step)
                act.wait_ge(a1_sums_ready, NB)
                nc.scalar.activation(norms[:, :, :], norms[:, :, :], ACT.Sqrt, scale=1.0 / DH0
                                     ).then_inc(a1_norms_ready, 1)

            @block.tensor
            def _(pe):
                def step(i, u):
                    b = i - 1
                    if live(b, NB):
                        pe.wait_ge(a1_lnT_ready, b + 1)
                        if live(b - 1, NB):
                            pe.wait_ge(a1_qkv_ready, b)
                            pe.wait_ge(a1_keys1_ready, b)
                            pe.wait_ge(a1_values1_ready, b)
                        nc.tensor.matmul(bank[1][:, 0:384], lnT, w_token[:, :], start=True, stop=True)
                        pe.wait_ge(a1_cnT_ready, b + 1)
                        nc.tensor.matmul(bank[2][0:CK, 0:256], cnT, w_context[:, :], start=True, stop=True)
                        pe.wait_ge(a1_rawT_ready, b + 1)
                        nc.tensor.matmul(bank[4][:, 0:CK], wkv1[:, 0:128], rawT, start=True, stop=True)
                        nc.tensor.matmul(bank[2][0:CK, 336:464], rawT, wkv1[:, 128:256], start=True, stop=True
                                         ).then_inc(a1_projected, 1)
                    if live(i, NB):
                        pe.wait_ge(a1_xn_ready, i + 1)
                        nc.tensor.transpose(bank[0][:, 0:128], xn, ident)
                        pe.wait_ge(a1_cn_ready, i + 1)
                        nc.tensor.transpose(bank[3][0:CD, 0:CK], cn, ident[0:CK, 0:CK]
                                            ).then_inc(a1_transposed, 1)

                skewed(pe, NB, 2, step)

        a2_q_normed = sem("a2_q_normed")
        a2_k_normed = sem("a2_k_normed")
        a2_transposed = sem("a2_transposed")
        a2_qT_ready = sem("a2_qT_ready")
        a2_kT_ready = sem("a2_kT_ready")
        a2_scored = sem("a2_scored")
        a2_max_ready = sem("a2_max_ready")
        a2_weights_ready = sem("a2_weights_ready")
        a2_weights_transposed = sem("a2_weights_transposed")
        a2_ctx_wT_ready = sem("a2_ctx_wT_ready")
        a2_lat_wT_ready = sem("a2_lat_wT_ready")
        a2_mixed = sem("a2_mixed")
        a2_inv_sum_ready = sem("a2_inv_sum_ready")
        a2_out_normed = sem("a2_out_normed")
        a2_out_transposed = sem("a2_out_transposed")
        a2_outT_ready = sem("a2_outT_ready")
        a2_out_projected = sem("a2_out_projected")
        a2_x_ready = sem("a2_x_ready")
        a2_x_bn_done = sem("a2_x_bn_done")
        x_moments_ready = sem("x_moments_ready")

        qk_n = view(stage, 0, 4, DH0)
        ck_n = view(stage, 256, 2, DH0)[0:CK]
        qT = view(stage, 384, 128)
        kT = view(stage, 512, KEYS0)
        weights = view(stage, 720, H0, KEYS0)
        ctx_wT = view(stage, 1136, H0, 128)[0:CK]
        lat_wT = view(stage, 1392, H0, 128)
        out_n = view(stage, 1648, H0, DH0)
        outT = view(stage, 1776, 128)
        neg_max = view(stage, 1904, H0)
        weight_sum = [view(stage, 1906, H0), view(stage, 1908, H0)]
        inv_sum = view(stage, 1910, H0)
        score = [bank[2], bank[3]]

        with nc.Block(no_gpsimd_drain=True) as block:
            @block.gpsimd
            def _(pool):
                def step(i, u):
                    if live(i, NB):
                        if live(i - 1, NB):
                            pool.wait_ge(a2_transposed, i)
                        nc.gpsimd.tensor_tensor(qk_n, qkv[:, i, 0:256].rearrange("p (h e) -> p h e", h=4),
                                                inv_norms[:, i, 0:4, None].to_broadcast([128, 4, DH0]), ALU.mult
                                                ).then_inc(a2_q_normed, 1)
                        nc.gpsimd.tensor_tensor(ck_n, ctx_kv[:, i, 0:128].rearrange("p (h e) -> p h e", h=2),
                                                inv_norms[0:CK, i, 4:6, None].to_broadcast([CK, 2, DH0]), ALU.mult
                                                ).then_inc(a2_k_normed, 1)

                skewed(pool, NB, 0, step)

            @block.tensor
            def _(pe):
                qk_flat = qk_n.rearrange("p h e -> p (h e)")
                ck_flat = ck_n.rearrange("p h e -> p (h e)")

                def step(i, u):
                    b = i - 5
                    if live(b, NB):
                        pe.wait_ge(a2_outT_ready, b + 1)
                        if live(b - 1, NB):
                            pe.wait_ge(a2_x_ready, b)
                        nc.tensor.matmul(bank[7][:, 0:128], outT, w_out[:, :], start=True, stop=True
                                         ).then_inc(a2_out_projected, 1)
                    b = i - 4
                    if live(b, NB):
                        pe.wait_ge(a2_out_normed, b + 1)
                        if live(i - 1, NB):
                            pe.wait_ge(a2_qT_ready, i)
                        nc.tensor.transpose(bank[0][:, 128:256], out_n.rearrange("p h e -> p (h e)"), ident
                                            ).then_inc(a2_out_transposed, 1)
                    b = i - 3
                    if live(b, NB):
                        pe.wait_ge(a2_ctx_wT_ready, b + 1)
                        pe.wait_ge(a2_lat_wT_ready, b + 1)
                        for h in range(H0):
                            o = bank[6][:, h * DH0:(h + 1) * DH0]
                            nc.tensor.matmul(o, ctx_wT[:, h, :], ctx_kv[:, b, 128 + h * DH0:128 + (h + 1) * DH0],
                                             start=True, stop=False)
                            last = nc.tensor.matmul(o, lat_wT[:, h, :], qkv[:, b, 256 + h * DH0:256 + (h + 1) * DH0],
                                                    start=False, stop=True)
                        last.then_inc(a2_mixed, 1)
                    b = i - 2
                    if live(b, NB):
                        pe.wait_ge(a2_weights_ready, b + 1)
                        for h in range(H0):
                            nc.tensor.transpose(bank[4][0:CK, h * 128:(h + 1) * 128], weights[:, h, 0:CK], ident)
                            last = nc.tensor.transpose(bank[5][:, h * 128:(h + 1) * 128], weights[:, h, CK:KEYS0],
                                                       ident)
                        last.then_inc(a2_weights_transposed, 1)
                    b = i - 1
                    if live(b, NB):
                        pe.wait_ge(a2_qT_ready, b + 1)
                        pe.wait_ge(a2_kT_ready, b + 1)
                        for h in range(H0):
                            rows = slice(h * DH0, (h + 1) * DH0)
                            nc.tensor.matmul(score[h][:, 0:KEYS0], qT[rows, :], kT[rows, :], start=True, stop=False)
                            last = nc.tensor.matmul(score[h][:, 0:CK], ones16[0:1, :], mask_k[:, bass.ds(b * CK, CK)],
                                                    start=False, stop=True)
                        last.then_inc(a2_scored, 1)
                    if live(i, NB):
                        pe.wait_ge(a2_q_normed, i + 1)
                        pe.wait_ge(a2_k_normed, i + 1)
                        if live(i - 4, NB):
                            pe.wait_ge(a2_outT_ready, i - 3)
                        nc.tensor.transpose(bank[0][:, 0:128], qk_flat[:, 0:128], ident)
                        nc.tensor.transpose(bank[1][:, 0:CK], ck_flat, ident[0:CK, 0:CK])
                        nc.tensor.transpose(bank[1][:, CK:KEYS0], qk_flat[:, 128:256], ident
                                            ).then_inc(a2_transposed, 1)

                skewed(pe, NB, 6, step)

            @block.scalar
            def _(act):
                def step(i, u):
                    b = i - 4
                    if live(b, NB):
                        act.wait_ge(a2_out_transposed, b + 1)
                        nc.scalar.copy(outT, bank[0][:, 128:256]).then_inc(a2_outT_ready, 1)
                    b = i - 2
                    if live(b, NB):
                        act.wait_ge(a2_weights_transposed, b + 1)
                        nc.scalar.copy(ctx_wT, bank[4][0:CK, 0:256].rearrange("p (h q) -> p h q", h=H0)
                                       ).then_inc(a2_ctx_wT_ready, 1)
                    b = i - 1
                    if live(b, NB):
                        act.wait_ge(a2_max_ready, b + 1)
                        if live(b - 2, NB):
                            act.wait_ge(a2_inv_sum_ready, b - 1)
                        for h in range(H0):
                            last = nc.scalar.activation(weights[:, h, :], score[h][:, 0:KEYS0], ACT.Exp,
                                                        bias=neg_max[:, h:h + 1], accum_out=weight_sum[(u + 1) % 2][:, h:h + 1])
                        last.then_inc(a2_weights_ready, 1)
                    if live(i, NB):
                        act.wait_ge(a2_transposed, i + 1)
                        nc.scalar.activation(qT, bank[0][:, 0:128], ACT.Copy, scale=columns[:, 6:7]
                                             ).then_inc(a2_qT_ready, 1)

                skewed(act, NB, 6, step, unroll=2)

            @block.vector
            def _(dve):
                def step(i, u):
                    b = i - 5
                    if live(b, NB):
                        dve.wait_ge(a2_out_projected, b + 1)
                        nc.vector.tensor_tensor(x_all[:, b, :], bank[7][:, 0:128], x_all[:, b, :], ALU.add
                                                ).then_inc(a2_x_ready, 1)
                        dve.wait_ge(a2_x_ready, b + 1)
                        nc.vector.bn_stats(bn[:, b, :], x_all[:, b, :]).then_inc(a2_x_bn_done, 1)
                    b = i - 3
                    if live(b, NB):
                        if live(b - 1, NB):
                            dve.wait_ge(a2_out_normed, b)
                        nc.vector.reciprocal(inv_sum, weight_sum[(u + 1) % 2]
                                             ).then_inc(a2_inv_sum_ready, 1)
                        dve.wait_ge(a2_inv_sum_ready, b + 1)
                        dve.wait_ge(a2_mixed, b + 1)
                        nc.vector.tensor_tensor(out_n, bank[6][:, 0:128].rearrange("p (h e) -> p h e", h=H0),
                                                inv_sum[:, :, None].to_broadcast([128, H0, DH0]), ALU.mult
                                                ).then_inc(a2_out_normed, 1)
                    b = i - 2
                    if live(b, NB):
                        dve.wait_ge(a2_weights_transposed, b + 1)
                        nc.vector.tensor_copy(lat_wT, bank[5][:, 0:256].rearrange("p (h q) -> p h q", h=H0)
                                              ).then_inc(a2_lat_wT_ready, 1)
                    b = i - 1
                    if live(b, NB):
                        dve.wait_ge(a2_scored, b + 1)
                        for h in range(H0):
                            last = nc.vector.tensor_reduce(neg_max[:, h:h + 1], score[h][:, 0:KEYS0], axis=AX.X,
                                                           op=ALU.max, negate=True)
                        last.then_inc(a2_max_ready, 1)
                    if live(i, NB):
                        dve.wait_ge(a2_transposed, i + 1)
                        nc.vector.tensor_copy(kT, bank[1][:, 0:KEYS0]).then_inc(a2_kT_ready, 1)

                skewed(dve, NB, 6, step, unroll=2)
                dve.wait_ge(a2_x_bn_done, NB)
                for b in range(NB):
                    last = nc.vector.bn_aggr(moments[:, b, :], bn[:, b, :])
                last.then_inc(x_moments_ready, 1)

        b1_h_ready = sem("b1_h_ready")
        b1_copied = sem("b1_copied")
        b1_transposed = sem("b1_transposed")
        b1_hT_ready = sem("b1_hT_ready")
        b1_logits_ready = sem("b1_logits_ready")
        b1_shifted = sem("b1_shifted")
        b1_exp_ready = sem("b1_exp_ready")
        b1_scores_ready = sem("b1_scores_ready")
        expert_w_loaded = [sem("expert_w_loaded_even"), sem("expert_w_loaded_odd")]

        rows = sb("rows_all", [128, NB, GROW])
        hT_all = sb("hT_all", [128, NT])
        scores = sb("scores", [128, NB, NE])
        h_now = view(stage, 0, 128)
        hT_now = view(stage, 128, 128)
        sm_max = view(stage, 256, NB)
        sm_sum = view(stage, 272, NB)

        with nc.Block(no_gpsimd_drain=True) as block:
            @block.sync
            def _(sp):
                for e in range(2):
                    sp.dma_start(w_slots[:, e], d["expert_w"][e]).then_inc(expert_w_loaded[e], 16)

            @block.scalar
            def _(act):
                batched_rstd(1, None, act, NB)

                def step(i, u):
                    if live(i, NB):
                        act.wait_ge(b1_transposed, i + 1)
                        if live(i - 1, NB):
                            act.wait_ge(b1_copied, 2 * i)
                        nc.scalar.copy(hT_now, bank[0][:, 0:128]).then_inc(b1_hT_ready, 1)

                skewed(act, NB, 2, step)
                act.wait_ge(b1_shifted, 1)
                nc.scalar.activation(scores[:, :, :], scores[:, :, :], ACT.Exp).then_inc(b1_exp_ready, 1)

            @block.gpsimd
            def _(pool):
                def step(i, u):
                    if live(i, NB):
                        pool.wait_ge(b1_h_ready, i + 1)
                        nc.gpsimd.tensor_copy(rows[:, i, 0:D], h_now).then_inc(b1_copied, 1)
                        pool.wait_ge(b1_hT_ready, i + 1)
                        nc.gpsimd.tensor_copy(hT_all[:, bass.ds(i * T, T)], hT_now).then_inc(b1_copied, 1)

                skewed(pool, NB, 2, step)
                pool.wait_ge(b1_scores_ready, 1)
                nc.gpsimd.tensor_copy(rows[:, :, D:GROW], scores[:, :, :]).then_inc(b1_copied, 1)

            @block.tensor
            def _(pe):
                def step(i, u):
                    b = i - 1
                    if live(b, NB):
                        pe.wait_ge(b1_hT_ready, b + 1)
                        last = nc.tensor.matmul(bank[7][:, bass.ds(b * NE, NE)], hT_now, gate_w[:, :],
                                                start=True, stop=True)
                        last.then_inc(b1_logits_ready, 1)
                    if live(i, NB):
                        pe.wait_ge(b1_h_ready, i + 1)
                        nc.tensor.transpose(bank[0][:, 0:128], h_now, ident).then_inc(b1_transposed, 1)

                skewed(pe, NB, 2, step)

            @block.vector
            def _(dve):
                batched_rstd(1, dve, None, NB)
                dve.wait_ge(shift_ready, 2)

                def step(i, u):
                    if live(i, NB):
                        if live(i - 1, NB):
                            dve.wait_ge(b1_transposed, i)
                            dve.wait_ge(b1_copied, 2 * i - 1)
                        nc.vector.tensor_scalar(h_now, x_all[:, i, :], rstd[:, bass.ds(i, 1)], shift[:, bass.ds(i, 1)],
                                                ALU.mult, ALU.add).then_inc(b1_h_ready, 1)

                skewed(dve, NB, 2, step)
                dve.wait_ge(b1_logits_ready, NB)
                logits = bank[7][:, 0:NB * NE].rearrange("p (b e) -> p b e", b=NB)
                link(dve, nc.vector.tensor_reduce(sm_max, logits, axis=AX.X, op=ALU.max))
                nc.vector.tensor_tensor(scores[:, :, :], logits, sm_max[:, :, None].to_broadcast([128, NB, NE]),
                                        ALU.subtract).then_inc(b1_shifted, 1)
                dve.wait_ge(b1_exp_ready, 1)
                link(dve, nc.vector.tensor_reduce(sm_sum, scores[:, :, :], axis=AX.X, op=ALU.add))
                link(dve, nc.vector.reciprocal(sm_max, sm_sum))
                nc.vector.tensor_tensor(scores[:, :, :], scores[:, :, :],
                                        sm_max[:, :, None].to_broadcast([128, NB, NE]), ALU.mult
                                        ).then_inc(b1_scores_ready, 1)
                dve.wait_ge(b1_copied, 2 * NB + 1)

        rows_stored = sem("rows_stored")
        sums_stored = sem("sums_stored")
        b2_scoresT = sem("b2_scoresT")
        b2_scoresT_ready = sem("b2_scoresT_ready")
        b2_found_zero = sem("b2_found_zero")
        b2_trial_ready = sem("b2_trial_ready")
        b2_counted = sem("b2_counted")
        b2_total_ready = sem("b2_total_ready")
        b2_hit_ready = sem("b2_hit_ready")
        b2_found_ready = sem("b2_found_ready")
        b2_gate_ready = sem("b2_gate_ready")
        b2_up_ready = sem("b2_up_ready")
        b2_gelu_ready = sem("b2_gelu_ready")
        b2_hidden_ready = sem("b2_hidden_ready")
        b2_shared_ready = sem("b2_shared_ready")
        b2_added = sem("b2_added")
        b3_wide_ready = sem("b3_wide_ready")
        b3_threshold_ready = sem("b3_threshold_ready")
        b3_above_ready = sem("b3_above_ready")
        b3_from_ready = sem("b3_from_ready")
        b3_scanned = sem("b3_scanned")
        b3_earlier_ready = sem("b3_earlier_ready")
        b3_above_counted = sem("b3_above_counted")
        b3_equal_ranked = sem("b3_equal_ranked")
        b3_in_need = sem("b3_in_need")
        b3_taken_ranked = sem("b3_taken_ranked")
        b3_low_ready = sem("b3_low_ready")

        scoresT = view(stage, 0, NB * T // 8)
        trial = view(stage, 256, 1).bitcast(I32)
        found = view(stage, 257, 1).bitcast(I32)
        hit = view(stage, 258, 1).bitcast(I32)
        zero_col = view(stage, 259, 1).bitcast(I32)
        count16 = sb("count16", [128, 2], BF16)
        junk16 = sb("junk16", [128, 256], BF16)
        gelu_s = view(stage, 260, 2, 256)
        hidden_s = view(stage, 772, 2, 256)
        wide = view(stage, 1284, 128)
        sel16 = sb("sel16", [128, 6, NE * NB], BF16)
        above, equal, earlier, taken = (sel16[:, n, :] for n in range(4))
        from16, in_need = sel16[:, 4, :], sel16[:, 5, :]
        need = view(stage, 1412, NE)
        scan = view(stage, 1430, NE * NB)
        place = view(stage, 1686, NE * NB)
        low = sb("low", [128, NE * NB])
        half = sb("half", [128, 2, NE * NB])
        halves = sb("halves", [128, NE * NB, 2], F16)

        def by_expert(ap):
            return ap.rearrange("p (b e) -> p e b", b=NB)

        def ranks(pe, bits, earlier_bits, out):
            nc.tensor.matmul(out, before, bits, start=True, stop=False)
            return nc.tensor.matmul(out, ones16, earlier_bits, start=False, stop=True)

        with nc.Block(no_gpsimd_drain=True) as block:
            @block.sync
            def _(sp):
                sp.dma_start(d["rows"].rearrange("(b t) c -> t b c", b=NB), rows[:, :, :]).then_inc(rows_stored, 16)
                sp.wait_ge(b2_added, 8)
                sp.dma_start(d["sums"].rearrange("(b t) c -> t b c", b=NB), x_all[:, :, :]).then_inc(sums_stored, 16)

            @block.tensor
            def _(pe):
                scores_flat = scores[:, :, :].rearrange("p b e -> p (b e)")
                for n in range(2):
                    last = nc.tensor.transpose(bank[6][:, n * 128:(n + 1) * 128], scores_flat[:, n * 128:(n + 1) * 128],
                                               ident)
                last.then_inc(b2_scoresT, 1)

                def down(c, m):
                    for k in range(2):
                        last = nc.tensor.matmul(bank[5][:, m * 128:(m + 1) * 128], hidden_s[:, k, m * 128:(m + 1) * 128],
                                                shared_down[:, k, :], start=(k == 0), stop=(k == 1))
                    return last

                def up(c, which, k):
                    bk = bank[1 + 2 * which]
                    return nc.tensor.matmul(bk[:, k * 256:(k + 1) * 256],
                                            shared_up[:, which, k * 128:(k + 1) * 128],
                                            hT_all[:, bass.ds(c * 256, 256)], start=True, stop=True)

                def total(n):
                    pe.wait_ge(b2_counted, n + 1)
                    nc.tensor.matmul(bank[6][:, 0:1], same_expert, count16[:, 0:1], start=True, stop=True
                                     ).then_inc(b2_total_ready, 1)

                def step(c, u):
                    n = c * 4
                    if live(c, 8):
                        total(n)
                        if live(c - 1, 8):
                            pe.wait_ge(b2_gelu_ready, c)
                        up(c, 0, 0)
                        up(c, 0, 1).then_inc(b2_gate_ready, 1)
                        total(n + 1)
                        if live(c - 1, 8):
                            pe.wait_ge(b2_hidden_ready, c)
                        up(c, 1, 0)
                        up(c, 1, 1).then_inc(b2_up_ready, 1)
                        total(n + 2)
                    if live(c - 1, 8):
                        pe.wait_ge(b2_hidden_ready, c)
                        if live(c - 2, 8):
                            pe.wait_ge(b2_added, c - 1)
                        down(c - 1, 0)
                        down(c - 1, 1).then_inc(b2_shared_ready, 1)
                    if live(c, 8):
                        total(n + 3)

                skewed(pe, 8, 2, step)
                pe.wait_ge(b3_wide_ready, 1)
                nc.tensor.transpose(bank[0][:, 0:128], wide, ident).then_inc(b3_threshold_ready, 1)
                pe.wait_ge(b3_above_ready, 1)
                nc.tensor.matmul(bank[1][:, 0:256], ones16, above, start=True, stop=True).then_inc(b3_above_counted, 1)
                pe.wait_ge(b3_earlier_ready, 1)
                ranks(pe, equal, earlier, bank[2][:, 0:256]).then_inc(b3_equal_ranked, 1)
                pe.wait_ge(b3_earlier_ready, 2)
                ranks(pe, taken, earlier, bank[3][:, 0:256]).then_inc(b3_taken_ranked, 1)

            @block.scalar
            def _(act):
                def step(c, u):
                    act.wait_ge(b2_gate_ready, c + 1)
                    if live(c - 1, 8):
                        act.wait_ge(b2_hidden_ready, c)
                    nc.scalar.activation(gelu_s, bank[1][:, 0:512].rearrange("p (k t) -> p k t", k=2), ACT.Gelu
                                         ).then_inc(b2_gelu_ready, 1)

                step(0, 0)
                with act.Fori(1, 8) as c:
                    step(c, 0)

            @block.vector
            def _(dve):
                dve.wait_ge(b2_scoresT, 1)
                nc.vector.tensor_copy(scoresT, bank[6][:, 0:256]).then_inc(b2_scoresT_ready, 1)
                nc.vector.memset(found, 0).then_inc(b2_found_zero, 1)
                nc.vector.tensor_copy(trial, bit_int[:, 0:1]).then_inc(b2_trial_ready, 1)
                dve.wait_ge(b2_scoresT_ready, 1)
                dve.wait_ge(b2_found_zero, 1)

                def bit(n, next_bit):
                    dve.wait_ge(b2_trial_ready, n + 1)
                    nc.vector.tensor_scalar(junk16[:, :], scoresT, trial.bitcast(F32), None, ALU.is_ge, ALU.add,
                                            accum_out=count16[:, 0:1]).then_inc(b2_counted, 1)
                    dve.wait_ge(b2_total_ready, n + 1)
                    nc.vector.tensor_scalar(hit, bank[6][:, 0:1], float(CAP), bit_value[:, bass.ds(n, 1)],
                                            ALU.is_ge, ALU.mult).then_inc(b2_hit_ready, 1)
                    dve.wait_ge(b2_hit_ready, n + 1)
                    nc.vector.tensor_tensor(found, found, hit, ALU.bitwise_or).then_inc(b2_found_ready, 1)
                    dve.wait_ge(b2_found_ready, n + 1)
                    if next_bit:
                        nc.vector.tensor_tensor(trial, found, bit_int[:, bass.ds(n + 1, 1)], ALU.bitwise_or
                                                ).then_inc(b2_trial_ready, 1)

                def step(c, u):
                    n = c * 4
                    if live(c, 8):
                        bit(n, True)
                        bit(n + 1, True)
                    if live(c - 1, 8):
                        pass
                    if live(c, 8):
                        bit(n + 2, True)
                        dve.wait_ge(b2_up_ready, c + 1)
                        dve.wait_ge(b2_gelu_ready, c + 1)
                        if live(c - 1, 8):
                            dve.wait_ge(b2_shared_ready, c)
                        nc.vector.tensor_tensor(hidden_s, gelu_s, bank[3][:, 0:512].rearrange("p (k t) -> p k t", k=2),
                                                ALU.mult).then_inc(b2_hidden_ready, 1)
                        bit(n + 3, not isinstance(c, int) or c < 7)
                    if live(c - 1, 8):
                        dve.wait_ge(b2_shared_ready, c)
                        xs = x_all[:, bass.ds((c - 1) * 2, 2), :]
                        nc.vector.tensor_tensor(xs, bank[5][:, 0:256].rearrange("p (b d) -> p b d", b=2), xs, ALU.add
                                                ).then_inc(b2_added, 1)

                step(0, 0)
                with dve.Fori(1, 7) as c:
                    step(c, 0)
                step(7, 0)
                step(8, 0)
                nc.vector.tensor_copy(wide, found.bitcast(F32).to_broadcast([128, 128])).then_inc(b3_wide_ready, 1)
                dve.wait_ge(b3_threshold_ready, 1)
                sc = scores[:, :, :].rearrange("p (n j) e -> p n (j e)", n=2)
                thr = bank[0][:, None, 0:128].to_broadcast([128, 2, 128])

                def compared(out, op, signal):
                    for n in range(2):
                        last = nc.vector.tensor_tensor(
                            out.rearrange("p (e n j) -> p n j e", n=2, j=8)[:, n],
                            scores[:, n * 8:(n + 1) * 8, :], bank[0][:, 0:128].rearrange("p (j e) -> p j e", j=8), op)
                    last.then_inc(signal, 1)

                compared(above, ALU.is_gt, b3_above_ready)
                compared(from16, ALU.is_ge, b3_from_ready)
                dve.wait_ge(b3_from_ready, 1)
                link(dve, nc.vector.tensor_tensor(equal, from16, above, ALU.subtract))

                def earlier_of(bits, n):
                    if n:
                        dve.wait_ge(b3_equal_ranked, n)
                    nc.vector.tensor_tensor_scan(scan, first_batch, bits, 0.0, ALU.mult, ALU.add
                                                 ).then_inc(b3_scanned, 1)
                    dve.wait_ge(b3_scanned, n + 1)
                    nc.vector.tensor_tensor(earlier, scan, bits, ALU.subtract).then_inc(b3_earlier_ready, 1)

                earlier_of(equal, 0)
                dve.wait_ge(b3_above_counted, 1)
                link(dve, nc.vector.tensor_reduce(need, bank[1][:, 0:256].rearrange("p (e b) -> p e b", b=NB), axis=AX.X,
                                        op=ALU.add))
                link(dve, nc.vector.tensor_scalar(need, need, -1.0, float(CAP), ALU.mult, ALU.add))
                dve.wait_ge(b3_equal_ranked, 1)
                eb = dict(b=NB)
                nc.vector.tensor_tensor(in_need.rearrange("p (e b) -> p e b", **eb),
                                        bank[2][:, 0:256].rearrange("p (e b) -> p e b", **eb),
                                        need[:, :, None].to_broadcast([128, NE, NB]), ALU.is_lt
                                        ).then_inc(b3_in_need, 1)
                dve.wait_ge(b3_in_need, 1)
                link(dve, nc.vector.tensor_tensor(in_need, in_need, equal, ALU.mult))
                link(dve, nc.vector.tensor_tensor(taken, in_need, above, ALU.add))
                earlier_of(taken, 1)
                dve.wait_ge(b3_taken_ranked, 1)
                link(dve, nc.vector.scalar_tensor_tensor(place, bank[3][:, 0:256], 1.0, taken, ALU.add, ALU.mult
                                               ))
                nc.vector.tensor_scalar(half[:, 1, :], place, 128.5, None, ALU.is_gt)
                link(dve, nc.vector.tensor_scalar(half[:, 0, :], place, 128.5, None, ALU.is_lt))
                nc.vector.scalar_tensor_tensor(low[:, :], half[:, 1, :], -128.0, place, ALU.mult, ALU.add)
                for n in range(2):
                    last = nc.vector.tensor_tensor(
                        halves[:, :, n].rearrange("p (e b) -> p e b", **eb),
                        half[:, n, :].rearrange("p (e b) -> p e b", **eb),
                        token_id[:, None, :].to_broadcast([128, NE, NB]), ALU.mult)
                last.then_inc(b3_low_ready, 1)

        e_onehot_ready = sem("e_onehot_ready")
        e_listed = sem("e_listed")
        e_list_row_ready = sem("e_list_row_ready")
        e_list_ready = sem("e_list_ready")
        e_gather_list_ready = sem("e_gather_list_ready")
        e_gathered = sem("e_gathered")
        e_weight_kept = sem("e_weight_kept")
        e_transposed = sem("e_transposed")
        e_xT_ready = sem("e_xT_ready")
        e_up_ready = sem("e_up_ready")
        e_gelu_ready = sem("e_gelu_ready")
        e_hidden_ready = sem("e_hidden_ready")
        e_down_ready = sem("e_down_ready")
        e_downT_ready = sem("e_downT_ready")
        e_output_ready = sem("e_output_ready")
        e_weighed = sem("e_weighed")
        e_scattered = sem("e_scattered")
        e_pool_turns = sem("e_pool_turns")

        onehot = sb("onehot", [128, 2, NB, 128], F16)
        list_all = sb("list_all", [128, NE, 2], I32)
        gather_list = sb("gather_list", [128, 2], I32)
        scatter_list = sb("scatter_list", [128, 2], I32)
        kept = sb("kept", [128, NE, 2])
        gathered = view(stage, 0, 2, GROW)
        xT = view(stage, 288, 256)
        gelu_e = view(stage, 544, NI, CAP)
        hidden_e = view(stage, 1568, NI, CAP)
        weighed = view(stage, 2592, 2, D)
        downT = view(stage, 2848, CAP)
        list_row = view(stage, 3104, 128)[0:2]

        with nc.Block(no_gpsimd_drain=True) as block:
            @block.sync
            def _(sp):
                with sp.Fori(0, NE // 2 - 1) as g:
                    for u in range(2):
                        sp.wait_ge(e_down_ready, g * 2 + u + 1)
                        sp.dma_start(w_slots[:, u], d["expert_w"][bass.ds(g * 2 + u + 2, 1)].rearrange(
                            "o p w i -> (o p) w i")).then_inc(expert_w_loaded[u], 16)
                sp.wait_ge(e_scattered, 32 * NE)
                sp.dma_start(x_all[:, :, :], d["sums"].rearrange("(b t) c -> t b c", b=NB)).then_inc(x_loaded, 16)

            @block.gpsimd
            def _(pool):
                pool.wait_ge(rows_stored, 16)
                pool.wait_ge(sums_stored, 16)

                def step(i, u):
                    e = i - 4
                    if live(e, NE):
                        pool.wait_ge(e_weighed, e + 1)
                        pool.sem_inc(e_pool_turns, 1)
                        for m in range(2):
                            nc.gpsimd.indirect_dma_start(
                                d["sums"], bass.IndirectOffsetOnAxis(scatter_list[:, m:m + 1], 0), weighed[:, m, :], None,
                                compute_op=ALU.add).then_inc(e_scattered, 16)
                    e = i - 1
                    if live(e, NE):
                        pool.wait_ge(e_gather_list_ready, e + 1)
                        pool.sem_inc(e_pool_turns, 1)
                        for m in range(2):
                            nc.gpsimd.indirect_dma_start(
                                gathered[:, m, :], None, d["rows"], bass.IndirectOffsetOnAxis(gather_list[:, m:m + 1], 0)
                                ).then_inc(e_gathered, 16)

                skewed(pool, NE, 4, step)

            @block.tensor
            def _(pe):
                def step(i, u):
                    e = i - 3
                    if live(e, NE):
                        pe.wait_ge(e_xT_ready, e + 1)
                        pe.wait_ge(expert_w_loaded[(u + 1) % 2], 8 * (e - (u + 1) % 2) + 16)
                        for s in range(2):
                            for which in range(2):
                                for k in range(2):
                                    c = 2 * s + k
                                    last = nc.tensor.matmul(
                                        bank[1 + s + 2 * which][:, k * 256:(k + 1) * 256],
                                        w_slots[:, (u + 1) % 2, which, c * 128:(c + 1) * 128], xT, start=True, stop=True)
                            last.then_inc(e_up_ready, 1)
                    e = i - 1
                    if live(e, NE):
                        pe.wait_ge(e_onehot_ready, e + 1)
                        for b in range(NB):
                            last = nc.tensor.matmul(bank[6][0:2, 0:128], halves[:, bass.ds(e * NB + b, 1), :]
                                                    .rearrange("p o n -> p (o n)"), onehot[:, (u + 1) % 2, b, :],
                                                    start=(b == 0), stop=(b == NB - 1))
                        last.then_inc(e_listed, 1)
                    e = i - 4
                    if live(e, NE):
                        pe.wait_ge(e_downT_ready, e + 1)
                        if live(i - 2, NE):
                            pe.wait_ge(e_gather_list_ready, i - 1)
                        if live(e - 1, NE):
                            pe.wait_ge(e_weighed, e)
                        for m in range(2):
                            last = nc.tensor.transpose(bank[7][:, m * 128:(m + 1) * 128], downT[:, m * 128:(m + 1) * 128],
                                                       ident)
                        last.then_inc(e_output_ready, 1)
                    e = i - 2
                    if live(e, NE):
                        pe.wait_ge(e_gathered, 32 * e + 32)
                        for m in range(2):
                            last = nc.tensor.transpose(bank[0][:, m * 128:(m + 1) * 128], gathered[:, m, 0:D], ident)
                        last.then_inc(e_transposed, 1)
                    e = i - 1
                    if live(e, NE):
                        pe.wait_ge(e_list_row_ready, e + 1)
                        if live(i - 4, NE):
                            pe.wait_ge(e_weighed, i - 3)
                        nc.tensor.matmul(bank[7][:, 256:258], list_row, ident[0:2, 0:2], start=True, stop=True
                                         ).then_inc(e_list_ready, 1)
                    e = i - 3
                    if live(e, NE):
                        pe.wait_ge(e_hidden_ready, 2 * e + 2)
                        for k in range(NI):
                            last = nc.tensor.matmul(bank[5][:, 0:CAP], w_slots[:, (u + 1) % 2, 2, k * 128:(k + 1) * 128],
                                                    hidden_e[:, k, :], start=(k == 0), stop=(k == NI - 1))
                        last.then_inc(e_down_ready, 1)

                skewed(pe, NE, 4, step, unroll=2)

            @block.scalar
            def _(act):
                def step(i, u):
                    e = i - 4
                    if live(e, NE):
                        act.wait_ge(e_down_ready, e + 1)
                        nc.scalar.copy(downT, bank[5][:, 0:CAP]).then_inc(e_downT_ready, 1)
                    e = i - 3
                    if live(e, NE):
                        for s in range(2):
                            act.wait_ge(e_up_ready, 2 * e + 1 + s)
                            nc.scalar.activation(gelu_e[:, 2 * s:2 * s + 2, :],
                                                 bank[1 + s][:, :].rearrange("p (k t) -> p k t", k=2), ACT.Gelu
                                                 ).then_inc(e_gelu_ready, 1)
                    e = i - 1
                    if live(e, NE):
                        act.wait_ge(e_listed, e + 1)
                        nc.scalar.copy(list_row, bank[6][0:2, 0:128]).then_inc(e_list_row_ready, 1)
                    e = i - 2
                    if live(e, NE):
                        act.wait_ge(e_transposed, e + 1)
                        nc.scalar.copy(xT, bank[0][:, 0:256]).then_inc(e_xT_ready, 1)

                skewed(act, NE, 4, step)

            @block.vector
            def _(dve):
                def hidden(e, s):
                    dve.wait_ge(e_gelu_ready, 2 * e + 1 + s)
                    nc.vector.tensor_tensor(hidden_e[:, 2 * s:2 * s + 2, :], gelu_e[:, 2 * s:2 * s + 2, :],
                                            bank[3 + s][:, :].rearrange("p (k t) -> p k t", k=2), ALU.mult
                                            ).then_inc(e_hidden_ready, 1)

                def places(i, u, part):
                    for b in range(part * NB // 2, (part + 1) * NB // 2):
                        last = nc.vector.tensor_scalar(onehot[:, u, b, :], iota1, low[:, bass.ds(i * NB + b, 1)], None,
                                                       ALU.is_equal)
                    if part:
                        last.then_inc(e_onehot_ready, 1)

                def step(i, u):
                    if live(i, NE):
                        places(i, u, 0)
                    if live(i - 3, NE):
                        hidden(i - 3, 0)
                    if live(i, NE):
                        places(i, u, 1)
                    if live(i - 3, NE):
                        hidden(i - 3, 1)
                    e = i - 2
                    if live(e, NE):
                        dve.wait_ge(e_gathered, 32 * e + 32)
                        nc.vector.tensor_copy(kept[:, e, :], gathered[:, :, bass.ds(e + D, 1)].rearrange("p m o -> p (m o)")
                                              ).then_inc(e_weight_kept, 1)
                    e = i - 4
                    if live(e, NE):
                        dve.wait_ge(e_output_ready, e + 1)
                        if live(e - 1, NE):
                            dve.wait_ge(e_scattered, 32 * e)
                        nc.vector.tensor_copy(scatter_list[:, :], list_all[:, e, :])
                        nc.vector.tensor_tensor(weighed, bank[7][:, 0:256].rearrange("p (m d) -> p m d", m=2),
                                                kept[:, e, :, None].to_broadcast([128, 2, D]), ALU.mult
                                                ).then_inc(e_weighed, 1)
                    e = i - 1
                    if live(e, NE):
                        dve.wait_ge(e_list_ready, e + 1)
                        nc.vector.tensor_copy(list_all[:, e, :], bank[7][:, 256:258])
                        nc.vector.tensor_copy(gather_list[:, :], bank[7][:, 256:258]).then_inc(e_gather_list_ready, 1)

                skewed(dve, NE, 4, step, unroll=2)
                blocks = wq4_in[:, :, :].rearrange("p m (n k) -> p (m n) k", k=WBLOCK)
                q4s3 = q4s[:, :, :].rearrange("p m (n k) -> p (m n) k", k=WBLOCK)
                link(dve, nc.vector.tensor_reduce(q4m, blocks, axis=AX.X, op=ALU.max, apply_absolute_value=True))
                link(dve, nc.vector.tensor_scalar(q4m, q4m, 1.0 / WMAX, TINY, ALU.mult, ALU.max))
                link(dve, nc.vector.reciprocal(q4i, q4m))
                link(dve, nc.vector.tensor_tensor(q4s3, blocks, q4i[:, :, None].to_broadcast([128, 36, WBLOCK]), ALU.mult))
                link(dve, nc.vector.tensor_scalar(q4s, q4s, ROUND, ROUND, ALU.add, ALU.subtract))
                nc.vector.tensor_tensor(q4s3, q4s3, q4m[:, :, None].to_broadcast([128, 36, WBLOCK]), ALU.mult
                                        ).then_inc(q4_ready, 1)

        c_bn_done = sem("c_bn_done")
        c_moments = sem("c_moments")
        c_gain_ready = sem("c_gain_ready")
        c_h_ready = sem("c_h_ready")
        c_transposed = sem("c_transposed")
        c_hT_ready = sem("c_hT_ready")
        c_queried = sem("c_queried")
        c_qT_ready = sem("c_qT_ready")
        c_keys_ready = sem("c_keys_ready")
        c_scored = sem("c_scored")
        c_max_ready = sem("c_max_ready")
        c_shifted = sem("c_shifted")
        c_weights_ready = sem("c_weights_ready")
        c_weights_transposed = sem("c_weights_transposed")
        c_wT_even_ready = sem("c_wT_even_ready")
        c_wT_odd_ready = sem("c_wT_odd_ready")
        c_mixed = sem("c_mixed")
        c_inv_ready = sem("c_inv_ready")
        c_out_ready = sem("c_out_ready")
        c_x_ready = sem("c_x_ready")
        c_x_bn_done = sem("c_x_bn_done")

        masked_rstd = view(stage, 0, NB)
        masked_shift = view(stage, 16, NB)
        h1_now = view(stage, 32, 128)
        hT1 = view(stage, 160, 128)
        qT1 = view(stage, 288, 128)
        out1 = view(stage, 416, H1, DH1)
        keys_now = view(stage, 544, QUAD, CK)
        max1 = view(stage, 856, H1)
        inv1 = view(stage, 872, H1)
        weights1 = view(stage, 1024, H1 * CK)
        wT1 = sb("wT1", [CK, H1, 128])

        with nc.Block(no_gpsimd_drain=True) as block:
            @block.gpsimd
            def _(pool):
                def step(i, u):
                    b = i - 1
                    if live(b, NB):
                        if live(b - 1, NB):
                            pool.wait_ge(c_scored, b)
                        nc.gpsimd.tensor_tensor(keys_now, keys1[:, b, None, :].to_broadcast([128, QUAD, CK]),
                                                head_of_row[:, :, None].to_broadcast([128, QUAD, CK]), ALU.mult
                                                ).then_inc(c_keys_ready, 1)
                    b = i - 4
                    if live(b, NB):
                        pool.wait_ge(c_out_ready, b + 1)
                        nc.gpsimd.tensor_tensor(x_all[:, b, :], x_all[:, b, :], out1.rearrange("p h e -> p (h e)"),
                                                ALU.add).then_inc(c_x_ready, 1)

                skewed(pool, NB, 4, step)

            @block.tensor
            def _(pe):
                pe.wait_ge(q4_ready, 1)
                for m in range(3):
                    for c in range(NQ):
                        last = nc.tensor.transpose(bank[m][:, c * 128:(c + 1) * 128], q4s[:, m, c * 128:(c + 1) * 128],
                                                   ident)
                    last.then_inc(q4_transposed, 1)

                def step(i, u):
                    b = i - 4
                    if live(b, NB):
                        pe.wait_ge(c_wT_even_ready, 2 * b + 2)
                        pe.wait_ge(c_wT_odd_ready, 2 * b + 2)
                        if live(i - 1, NB):
                            pe.wait_ge(c_hT_ready, i)
                        for h in range(H1):
                            last = nc.tensor.matmul(bank[7][:, h * (DH1 + 1):(h + 1) * (DH1 + 1)], wT1[:, h, :],
                                                    values1[:, b, h, :], start=True, stop=True)
                        last.then_inc(c_mixed, 1)
                    b = i - 3
                    if live(b, NB):
                        pe.wait_ge(c_weights_ready, b + 1)
                        for g in range(QUAD):
                            if g >= 2:
                                pe.wait_ge(c_wT_even_ready if g % 2 == 0 else c_wT_odd_ready, 2 * b + 1)
                            for j in range(QUAD):
                                h = g * QUAD + j
                                last = nc.tensor.transpose(bank[4 + g % 2][0:CK, j * 128:(j + 1) * 128],
                                                           weights1[:, h * CK:(h + 1) * CK], ident)
                            last.then_inc(c_weights_transposed, 1)
                    b = i - 2
                    if live(b, NB):
                        pe.wait_ge(c_qT_ready, b + 1)
                        pe.wait_ge(c_keys_ready, b + 1)
                        for g in range(QUAD):
                            r = slice(32 * g, 32 * g + 32)
                            last = nc.tensor.matmul(bank[g][:, 0:QUAD * CK], qT1[r, :],
                                                    keys_now[r].rearrange("p j k -> p (j k)"), start=True, stop=True,
                                                    tile_position=(32 * g, 0))
                        last.then_inc(c_scored, 1)
                    b = i - 1
                    if live(b, NB):
                        pe.wait_ge(c_hT_ready, b + 1)
                        nc.tensor.matmul(bank[6][:, 0:128], wq1[:, :], hT1, start=True, stop=True
                                         ).then_inc(c_queried, 1)
                    if live(i, NB):
                        pe.wait_ge(c_h_ready, i + 1)
                        if live(i - 4, NB):
                            pe.wait_ge(c_out_ready, i - 3)
                        nc.tensor.transpose(bank[7][:, 256:384], h1_now, ident).then_inc(c_transposed, 1)

                skewed(pe, NB, 4, step)

            @block.scalar
            def _(act):
                batched_rstd(2, None, act, NB)
                act.wait_ge(c_gain_ready, 1)

                def step(i, u):
                    if live(i, NB):
                        if live(i - 1, NB):
                            act.wait_ge(c_transposed, i)
                        nc.scalar.activation(h1_now, x_all[:, i, :], ACT.Identity, bias=masked_shift[:, bass.ds(i, 1)],
                                             scale=masked_rstd[:, bass.ds(i, 1)]).then_inc(c_h_ready, 1)
                    b = i - 3
                    if live(b, NB):
                        for g in (0, 2):
                            act.wait_ge(c_weights_transposed, 4 * b + g + 1)
                            nc.scalar.copy(wT1[:, g * QUAD:(g + 1) * QUAD, :],
                                           bank[4][0:CK, :].rearrange("p (j q) -> p j q", j=QUAD)
                                           ).then_inc(c_wT_even_ready, 1)
                    b = i - 2
                    if live(b, NB):
                        act.wait_ge(c_shifted, b + 1)
                        nc.scalar.activation(weights1, weights1, ACT.Exp).then_inc(c_weights_ready, 1)
                    b = i - 1
                    if live(b, NB):
                        act.wait_ge(c_queried, b + 1)
                        nc.scalar.mul(qT1, bank[6][:, 0:128], DH1 ** -0.5).then_inc(c_qT_ready, 1)

                skewed(act, NB, 4, step)

            @block.vector
            def _(dve):
                for m in range(3):
                    dve.wait_ge(q4_transposed, m + 1)
                    nc.vector.tensor_copy(wq4[:, m, :], bank[m][:, 0:IQ])
                dve.wait_ge(x_loaded, 32)
                for b in range(NB):
                    nc.vector.bn_stats(bn[:, b, :], x_all[:, b, :]).then_inc(c_bn_done, 1)
                dve.wait_ge(c_bn_done, NB)
                for b in range(NB):
                    last = nc.vector.bn_aggr(moments[:, b, :], bn[:, b, :])
                last.then_inc(c_moments, 1)
                dve.wait_ge(c_moments, 1)
                batched_rstd(2, dve, None, NB)
                dve.wait_ge(shift_ready, 3)
                nc.vector.tensor_tensor(masked_rstd, rstd[:, 0:NB], mask_q[:, :], ALU.mult)
                nc.vector.tensor_tensor(masked_shift, shift[:, 0:NB], mask_q[:, :], ALU.mult).then_inc(c_gain_ready, 1)

                def step(i, u):
                    b = i - 4
                    if live(b, NB):
                        dve.wait_ge(c_mixed, b + 1)
                        o = bank[7][:, 0:H1 * (DH1 + 1)].rearrange("p (h e) -> p h e", h=H1)
                        if live(b - 1, NB):
                            dve.wait_ge(c_x_ready, b)
                        nc.vector.reciprocal(inv1, o[:, :, DH1]).then_inc(c_inv_ready, 1)
                        dve.wait_ge(c_inv_ready, b + 1)
                        nc.vector.tensor_tensor(out1, o[:, :, 0:DH1], inv1[:, :, None].to_broadcast([128, H1, DH1]),
                                                ALU.mult).then_inc(c_out_ready, 1)
                    b = i - 3
                    if live(b, NB):
                        for g in (1, 3):
                            dve.wait_ge(c_weights_transposed, 4 * b + g + 1)
                            nc.vector.tensor_copy(wT1[:, g * QUAD:(g + 1) * QUAD, :],
                                                  bank[5][0:CK, :].rearrange("p (j q) -> p j q", j=QUAD)
                                                  ).then_inc(c_wT_odd_ready, 1)
                    b = i - 2
                    if live(b, NB):
                        dve.wait_ge(c_scored, b + 1)
                        if live(b - 1, NB):
                            dve.wait_ge(c_shifted, b)
                        for g in range(QUAD):
                            last = nc.vector.tensor_reduce(
                                max1[:, g * QUAD:(g + 1) * QUAD], bank[g][:, 0:QUAD * CK].rearrange(
                                    "p (j k) -> p j k", j=QUAD), axis=AX.X, op=ALU.max)
                        last.then_inc(c_max_ready, 1)
                        dve.wait_ge(c_max_ready, b + 1)
                        for g in range(QUAD):
                            last = nc.vector.tensor_tensor(
                                weights1[:, g * QUAD * CK:(g + 1) * QUAD * CK].rearrange("p (j k) -> p j k", j=QUAD),
                                bank[g][:, 0:QUAD * CK].rearrange("p (j k) -> p j k", j=QUAD),
                                max1[:, g * QUAD:(g + 1) * QUAD, None].to_broadcast([128, QUAD, CK]), ALU.subtract)
                        last.then_inc(c_shifted, 1)
                    if live(i, NB):
                        dve.wait_ge(c_transposed, i + 1)
                        nc.vector.tensor_copy(hT1, bank[7][:, 256:384]).then_inc(c_hT_ready, 1)
                    b = i - 4
                    if live(b, NB):
                        dve.wait_ge(c_x_ready, b + 1)
                        nc.vector.bn_stats(bn[:, b, :], x_all[:, b, :]).then_inc(c_x_bn_done, 1)

                skewed(dve, NB, 4, step)
                dve.wait_ge(c_x_bn_done, NB)
                for b in range(NB):
                    last = nc.vector.bn_aggr(moments[:, b, :], bn[:, b, :])
                last.then_inc(x_moments_ready, 1)

        d_h_ready = sem("d_h_ready")
        d_h_max = sem("d_h_max")
        d_transposed = sem("d_transposed")
        d_hT_ready = sem("d_hT_ready")
        d_max_ready = sem("d_max_ready")
        d_all_max = sem("d_all_max")
        d_scale_ready = sem("d_scale_ready")
        d_h_ints = sem("d_h_ints")
        d_projected = sem("d_projected")
        d_copied = sem("d_copied")
        d_gate_part = sem("d_gate_part")
        d_up_part = sem("d_up_part")
        d_gate_ints = sem("d_gate_ints")
        d_sigmoid_ready = sem("d_sigmoid_ready")
        d_product_part = sem("d_product_part")
        d_up_ints = sem("d_up_ints")
        d_t_ints = sem("d_t_ints")
        d_o_part = sem("d_o_part")
        d_o_rounded = sem("d_o_rounded")
        d_o_ints = sem("d_o_ints")
        d_down = sem("d_down")
        d_y_ready = sem("d_y_ready")
        y_stored = sem("y_stored")

        h_max = view(stage, 0, NB)
        own_max = view(stage, 16, 8)
        all_max = view(stage, 24, 8)
        scale = view(stage, 32, 8)
        inv_scale = view(stage, 40, 8)
        factor = view(stage, 48, 8)
        part_max = view(stage, 64, NQ * 4)
        hd_now = view(stage, 128, 128)
        o_ints = view(stage, 256, NQ, 128)
        y_now = view(stage, 1024, 2, 128)
        gate_all = sb("gate_all", [128, NQ, NT])
        hq = hT_all
        WIDE = 512
        PIECES = NQ * NT // WIDE
        PX, PG, PU, PT, PO = range(5)

        with nc.Block(no_gpsimd_drain=True) as block:
            up_all = qkv[:, :, :].rearrange("p b c -> p (b c)")
            gate_flat = gate_all[:, :, :].rearrange("p c t -> p (c t)")

            @block.gpsimd
            def _(pool):
                for n in range(5):
                    pool.wait_ge(d_max_ready, n + 1)
                    nc.gpsimd.partition_all_reduce(all_max[:, n:n + 1], own_max[:, n:n + 1], 128, bass.bass_isa.ReduceOp.max
                                                   ).then_inc(d_all_max, 1)

            @block.tensor
            def _(pe):
                def step(i, u):
                    if live(i, NB):
                        pe.wait_ge(d_h_ready, i + 1)
                        if live(i - 1, NB):
                            pe.wait_ge(d_hT_ready, i)
                        nc.tensor.transpose(bank[0][:, 0:128], hd_now, ident).then_inc(d_transposed, 1)

                skewed(pe, NB, 0, step)
                pe.wait_ge(d_h_ints, 1)
                for which in range(2):
                    for c in range(NQ):
                        def piece(n, u):
                            k = (which * NQ + c) * 4 + n
                            if which or c or live(n - 2, 4):
                                pe.wait_ge(d_copied, k - 1)
                            nc.tensor.matmul(bank[u][:, :], wq4[:, which, c * 128:(c + 1) * 128],
                                             hq[:, bass.ds(n * WIDE, WIDE)], start=True, stop=True
                                             ).then_inc(d_projected, 1)

                        for n in range(4):
                            piece(n, n % 2)

                def down(b, u):
                    if live(b, NB):
                        pe.wait_ge(d_o_ints, b + 1)
                        if live(b - 1, NB):
                            pe.wait_ge(d_y_ready, b)
                        for c in range(NQ):
                            last = nc.tensor.matmul(bank[2][:, 0:128], o_ints[:, c, :],
                                                    wq4[:, 2, c * 128:(c + 1) * 128], start=(c == 0), stop=(c == NQ - 1))
                        last.then_inc(d_down, 1)

                down(0, 0)
                with pe.Fori(1, NB) as b:
                    down(b, 0)

            @block.scalar
            def _(act):
                batched_rstd(3, None, act, NB)

                def step(i, u):
                    if live(i, NB):
                        act.wait_ge(d_transposed, i + 1)
                        nc.scalar.copy(hq[:, bass.ds(i * T, T)], bank[0][:, 0:128]).then_inc(d_hT_ready, 1)

                skewed(act, NB, 0, step)
                for which in range(2):
                    dst = (gate_flat, up_all)[which]
                    for n in range(PIECES):
                        k = which * PIECES + n
                        act.wait_ge(d_projected, k + 1)
                        nc.scalar.copy(dst[:, n * WIDE:(n + 1) * WIDE], bank[n % 2][:, :]).then_inc(d_copied, 1)
                for n in range(NQ):
                    act.wait_ge(d_gate_ints, n + 1)
                    nc.scalar.activation(sig_all[:, n * NT:(n + 1) * NT], gate_flat[:, n * NT:(n + 1) * NT], ACT.Sigmoid,
                                         scale=scale[:, PG:PG + 1]).then_inc(d_sigmoid_ready, 1)

            @block.vector
            def _(dve):
                batched_rstd(3, dve, None, NB)
                dve.wait_ge(shift_ready, 4)

                def step(i, u):
                    if live(i, NB):
                        if live(i - 1, NB):
                            dve.wait_ge(d_transposed, i)
                            dve.wait_ge(d_h_max, i)
                        nc.vector.tensor_scalar(hd_now, x_all[:, i, :], rstd[:, bass.ds(i, 1)], shift[:, bass.ds(i, 1)],
                                                ALU.mult, ALU.add).then_inc(d_h_ready, 1)
                        dve.wait_ge(d_h_ready, i + 1)
                        nc.vector.tensor_reduce(h_max[:, bass.ds(i, 1)], hd_now, axis=AX.X, op=ALU.max,
                                                apply_absolute_value=True).then_inc(d_h_max, 1)

                skewed(dve, NB, 0, step)
                def new_scale(n, parts, unit):
                    link(dve, nc.vector.tensor_reduce(own_max[:, n:n + 1], parts, axis=AX.X, op=ALU.max))
                    nc.vector.tensor_copy(own_max[:, n:n + 1], own_max[:, n:n + 1]).then_inc(d_max_ready, 1)
                    dve.wait_ge(d_all_max, n + 1)
                    col = slice(n, n + 1)
                    if unit is None:
                        link(dve, nc.vector.tensor_scalar(scale[:, col], all_max[:, col], 1.0 / QMAX, TINY, ALU.mult, ALU.max))
                        link(dve, nc.vector.reciprocal(factor[:, col], scale[:, col]))
                    else:
                        link(dve, nc.vector.tensor_scalar(scale[:, col], all_max[:, col], unit, 1.0 / QMAX, ALU.mult, ALU.mult))
                        link(dve, nc.vector.tensor_scalar(scale[:, col], scale[:, col], TINY, None, ALU.max))
                        link(dve, nc.vector.reciprocal(inv_scale[:, col], scale[:, col]))
                        link(dve, nc.vector.tensor_tensor(factor[:, col], inv_scale[:, col], unit, ALU.mult))

                def rounded(dst, src, n, signal):
                    link(dve, nc.vector.tensor_scalar(dst, src, factor[:, n:n + 1], ROUND, ALU.mult, ALU.add))
                    nc.vector.tensor_scalar(dst, dst, ROUND, None, ALU.subtract).then_inc(signal, 1)

                unit = view(stage, 56, 8)
                dve.wait_ge(d_h_max, NB)
                dve.wait_ge(d_hT_ready, NB)
                new_scale(PX, h_max, None)
                rounded(hq[:, :], hq[:, :], PX, d_h_ints)
                for which, part in ((0, d_gate_part), (1, d_up_part)):
                    src = (gate_flat, up_all)[which]
                    for n in range(PIECES):
                        dve.wait_ge(d_copied, which * PIECES + n + 1)
                        nc.vector.tensor_reduce(part_max[:, n:n + 1], src[:, n * WIDE:(n + 1) * WIDE], axis=AX.X, op=ALU.max,
                                                apply_absolute_value=True).then_inc(part, 1)
                    dve.wait_ge(part, PIECES)
                    new_scale(PG + which, part_max, scale[:, PX:PX + 1])
                    if which == 0:
                        for n in range(NQ):
                            piece = gate_flat[:, n * NT:(n + 1) * NT]
                            rounded(piece, piece, PG, d_gate_ints)
                for n in range(NQ):
                    piece = up_all[:, n * NT:(n + 1) * NT]
                    rounded(piece, piece, PU, d_up_ints)
                for n in range(NQ):
                    s, g = (t[:, n * NT:(n + 1) * NT] for t in (sig_all, gate_flat))
                    dve.wait_ge(d_sigmoid_ready, n + 1)
                    link(dve, nc.vector.tensor_scalar(s, s, 65536.0, ROUND, ALU.mult, ALU.add))
                    link(dve, nc.vector.tensor_scalar(s, s, ROUND, 65535.0, ALU.subtract, ALU.min))
                    link(dve, nc.vector.tensor_tensor(s, s, g, ALU.mult))
                    nc.vector.tensor_reduce(part_max[:, n:n + 1], s, axis=AX.X, op=ALU.max, apply_absolute_value=True
                                            ).then_inc(d_product_part, 1)
                dve.wait_ge(d_product_part, NQ)
                link(dve, nc.vector.tensor_scalar(unit[:, 0:1], scale[:, PG:PG + 1], 1.0 / 65536.0, None, ALU.mult))
                new_scale(PT, part_max[:, 0:NQ], unit[:, 0:1])
                for n in range(NQ):
                    s, up = (t[:, n * NT:(n + 1) * NT] for t in (sig_all, up_all))
                    rounded(s, s, PT, d_t_ints)
                    dve.wait_ge(d_t_ints, n + 1)
                    link(dve, nc.vector.tensor_tensor(s, s, up, ALU.mult))
                    nc.vector.tensor_reduce(part_max[:, n:n + 1], s, axis=AX.X, op=ALU.max, apply_absolute_value=True
                                            ).then_inc(d_o_part, 1)
                dve.wait_ge(d_o_part, NQ)
                link(dve, nc.vector.tensor_tensor(unit[:, 1:2], scale[:, PT:PT + 1], scale[:, PU:PU + 1], ALU.mult))
                new_scale(PO, part_max[:, 0:NQ], unit[:, 1:2])

                def out(b, u):
                    if live(b, NB):
                        if live(b - 1, NB):
                            dve.wait_ge(d_down, b)
                        o3 = sig_all[:, :].rearrange("p (c t) -> p c t", c=NQ)
                        nc.vector.tensor_scalar(o_ints, o3[:, :, bass.ds(b * T, T)], factor[:, PO:PO + 1], ROUND,
                                                ALU.mult, ALU.add).then_inc(d_o_rounded, 1)
                        dve.wait_ge(d_o_rounded, b + 1)
                        nc.vector.tensor_scalar(o_ints, o_ints, ROUND, None, ALU.subtract).then_inc(d_o_ints, 1)
                        dve.wait_ge(d_down, b + 1)
                        nc.vector.scalar_tensor_tensor(x_all[:, b, :], bank[2][:, 0:128], scale[:, PO:PO + 1],
                                                       x_all[:, b, :], ALU.mult, ALU.add).then_inc(d_y_ready, 1)

                out(0, 0)
                with dve.Fori(1, NB) as b:
                    out(b, 0)

            @block.sync
            def _(sp):
                for g in range(4):
                    sp.wait_ge(d_y_ready, 4 * g + 4)
                    sp.dma_start(d["out"][4 * g:4 * g + 4].rearrange("b t d -> t b d"), x_all[:, 4 * g:4 * g + 4, :]
                                 ).then_inc(y_stored, 16)
                sp.wait_ge(y_stored, 64)


def kernel(**inputs):
    import ml_dtypes
    import numpy as np
    from concourse import bacc, mybir
    from concourse.bass_utils import run_bass_kernel_spmd

    a = {k: np.asarray(v) for k, v in inputs.items()}
    k = np.arange(128)
    eye = np.eye(128, dtype=np.float32)
    const = np.concatenate([
        eye,
        ((k[:, None] % 32) // DH1 == np.arange(QUAD)[None, :]).astype(np.float32),
        np.tile(np.float32([2.0 ** max(0, BITS - 3 - n) * (n < BITS - 2) for n in range(BITS)]), (128, 1)),
        (np.arange(NB)[None, :] * T + k[:, None]).astype(np.float32),
        np.tile((np.arange(NE * NB) % NB != 0).astype(np.float32), (128, 1)),
    ], axis=1)
    const16 = np.concatenate([
        (k[:, None] < k[None, :]).astype(np.float32),
        np.ones((128, 128), np.float32),
        (k[:, None] % NE == k[None, :] % NE).astype(np.float32),
        np.tile((k + 1).astype(np.float32), (128, 1)),
    ], axis=1).astype(ml_dtypes.bfloat16)
    bit_int = np.tile(np.array([2 ** max(0, BITS - 3 - n) * (n < BITS - 2) for n in range(BITS)], np.int32), (128, 1))
    columns = np.zeros((128, 8), np.float32)
    columns[:, 0], columns[:, 1] = a["L0_xattn_ln_l_g"], a["L0_xattn_ln_l_b"]
    columns[:CD, 2], columns[:CD, 3] = a["L0_xattn_ln_x_g"], a["L0_xattn_ln_x_b"]
    columns[:, 4], columns[:, 5] = np.tile(a["L0_xattn_qn_g"], H0), np.tile(a["L0_xattn_kn_g"], H0)

    def chunks(w):
        return np.ascontiguousarray(w.reshape(-1, 128, w.shape[1]).transpose(1, 0, 2))

    arrays = {
        "x": a["x"], "context": a["ctx_768"], "context_t": a["ctx_768"].transpose(2, 0, 1),
        "mask_k": a["mask_BxS2_bk0"].reshape(-1), "mask_q": a["mask_BxS_bk0"].T,
        "const": const, "const16": const16, "bit_int": bit_int, "columns": columns,
        "w_token": np.concatenate([a["L0_xattn_Wq"], a["L0_xattn_Wlkv"]]).T,
        "w_context": a["L0_xattn_Wkv"].T, "w_out": a["L0_xattn_Wo"].T, "bias_out": a["L0_xattn_bo"],
        "wq1": a["L1_xattn_Wq"].T, "wkv1": a["L1_xattn_Wkv"].T, "gate_w": a["L0_ffn_gate_w"].T,
        "shared_up": np.stack([a["L0_ffn_Sg"].T, a["L0_ffn_Su"].T], axis=1),
        "shared_down": chunks(a["L0_ffn_Sd"].T),
        "expert_w": np.stack([a["L0_ffn_Wg"].transpose(0, 2, 1), a["L0_ffn_Wu"].transpose(0, 2, 1),
                              a["L0_ffn_Wd"].transpose(0, 2, 1).reshape(NE, NI, 128, 128).transpose(0, 2, 1, 3)
                              .reshape(NE, 128, IE)], axis=2),
        "w_gate": a["L1_ffn_w_gate"], "w_up": a["L1_ffn_w_up"], "w_down": a["L1_ffn_w_down"],
    }
    nc = bacc.Bacc("TRN2", target_bir_lowering=False, num_devices=1)
    dram = {}
    for name, v in arrays.items():
        arrays[name] = v = np.ascontiguousarray(v)
        dram[name] = nc.dram_tensor(f"in_{name}", v.shape, mybir.dt.from_np(v.dtype), kind="ExternalInput").ap()
    dram["rows"] = nc.dram_tensor("rows", (NT, GROW), mybir.dt.float32).ap()
    dram["sums"] = nc.dram_tensor("sums", (NT, D), mybir.dt.float32).ap()
    dram["out"] = nc.dram_tensor("out", (NB, T, D), mybir.dt.float32, kind="ExternalOutput").ap()
    build(nc, dram)
    r = run_bass_kernel_spmd(nc, [{f"in_{name}": v for name, v in arrays.items()}], core_ids=[0])
    return r.results[0]["out"]
```

```python
from contextlib import ExitStack

import concourse.bass as bass
import concourse.mybir as mybir

F32, BF16, F16, I32, U8 = (mybir.dt.float32, mybir.dt.bfloat16, mybir.dt.float16, mybir.dt.int32, mybir.dt.uint8)
ALU = mybir.AluOpType
ACT = mybir.ActivationFunctionType
AX = mybir.AxisListType

NB, T, D = 16, 128, 128
NT = NB * T
CK, CD = 77, 96
H0, DH0 = 2, 64
KEYS0 = CK + T
H1, DH1 = 16, 8
QUAD = 4
NE, CAP, IE = 16, 256, 512
NI = IE // 128
IS = 256
IQ = 384
NQ = IQ // 128
WBLOCK = 32
GROW = D + NE
LN_EPS, RMS_EPS = 1e-5, 1e-8
MASKED = -(2.0 ** 100)
ROUND = 1.5 * 2.0 ** 23
QMAX, WMAX, TINY = 32767.0, 7.0, 1e-12
BITS = 32


def live(b, n):
    return 0 <= b < n if isinstance(b, int) else True


def skewed(eng, n, lag, body, unroll=1):
    for i in range(lag):
        body(i, i % unroll)
    with eng.Fori(lag // unroll, n // unroll) as g:
        for u in range(unroll):
            body(g * unroll + u, u)
    for i in range(n, n + lag):
        body(i, i % unroll)


def build(nc, d, last_phase=9):
    with ExitStack() as ctx:
        def sb(name, shape, dt=F32):
            return ctx.enter_context(nc.sbuf_tensor(name, shape, dt))

        def sem(name):
            return ctx.enter_context(nc.semaphore(name))

        bank = [ctx.enter_context(nc.psum_tensor(f"bank{n}", [128, 512], F32)) for n in range(8)]

        x_all = sb("x_all", [128, NB, D])
        moments = sb("moments", [128, 2 * NB, 2])
        variance = sb("variance", [128, 2 * NB])
        deviation = sb("deviation", [128, 2 * NB])
        rstd = sb("rstd", [128, 2 * NB])
        shift = sb("shift", [128, 2 * NB])
        bn = sb("bn", [128, 2 * NB, 6])
        const = sb("const", [128, d["const"].shape[1]])
        const16 = sb("const16", [128, d["const16"].shape[1]], BF16)
        ident = const[:, 0:128]
        head_of_row = const[:, 128:132]
        bit_value = const[:, 132:132 + BITS]
        token_id = const[:, 164:180]
        first_batch = const[:, 180:436]
        before = const16[:, 0:128]
        ones16 = const16[:, 128:256]
        same_expert = const16[:, 256:384]
        iota1 = const16[:, 384:512]
        bit_int = sb("bit_int", [128, BITS], I32)
        stage = sb("stage", [128, 4096])

        def view(tensor, start, *shape):
            n = 1
            for s in shape:
                n *= s
            flat = tensor[:, start:start + n]
            if len(shape) == 1:
                return flat
            names = "abc"[:len(shape)]
            return flat.rearrange(f"p ({' '.join(names)}) -> p {' '.join(names)}",
                                  **{k: v for k, v in zip(names, shape)})

        loads = sem("loads")
        N_LOADS = [0]

        def load(eng, dst, src):
            eng.dma_start(dst, src).then_inc(loads, 16)
            N_LOADS[0] += 1

        w_token = sb("w_token", [128, 384])
        w_context = sb("w_context", [CD, 256])
        w_out = sb("w_out", [128, 128])
        bias_out = sb("bias_out", [128, 128])
        columns = sb("columns", [128, 8])
        wq1 = sb("wq1", [128, 128])
        wkv1 = sb("wkv1", [CD, 256])
        gate_w = sb("gate_w", [128, NE])
        shared_up = sb("shared_up", [128, 2, IS])
        shared_down = sb("shared_down", [128, 2, 128])
        wq4_in = sb("wq4_in", [128, 3, IQ])
        wq4 = sb("wq4", [128, 3, IQ])
        mask_q8 = sb("mask_q8", [128, NB], U8)
        mask_q = sb("mask_q", [128, NB])
        mask_k8 = sb("mask_k8", [1, NB * CK], U8)
        mask_k = sb("mask_k", [1, NB * CK], BF16)
        sig_all = sb("sig_all", [128, NQ * NT])
        context = sig_all[0:CK, NB * 256:NB * (256 + CD)].rearrange("k (b d) -> k b d", b=NB)
        context_t = sb("context_t", [CD, NB, CK])
        qkv = sb("qkv", [128, NB, 384])
        ctx_kv = sig_all[0:CK, 0:NB * 256].rearrange("k (b n) -> k b n", b=NB)
        keys1 = sb("keys1", [128, NB, CK])
        values1 = sb("values1", [CK, NB, H1, DH1 + 1])
        norms = sb("norms", [128, NB, 6])
        inv_norms = sb("inv_norms", [128, NB, 6])
        w_slots = sb("w_slots", [128, 2, 3, IE])

        memory_set = sem("memory_set")
        bn_done = sem("bn_done")
        var_ready = sem("var_ready")
        dev_ready = sem("dev_ready")
        rstd_ready = sem("rstd_ready")
        shift_ready = sem("shift_ready")
        q4_ready = sem("q4_ready")
        q4_transposed = sem("q4_transposed")
        gain_ready = sem("gain_ready")
        x_loaded = sem("x_loaded")
        ctx_loaded = sem("ctx_loaded")

        vector_chain = sem("vector_chain")
        linked = [0]

        def link(dve, instruction):
            linked[0] += 1
            instruction.then_inc(vector_chain, 1)
            dve.wait_ge(vector_chain, linked[0])

        q4_work = sb("q4_work", [128, 3 * IQ + 72])
        q4s = view(q4_work, 0, 3, IQ)
        q4m = view(q4_work, 1152, 36)
        q4i = view(q4_work, 1188, 36)
        def batched_rstd(k, dve, act, n):
            if dve is not None:
                if n == 2 * NB:
                    nc.vector.tensor_scalar(variance[:, 0:NB], moments[:, 0:NB, 1], 1.0 + LN_EPS, LN_EPS * LN_EPS,
                                            ALU.mult, ALU.add)
                    nc.vector.tensor_scalar(variance[:, NB:2 * NB], moments[:, NB:2 * NB, 1], LN_EPS, None,
                                            ALU.add).then_inc(var_ready, 1)
                else:
                    nc.vector.tensor_scalar(variance[:, 0:n], moments[:, 0:n, 1], LN_EPS, None,
                                            ALU.add).then_inc(var_ready, 1)
                dve.wait_ge(dev_ready, k + 1)
                nc.vector.reciprocal(rstd[:, 0:n], deviation[:, 0:n]).then_inc(rstd_ready, 1)
                dve.wait_ge(rstd_ready, k + 1)
                nc.vector.scalar_tensor_tensor(shift[:, 0:n], moments[:, 0:n, 0], -1.0, rstd[:, 0:n],
                                               ALU.mult, ALU.mult).then_inc(shift_ready, 1)
            if act is not None:
                act.wait_ge(var_ready, k + 1)
                nc.scalar.activation(deviation[:, 0:n], variance[:, 0:n], ACT.Sqrt).then_inc(dev_ready, 1)

        with nc.Block(no_gpsimd_drain=True) as block:
            @block.sync
            def _(sp):
                sp.dma_start(x_all[:, :, :], d["x"].rearrange("b t d -> t b d")).then_inc(x_loaded, 16)
                load(sp, const[:, :], d["const"])
                load(sp, columns[:, :], d["columns"])
                load(sp, w_token[:, :], d["w_token"])
                load(sp, w_context[:, :], d["w_context"])
                load(sp, w_out[:, :], d["w_out"])
                load(sp, bias_out[:, :], d["bias_out"].rearrange("(a n) -> a n", a=1).to_broadcast([128, 128]))
                load(sp, wq4_in[:, 0, :].rearrange("p (c i) -> p c i", c=NQ), d["w_gate"].rearrange("(c p) i -> p c i", p=128))
                load(sp, wq4_in[:, 1, :].rearrange("p (c i) -> p c i", c=NQ), d["w_up"].rearrange("(c p) i -> p c i", p=128))
                load(sp, wq4_in[:, 2, :], d["w_down"])

            @block.scalar
            def _(act):
                act.dma_start(context[:, :, :], d["context"].rearrange("b k d -> k b d")).then_inc(ctx_loaded, 16)
                load(act, const16[:, :], d["const16"])
                load(act, context_t[:, :, :], d["context_t"])
                load(act, bit_int[:, :], d["bit_int"])
                load(act, wq1[:, :], d["wq1"])
                load(act, wkv1[:, :], d["wkv1"])
                load(act, gate_w[:, :], d["gate_w"])
                load(act, shared_up[:, :, :], d["shared_up"])
                load(act, shared_down[:, :, :], d["shared_down"])
                load(act, mask_q8[:, :], d["mask_q"])
                load(act, mask_k8[:, :], d["mask_k"].rearrange("(a n) -> a n", a=1))
                batched_rstd(0, None, act, 2 * NB)

            @block.gpsimd
            def _(pool):
                nc.gpsimd.memset(moments[:, :, :], 1.0).then_inc(memory_set, 1)
                nc.gpsimd.memset(norms[:, :, :], 1.0).then_inc(memory_set, 1)
                nc.gpsimd.memset(values1[:, :, :, DH1:DH1 + 1], 1.0).then_inc(memory_set, 1)

            @block.vector
            def _(dve):
                dve.wait_ge(memory_set, 3)
                dve.wait_ge(x_loaded, 16)
                for b in range(NB):
                    nc.vector.bn_stats(bn[:, b, :], x_all[:, b, :]).then_inc(bn_done, 1)
                dve.wait_ge(ctx_loaded, 16)
                for b in range(NB):
                    nc.vector.bn_stats(bn[0:CK, NB + b, :], context[:, b, :]).then_inc(bn_done, 1)
                dve.wait_ge(bn_done, 2 * NB)
                for b in range(2 * NB):
                    p = 128 if b < NB else CK
                    last = nc.vector.bn_aggr(moments[0:p, b, :], bn[0:p, b, :])
                link(dve, last)
                batched_rstd(0, dve, None, 2 * NB)
                dve.wait_ge(loads, 16 * N_LOADS[0])
                nc.vector.tensor_copy(mask_q[:, :], mask_q8[:, :])
                nc.vector.tensor_scalar(mask_k[:, :], mask_k8[:, :], -1.0, -MASKED, ALU.add, ALU.mult)
                nc.vector.scalar_tensor_tensor(columns[:, 6:7], columns[:, 4:5], DH0 ** -0.5, columns[:, 5:6],
                                               ALU.mult, ALU.mult).then_inc(gain_ready, 1)

        a1_xn_ready = sem("a1_xn_ready")
        a1_cn_ready = sem("a1_cn_ready")
        a1_transposed = sem("a1_transposed")
        a1_lnT_ready = sem("a1_lnT_ready")
        a1_cnT_ready = sem("a1_cnT_ready")
        a1_rawT_ready = sem("a1_rawT_ready")
        a1_projected = sem("a1_projected")
        a1_qkv_ready = sem("a1_qkv_ready")
        a1_keys1_ready = sem("a1_keys1_ready")
        a1_ctx_kv_ready = sem("a1_ctx_kv_ready")
        a1_values1_ready = sem("a1_values1_ready")
        a1_squares_ready = sem("a1_squares_ready")
        a1_ctx_squares_ready = sem("a1_ctx_squares_ready")
        a1_sums_ready = sem("a1_sums_ready")
        a1_norms_ready = sem("a1_norms_ready")

        xn = view(stage, 0, 128)
        cn = view(stage, 128, CD)[0:CK]
        lnT = view(stage, 256, 128)
        cnT = view(stage, 384, CK)[0:CD]
        rawT = view(stage, 464, CK)[0:CD]
        squares = view(stage, 544, 4, DH0)
        ctx_squares = view(stage, 800, 2, DH0)[0:CK]

        with nc.Block(no_gpsimd_drain=True) as block:
            @block.gpsimd
            def _(pool):
                def step(i, u):
                    if live(i, NB):
                        if live(i - 1, NB):
                            pool.wait_ge(a1_projected, i)
                        nc.gpsimd.tensor_copy(rawT, context_t[:, i, :]).then_inc(a1_rawT_ready, 1)
                        pool.wait_ge(a1_xn_ready, i + 1)
                        nc.gpsimd.tensor_tensor(x_all[:, i, :], x_all[:, i, :], bias_out[:, :], ALU.add)
                    b = i - 1
                    if live(b, NB):
                        if live(b - 1, NB):
                            pool.wait_ge(a1_sums_ready, b)
                        pool.wait_ge(a1_qkv_ready, b + 1)
                        qk = qkv[:, b, 0:256].rearrange("p (h e) -> p h e", h=4)
                        nc.gpsimd.tensor_tensor(squares, qk, qk, ALU.mult).then_inc(a1_squares_ready, 1)
                        pool.wait_ge(a1_ctx_kv_ready, b + 1)
                        ck = ctx_kv[:, b, 0:128].rearrange("p (h e) -> p h e", h=2)
                        nc.gpsimd.tensor_tensor(ctx_squares, ck, ck, ALU.mult).then_inc(a1_ctx_squares_ready, 1)

                skewed(pool, NB, 2, step)

            @block.vector
            def _(dve):
                def step(i, u):
                    if live(i, NB):
                        if live(i - 1, NB):
                            dve.wait_ge(a1_transposed, i)
                        nc.vector.tensor_scalar(xn, x_all[:, i, :], rstd[:, bass.ds(i, 1)], shift[:, bass.ds(i, 1)],
                                                ALU.mult, ALU.add).then_inc(a1_xn_ready, 1)
                    b = i - 1
                    if live(b, NB):
                        dve.wait_ge(a1_projected, b + 1)
                        nc.vector.tensor_copy(ctx_kv[:, b, :], bank[2][0:CK, 0:256]).then_inc(a1_ctx_kv_ready, 1)
                        nc.vector.tensor_copy(values1[:, b, :, 0:DH1], bank[2][0:CK, 336:464].rearrange(
                            "p (h e) -> p h e", h=H1)).then_inc(a1_values1_ready, 1)
                    if live(i, NB):
                        dve.wait_ge(a1_transposed, i + 1)
                        nc.vector.tensor_scalar(cnT, bank[3][0:CD, 0:CK], columns[0:CD, 2:3], columns[0:CD, 3:4],
                                                ALU.mult, ALU.add).then_inc(a1_cnT_ready, 1)
                    b = i - 2
                    if live(b, NB):
                        dve.wait_ge(a1_squares_ready, b + 1)
                        nc.vector.tensor_reduce(norms[:, b, 0:4], squares, axis=AX.X, op=ALU.add)
                        dve.wait_ge(a1_ctx_squares_ready, b + 1)
                        nc.vector.tensor_reduce(norms[0:CK, b, 4:6], ctx_squares, axis=AX.X,
                                                op=ALU.add).then_inc(a1_sums_ready, 1)

                skewed(dve, NB, 2, step)
                dve.wait_ge(a1_norms_ready, 1)
                link(dve, nc.vector.tensor_scalar(norms[:, :, :], norms[:, :, :], RMS_EPS, None, ALU.max
                                        ))
                nc.vector.reciprocal(inv_norms[:, :, :], norms[:, :, :])

            @block.scalar
            def _(act):
                def step(i, u):
                    if live(i, NB):
                        if live(i - 1, NB):
                            act.wait_ge(a1_transposed, i)
                        nc.scalar.activation(cn, context[:, i, :], ACT.Identity, bias=shift[0:CK, bass.ds(i + NB, 1)],
                                             scale=rstd[0:CK, bass.ds(i + NB, 1)]).then_inc(a1_cn_ready, 1)
                    b = i - 1
                    if live(b, NB):
                        act.wait_ge(a1_projected, b + 1)
                        nc.scalar.copy(qkv[:, b, :], bank[1][:, 0:384]).then_inc(a1_qkv_ready, 1)
                        nc.scalar.copy(keys1[:, b, :], bank[4][:, 0:CK]).then_inc(a1_keys1_ready, 1)
                    if live(i, NB):
                        act.wait_ge(a1_transposed, i + 1)
                        nc.scalar.activation(lnT, bank[0][:, 0:128], ACT.Identity, bias=columns[:, 1:2],
                                             scale=columns[:, 0:1]).then_inc(a1_lnT_ready, 1)

                skewed(act, NB, 2, step)
                act.wait_ge(a1_sums_ready, NB)
                nc.scalar.activation(norms[:, :, :], norms[:, :, :], ACT.Sqrt, scale=1.0 / DH0
                                     ).then_inc(a1_norms_ready, 1)

            @block.tensor
            def _(pe):
                def step(i, u):
                    b = i - 1
                    if live(b, NB):
                        pe.wait_ge(a1_lnT_ready, b + 1)
                        if live(b - 1, NB):
                            pe.wait_ge(a1_qkv_ready, b)
                            pe.wait_ge(a1_keys1_ready, b)
                            pe.wait_ge(a1_values1_ready, b)
                        nc.tensor.matmul(bank[1][:, 0:384], lnT, w_token[:, :], start=True, stop=True)
                        pe.wait_ge(a1_cnT_ready, b + 1)
                        nc.tensor.matmul(bank[2][0:CK, 0:256], cnT, w_context[:, :], start=True, stop=True)
                        pe.wait_ge(a1_rawT_ready, b + 1)
                        nc.tensor.matmul(bank[4][:, 0:CK], wkv1[:, 0:128], rawT, start=True, stop=True)
                        nc.tensor.matmul(bank[2][0:CK, 336:464], rawT, wkv1[:, 128:256], start=True, stop=True
                                         ).then_inc(a1_projected, 1)
                    if live(i, NB):
                        pe.wait_ge(a1_xn_ready, i + 1)
                        nc.tensor.transpose(bank[0][:, 0:128], xn, ident)
                        pe.wait_ge(a1_cn_ready, i + 1)
                        nc.tensor.transpose(bank[3][0:CD, 0:CK], cn, ident[0:CK, 0:CK]
                                            ).then_inc(a1_transposed, 1)

                skewed(pe, NB, 2, step)

        a2_q_normed = sem("a2_q_normed")
        a2_k_normed = sem("a2_k_normed")
        a2_transposed = sem("a2_transposed")
        a2_qT_ready = sem("a2_qT_ready")
        a2_kT_ready = sem("a2_kT_ready")
        a2_scored = sem("a2_scored")
        a2_max_ready = sem("a2_max_ready")
        a2_weights_ready = sem("a2_weights_ready")
        a2_weights_transposed = sem("a2_weights_transposed")
        a2_ctx_wT_ready = sem("a2_ctx_wT_ready")
        a2_lat_wT_ready = sem("a2_lat_wT_ready")
        a2_mixed = sem("a2_mixed")
        a2_inv_sum_ready = sem("a2_inv_sum_ready")
        a2_out_normed = sem("a2_out_normed")
        a2_out_transposed = sem("a2_out_transposed")
        a2_outT_ready = sem("a2_outT_ready")
        a2_out_projected = sem("a2_out_projected")
        a2_x_ready = sem("a2_x_ready")
        a2_x_bn_done = sem("a2_x_bn_done")
        x_moments_ready = sem("x_moments_ready")

        qk_n = view(stage, 0, 4, DH0)
        ck_n = view(stage, 256, 2, DH0)[0:CK]
        qT = view(stage, 384, 128)
        kT = view(stage, 512, KEYS0)
        weights = view(stage, 720, H0, KEYS0)
        ctx_wT = view(stage, 1136, H0, 128)[0:CK]
        lat_wT = view(stage, 1392, H0, 128)
        out_n = view(stage, 1648, H0, DH0)
        outT = view(stage, 1776, 128)
        neg_max = view(stage, 1904, H0)
        weight_sum = [view(stage, 1906, H0), view(stage, 1908, H0)]
        inv_sum = view(stage, 1910, H0)
        score = [bank[2], bank[3]]

        with nc.Block(no_gpsimd_drain=True) as block:
            @block.gpsimd
            def _(pool):
                def step(i, u):
                    if live(i, NB):
                        if live(i - 1, NB):
                            pool.wait_ge(a2_transposed, i)
                        nc.gpsimd.tensor_tensor(qk_n, qkv[:, i, 0:256].rearrange("p (h e) -> p h e", h=4),
                                                inv_norms[:, i, 0:4, None].to_broadcast([128, 4, DH0]), ALU.mult
                                                ).then_inc(a2_q_normed, 1)
                        nc.gpsimd.tensor_tensor(ck_n, ctx_kv[:, i, 0:128].rearrange("p (h e) -> p h e", h=2),
                                                inv_norms[0:CK, i, 4:6, None].to_broadcast([CK, 2, DH0]), ALU.mult
                                                ).then_inc(a2_k_normed, 1)

                skewed(pool, NB, 0, step)

            @block.tensor
            def _(pe):
                qk_flat = qk_n.rearrange("p h e -> p (h e)")
                ck_flat = ck_n.rearrange("p h e -> p (h e)")

                def step(i, u):
                    b = i - 5
                    if live(b, NB):
                        pe.wait_ge(a2_outT_ready, b + 1)
                        if live(b - 1, NB):
                            pe.wait_ge(a2_x_ready, b)
                        nc.tensor.matmul(bank[7][:, 0:128], outT, w_out[:, :], start=True, stop=True
                                         ).then_inc(a2_out_projected, 1)
                    b = i - 4
                    if live(b, NB):
                        pe.wait_ge(a2_out_normed, b + 1)
                        if live(i - 1, NB):
                            pe.wait_ge(a2_qT_ready, i)
                        nc.tensor.transpose(bank[0][:, 128:256], out_n.rearrange("p h e -> p (h e)"), ident
                                            ).then_inc(a2_out_transposed, 1)
                    b = i - 3
                    if live(b, NB):
                        pe.wait_ge(a2_ctx_wT_ready, b + 1)
                        pe.wait_ge(a2_lat_wT_ready, b + 1)
                        for h in range(H0):
                            o = bank[6][:, h * DH0:(h + 1) * DH0]
                            nc.tensor.matmul(o, ctx_wT[:, h, :], ctx_kv[:, b, 128 + h * DH0:128 + (h + 1) * DH0],
                                             start=True, stop=False)
                            last = nc.tensor.matmul(o, lat_wT[:, h, :], qkv[:, b, 256 + h * DH0:256 + (h + 1) * DH0],
                                                    start=False, stop=True)
                        last.then_inc(a2_mixed, 1)
                    b = i - 2
                    if live(b, NB):
                        pe.wait_ge(a2_weights_ready, b + 1)
                        for h in range(H0):
                            nc.tensor.transpose(bank[4][0:CK, h * 128:(h + 1) * 128], weights[:, h, 0:CK], ident)
                            last = nc.tensor.transpose(bank[5][:, h * 128:(h + 1) * 128], weights[:, h, CK:KEYS0],
                                                       ident)
                        last.then_inc(a2_weights_transposed, 1)
                    b = i - 1
                    if live(b, NB):
                        pe.wait_ge(a2_qT_ready, b + 1)
                        pe.wait_ge(a2_kT_ready, b + 1)
                        for h in range(H0):
                            rows = slice(h * DH0, (h + 1) * DH0)
                            nc.tensor.matmul(score[h][:, 0:KEYS0], qT[rows, :], kT[rows, :], start=True, stop=False)
                            last = nc.tensor.matmul(score[h][:, 0:CK], ones16[0:1, :], mask_k[:, bass.ds(b * CK, CK)],
                                                    start=False, stop=True)
                        last.then_inc(a2_scored, 1)
                    if live(i, NB):
                        pe.wait_ge(a2_q_normed, i + 1)
                        pe.wait_ge(a2_k_normed, i + 1)
                        if live(i - 4, NB):
                            pe.wait_ge(a2_outT_ready, i - 3)
                        nc.tensor.transpose(bank[0][:, 0:128], qk_flat[:, 0:128], ident)
                        nc.tensor.transpose(bank[1][:, 0:CK], ck_flat, ident[0:CK, 0:CK])
                        nc.tensor.transpose(bank[1][:, CK:KEYS0], qk_flat[:, 128:256], ident
                                            ).then_inc(a2_transposed, 1)

                skewed(pe, NB, 6, step)

            @block.scalar
            def _(act):
                def step(i, u):
                    b = i - 4
                    if live(b, NB):
                        act.wait_ge(a2_out_transposed, b + 1)
                        nc.scalar.copy(outT, bank[0][:, 128:256]).then_inc(a2_outT_ready, 1)
                    b = i - 2
                    if live(b, NB):
                        act.wait_ge(a2_weights_transposed, b + 1)
                        nc.scalar.copy(ctx_wT, bank[4][0:CK, 0:256].rearrange("p (h q) -> p h q", h=H0)
                                       ).then_inc(a2_ctx_wT_ready, 1)
                    b = i - 1
                    if live(b, NB):
                        act.wait_ge(a2_max_ready, b + 1)
                        if live(b - 2, NB):
                            act.wait_ge(a2_inv_sum_ready, b - 1)
                        for h in range(H0):
                            last = nc.scalar.activation(weights[:, h, :], score[h][:, 0:KEYS0], ACT.Exp,
                                                        bias=neg_max[:, h:h + 1], accum_out=weight_sum[(u + 1) % 2][:, h:h + 1])
                        last.then_inc(a2_weights_ready, 1)
                    if live(i, NB):
                        act.wait_ge(a2_transposed, i + 1)
                        nc.scalar.activation(qT, bank[0][:, 0:128], ACT.Copy, scale=columns[:, 6:7]
                                             ).then_inc(a2_qT_ready, 1)

                skewed(act, NB, 6, step, unroll=2)

            @block.vector
            def _(dve):
                def step(i, u):
                    b = i - 5
                    if live(b, NB):
                        dve.wait_ge(a2_out_projected, b + 1)
                        nc.vector.tensor_tensor(x_all[:, b, :], bank[7][:, 0:128], x_all[:, b, :], ALU.add
                                                ).then_inc(a2_x_ready, 1)
                        dve.wait_ge(a2_x_ready, b + 1)
                        nc.vector.bn_stats(bn[:, b, :], x_all[:, b, :]).then_inc(a2_x_bn_done, 1)
                    b = i - 3
                    if live(b, NB):
                        if live(b - 1, NB):
                            dve.wait_ge(a2_out_normed, b)
                        nc.vector.reciprocal(inv_sum, weight_sum[(u + 1) % 2]
                                             ).then_inc(a2_inv_sum_ready, 1)
                        dve.wait_ge(a2_inv_sum_ready, b + 1)
                        dve.wait_ge(a2_mixed, b + 1)
                        nc.vector.tensor_tensor(out_n, bank[6][:, 0:128].rearrange("p (h e) -> p h e", h=H0),
                                                inv_sum[:, :, None].to_broadcast([128, H0, DH0]), ALU.mult
                                                ).then_inc(a2_out_normed, 1)
                    b = i - 2
                    if live(b, NB):
                        dve.wait_ge(a2_weights_transposed, b + 1)
                        nc.vector.tensor_copy(lat_wT, bank[5][:, 0:256].rearrange("p (h q) -> p h q", h=H0)
                                              ).then_inc(a2_lat_wT_ready, 1)
                    b = i - 1
                    if live(b, NB):
                        dve.wait_ge(a2_scored, b + 1)
                        for h in range(H0):
                            last = nc.vector.tensor_reduce(neg_max[:, h:h + 1], score[h][:, 0:KEYS0], axis=AX.X,
                                                           op=ALU.max, negate=True)
                        last.then_inc(a2_max_ready, 1)
                    if live(i, NB):
                        dve.wait_ge(a2_transposed, i + 1)
                        nc.vector.tensor_copy(kT, bank[1][:, 0:KEYS0]).then_inc(a2_kT_ready, 1)

                skewed(dve, NB, 6, step, unroll=2)
                dve.wait_ge(a2_x_bn_done, NB)
                for b in range(NB):
                    last = nc.vector.bn_aggr(moments[:, b, :], bn[:, b, :])
                last.then_inc(x_moments_ready, 1)

        b1_h_ready = sem("b1_h_ready")
        b1_copied = sem("b1_copied")
        b1_transposed = sem("b1_transposed")
        b1_hT_ready = sem("b1_hT_ready")
        b1_logits_ready = sem("b1_logits_ready")
        b1_shifted = sem("b1_shifted")
        b1_exp_ready = sem("b1_exp_ready")
        b1_scores_ready = sem("b1_scores_ready")
        expert_w_loaded = [sem("expert_w_loaded_even"), sem("expert_w_loaded_odd")]

        rows = sb("rows_all", [128, NB, GROW])
        hT_all = sb("hT_all", [128, NT])
        scores = sb("scores", [128, NB, NE])
        h_now = view(stage, 0, 128)
        hT_now = view(stage, 128, 128)
        sm_max = view(stage, 256, NB)
        sm_sum = view(stage, 272, NB)

        with nc.Block(no_gpsimd_drain=True) as block:
            @block.sync
            def _(sp):
                for e in range(2):
                    sp.dma_start(w_slots[:, e], d["expert_w"][e]).then_inc(expert_w_loaded[e], 16)

            @block.scalar
            def _(act):
                batched_rstd(1, None, act, NB)

                def step(i, u):
                    if live(i, NB):
                        act.wait_ge(b1_transposed, i + 1)
                        if live(i - 1, NB):
                            act.wait_ge(b1_copied, 2 * i)
                        nc.scalar.copy(hT_now, bank[0][:, 0:128]).then_inc(b1_hT_ready, 1)

                skewed(act, NB, 2, step)
                act.wait_ge(b1_shifted, 1)
                nc.scalar.activation(scores[:, :, :], scores[:, :, :], ACT.Exp).then_inc(b1_exp_ready, 1)

            @block.gpsimd
            def _(pool):
                def step(i, u):
                    if live(i, NB):
                        pool.wait_ge(b1_h_ready, i + 1)
                        nc.gpsimd.tensor_copy(rows[:, i, 0:D], h_now).then_inc(b1_copied, 1)
                        pool.wait_ge(b1_hT_ready, i + 1)
                        nc.gpsimd.tensor_copy(hT_all[:, bass.ds(i * T, T)], hT_now).then_inc(b1_copied, 1)

                skewed(pool, NB, 2, step)
                pool.wait_ge(b1_scores_ready, 1)
                nc.gpsimd.tensor_copy(rows[:, :, D:GROW], scores[:, :, :]).then_inc(b1_copied, 1)

            @block.tensor
            def _(pe):
                def step(i, u):
                    b = i - 1
                    if live(b, NB):
                        pe.wait_ge(b1_hT_ready, b + 1)
                        last = nc.tensor.matmul(bank[7][:, bass.ds(b * NE, NE)], hT_now, gate_w[:, :],
                                                start=True, stop=True)
                        last.then_inc(b1_logits_ready, 1)
                    if live(i, NB):
                        pe.wait_ge(b1_h_ready, i + 1)
                        nc.tensor.transpose(bank[0][:, 0:128], h_now, ident).then_inc(b1_transposed, 1)

                skewed(pe, NB, 2, step)

            @block.vector
            def _(dve):
                batched_rstd(1, dve, None, NB)
                dve.wait_ge(shift_ready, 2)

                def step(i, u):
                    if live(i, NB):
                        if live(i - 1, NB):
                            dve.wait_ge(b1_transposed, i)
                            dve.wait_ge(b1_copied, 2 * i - 1)
                        nc.vector.tensor_scalar(h_now, x_all[:, i, :], rstd[:, bass.ds(i, 1)], shift[:, bass.ds(i, 1)],
                                                ALU.mult, ALU.add).then_inc(b1_h_ready, 1)

                skewed(dve, NB, 2, step)
                dve.wait_ge(b1_logits_ready, NB)
                logits = bank[7][:, 0:NB * NE].rearrange("p (b e) -> p b e", b=NB)
                link(dve, nc.vector.tensor_reduce(sm_max, logits, axis=AX.X, op=ALU.max))
                nc.vector.tensor_tensor(scores[:, :, :], logits, sm_max[:, :, None].to_broadcast([128, NB, NE]),
                                        ALU.subtract).then_inc(b1_shifted, 1)
                dve.wait_ge(b1_exp_ready, 1)
                link(dve, nc.vector.tensor_reduce(sm_sum, scores[:, :, :], axis=AX.X, op=ALU.add))
                link(dve, nc.vector.reciprocal(sm_max, sm_sum))
                nc.vector.tensor_tensor(scores[:, :, :], scores[:, :, :],
                                        sm_max[:, :, None].to_broadcast([128, NB, NE]), ALU.mult
                                        ).then_inc(b1_scores_ready, 1)
                dve.wait_ge(b1_copied, 2 * NB + 1)

        rows_stored = sem("rows_stored")
        sums_stored = sem("sums_stored")
        b2_scoresT = sem("b2_scoresT")
        b2_scoresT_ready = sem("b2_scoresT_ready")
        b2_found_zero = sem("b2_found_zero")
        b2_trial_ready = sem("b2_trial_ready")
        b2_counted = sem("b2_counted")
        b2_total_ready = sem("b2_total_ready")
        b2_hit_ready = sem("b2_hit_ready")
        b2_found_ready = sem("b2_found_ready")
        b2_gate_ready = sem("b2_gate_ready")
        b2_up_ready = sem("b2_up_ready")
        b2_gelu_ready = sem("b2_gelu_ready")
        b2_hidden_ready = sem("b2_hidden_ready")
        b2_shared_ready = sem("b2_shared_ready")
        b2_added = sem("b2_added")
        b3_wide_ready = sem("b3_wide_ready")
        b3_threshold_ready = sem("b3_threshold_ready")
        b3_above_ready = sem("b3_above_ready")
        b3_from_ready = sem("b3_from_ready")
        b3_scanned = sem("b3_scanned")
        b3_earlier_ready = sem("b3_earlier_ready")
        b3_above_counted = sem("b3_above_counted")
        b3_equal_ranked = sem("b3_equal_ranked")
        b3_in_need = sem("b3_in_need")
        b3_taken_ranked = sem("b3_taken_ranked")
        b3_low_ready = sem("b3_low_ready")

        scoresT = view(stage, 0, NB * T // 8)
        trial = view(stage, 256, 1).bitcast(I32)
        found = view(stage, 257, 1).bitcast(I32)
        hit = view(stage, 258, 1).bitcast(I32)
        zero_col = view(stage, 259, 1).bitcast(I32)
        count16 = sb("count16", [128, 2], BF16)
        junk16 = sb("junk16", [128, 256], BF16)
        gelu_s = view(stage, 260, 2, 256)
        hidden_s = view(stage, 772, 2, 256)
        wide = view(stage, 1284, 128)
        sel16 = sb("sel16", [128, 6, NE * NB], BF16)
        above, equal, earlier, taken = (sel16[:, n, :] for n in range(4))
        from16, in_need = sel16[:, 4, :], sel16[:, 5, :]
        need = view(stage, 1412, NE)
        scan = view(stage, 1430, NE * NB)
        place = view(stage, 1686, NE * NB)
        low = sb("low", [128, NE * NB])
        half = sb("half", [128, 2, NE * NB])
        halves = sb("halves", [128, NE * NB, 2], F16)

        def by_expert(ap):
            return ap.rearrange("p (b e) -> p e b", b=NB)

        def ranks(pe, bits, earlier_bits, out):
            nc.tensor.matmul(out, before, bits, start=True, stop=False)
            return nc.tensor.matmul(out, ones16, earlier_bits, start=False, stop=True)

        with nc.Block(no_gpsimd_drain=True) as block:
            @block.sync
            def _(sp):
                sp.dma_start(d["rows"].rearrange("(b t) c -> t b c", b=NB), rows[:, :, :]).then_inc(rows_stored, 16)
                sp.wait_ge(b2_added, 8)
                sp.dma_start(d["sums"].rearrange("(b t) c -> t b c", b=NB), x_all[:, :, :]).then_inc(sums_stored, 16)

            @block.tensor
            def _(pe):
                scores_flat = scores[:, :, :].rearrange("p b e -> p (b e)")
                for n in range(2):
                    last = nc.tensor.transpose(bank[6][:, n * 128:(n + 1) * 128], scores_flat[:, n * 128:(n + 1) * 128],
                                               ident)
                last.then_inc(b2_scoresT, 1)

                def down(c, m):
                    for k in range(2):
                        last = nc.tensor.matmul(bank[5][:, m * 128:(m + 1) * 128], hidden_s[:, k, m * 128:(m + 1) * 128],
                                                shared_down[:, k, :], start=(k == 0), stop=(k == 1))
                    return last

                def up(c, which, k):
                    bk = bank[1 + 2 * which]
                    return nc.tensor.matmul(bk[:, k * 256:(k + 1) * 256],
                                            shared_up[:, which, k * 128:(k + 1) * 128],
                                            hT_all[:, bass.ds(c * 256, 256)], start=True, stop=True)

                def total(n):
                    pe.wait_ge(b2_counted, n + 1)
                    nc.tensor.matmul(bank[6][:, 0:1], same_expert, count16[:, 0:1], start=True, stop=True
                                     ).then_inc(b2_total_ready, 1)

                def step(c, u):
                    n = c * 4
                    if live(c, 8):
                        total(n)
                        if live(c - 1, 8):
                            pe.wait_ge(b2_gelu_ready, c)
                        up(c, 0, 0)
                        up(c, 0, 1).then_inc(b2_gate_ready, 1)
                        total(n + 1)
                        if live(c - 1, 8):
                            pe.wait_ge(b2_hidden_ready, c)
                        up(c, 1, 0)
                        up(c, 1, 1).then_inc(b2_up_ready, 1)
                        total(n + 2)
                    if live(c - 1, 8):
                        pe.wait_ge(b2_hidden_ready, c)
                        if live(c - 2, 8):
                            pe.wait_ge(b2_added, c - 1)
                        down(c - 1, 0)
                        down(c - 1, 1).then_inc(b2_shared_ready, 1)
                    if live(c, 8):
                        total(n + 3)

                skewed(pe, 8, 2, step)
                pe.wait_ge(b3_wide_ready, 1)
                nc.tensor.transpose(bank[0][:, 0:128], wide, ident).then_inc(b3_threshold_ready, 1)
                pe.wait_ge(b3_above_ready, 1)
                nc.tensor.matmul(bank[1][:, 0:256], ones16, above, start=True, stop=True).then_inc(b3_above_counted, 1)
                pe.wait_ge(b3_earlier_ready, 1)
                ranks(pe, equal, earlier, bank[2][:, 0:256]).then_inc(b3_equal_ranked, 1)
                pe.wait_ge(b3_earlier_ready, 2)
                ranks(pe, taken, earlier, bank[3][:, 0:256]).then_inc(b3_taken_ranked, 1)

            @block.scalar
            def _(act):
                def step(c, u):
                    act.wait_ge(b2_gate_ready, c + 1)
                    if live(c - 1, 8):
                        act.wait_ge(b2_hidden_ready, c)
                    nc.scalar.activation(gelu_s, bank[1][:, 0:512].rearrange("p (k t) -> p k t", k=2), ACT.Gelu
                                         ).then_inc(b2_gelu_ready, 1)

                step(0, 0)
                with act.Fori(1, 8) as c:
                    step(c, 0)

            @block.vector
            def _(dve):
                dve.wait_ge(b2_scoresT, 1)
                nc.vector.tensor_copy(scoresT, bank[6][:, 0:256]).then_inc(b2_scoresT_ready, 1)
                nc.vector.memset(found, 0).then_inc(b2_found_zero, 1)
                nc.vector.tensor_copy(trial, bit_int[:, 0:1]).then_inc(b2_trial_ready, 1)
                dve.wait_ge(b2_scoresT_ready, 1)
                dve.wait_ge(b2_found_zero, 1)

                def bit(n, next_bit):
                    dve.wait_ge(b2_trial_ready, n + 1)
                    nc.vector.tensor_scalar(junk16[:, :], scoresT, trial.bitcast(F32), None, ALU.is_ge, ALU.add,
                                            accum_out=count16[:, 0:1]).then_inc(b2_counted, 1)
                    dve.wait_ge(b2_total_ready, n + 1)
                    nc.vector.tensor_scalar(hit, bank[6][:, 0:1], float(CAP), bit_value[:, bass.ds(n, 1)],
                                            ALU.is_ge, ALU.mult).then_inc(b2_hit_ready, 1)
                    dve.wait_ge(b2_hit_ready, n + 1)
                    nc.vector.tensor_tensor(found, found, hit, ALU.bitwise_or).then_inc(b2_found_ready, 1)
                    dve.wait_ge(b2_found_ready, n + 1)
                    if next_bit:
                        nc.vector.tensor_tensor(trial, found, bit_int[:, bass.ds(n + 1, 1)], ALU.bitwise_or
                                                ).then_inc(b2_trial_ready, 1)

                def step(c, u):
                    n = c * 4
                    if live(c, 8):
                        bit(n, True)
                        bit(n + 1, True)
                    if live(c - 1, 8):
                        pass
                    if live(c, 8):
                        bit(n + 2, True)
                        dve.wait_ge(b2_up_ready, c + 1)
                        dve.wait_ge(b2_gelu_ready, c + 1)
                        if live(c - 1, 8):
                            dve.wait_ge(b2_shared_ready, c)
                        nc.vector.tensor_tensor(hidden_s, gelu_s, bank[3][:, 0:512].rearrange("p (k t) -> p k t", k=2),
                                                ALU.mult).then_inc(b2_hidden_ready, 1)
                        bit(n + 3, not isinstance(c, int) or c < 7)
                    if live(c - 1, 8):
                        dve.wait_ge(b2_shared_ready, c)
                        xs = x_all[:, bass.ds((c - 1) * 2, 2), :]
                        nc.vector.tensor_tensor(xs, bank[5][:, 0:256].rearrange("p (b d) -> p b d", b=2), xs, ALU.add
                                                ).then_inc(b2_added, 1)

                step(0, 0)
                with dve.Fori(1, 7) as c:
                    step(c, 0)
                step(7, 0)
                step(8, 0)
                nc.vector.tensor_copy(wide, found.bitcast(F32).to_broadcast([128, 128])).then_inc(b3_wide_ready, 1)
                dve.wait_ge(b3_threshold_ready, 1)
                sc = scores[:, :, :].rearrange("p (n j) e -> p n (j e)", n=2)
                thr = bank[0][:, None, 0:128].to_broadcast([128, 2, 128])

                def compared(out, op, signal):
                    for n in range(2):
                        last = nc.vector.tensor_tensor(
                            out.rearrange("p (e n j) -> p n j e", n=2, j=8)[:, n],
                            scores[:, n * 8:(n + 1) * 8, :], bank[0][:, 0:128].rearrange("p (j e) -> p j e", j=8), op)
                    last.then_inc(signal, 1)

                compared(above, ALU.is_gt, b3_above_ready)
                compared(from16, ALU.is_ge, b3_from_ready)
                dve.wait_ge(b3_from_ready, 1)
                link(dve, nc.vector.tensor_tensor(equal, from16, above, ALU.subtract))

                def earlier_of(bits, n):
                    if n:
                        dve.wait_ge(b3_equal_ranked, n)
                    nc.vector.tensor_tensor_scan(scan, first_batch, bits, 0.0, ALU.mult, ALU.add
                                                 ).then_inc(b3_scanned, 1)
                    dve.wait_ge(b3_scanned, n + 1)
                    nc.vector.tensor_tensor(earlier, scan, bits, ALU.subtract).then_inc(b3_earlier_ready, 1)

                earlier_of(equal, 0)
                dve.wait_ge(b3_above_counted, 1)
                link(dve, nc.vector.tensor_reduce(need, bank[1][:, 0:256].rearrange("p (e b) -> p e b", b=NB), axis=AX.X,
                                        op=ALU.add))
                link(dve, nc.vector.tensor_scalar(need, need, -1.0, float(CAP), ALU.mult, ALU.add))
                dve.wait_ge(b3_equal_ranked, 1)
                eb = dict(b=NB)
                nc.vector.tensor_tensor(in_need.rearrange("p (e b) -> p e b", **eb),
                                        bank[2][:, 0:256].rearrange("p (e b) -> p e b", **eb),
                                        need[:, :, None].to_broadcast([128, NE, NB]), ALU.is_lt
                                        ).then_inc(b3_in_need, 1)
                dve.wait_ge(b3_in_need, 1)
                link(dve, nc.vector.tensor_tensor(in_need, in_need, equal, ALU.mult))
                link(dve, nc.vector.tensor_tensor(taken, in_need, above, ALU.add))
                earlier_of(taken, 1)
                dve.wait_ge(b3_taken_ranked, 1)
                link(dve, nc.vector.scalar_tensor_tensor(place, bank[3][:, 0:256], 1.0, taken, ALU.add, ALU.mult
                                               ))
                nc.vector.tensor_scalar(half[:, 1, :], place, 128.5, None, ALU.is_gt)
                link(dve, nc.vector.tensor_scalar(half[:, 0, :], place, 128.5, None, ALU.is_lt))
                nc.vector.scalar_tensor_tensor(low[:, :], half[:, 1, :], -128.0, place, ALU.mult, ALU.add)
                for n in range(2):
                    last = nc.vector.tensor_tensor(
                        halves[:, :, n].rearrange("p (e b) -> p e b", **eb),
                        half[:, n, :].rearrange("p (e b) -> p e b", **eb),
                        token_id[:, None, :].to_broadcast([128, NE, NB]), ALU.mult)
                last.then_inc(b3_low_ready, 1)

        e_onehot_ready = sem("e_onehot_ready")
        e_listed = sem("e_listed")
        e_list_row_ready = sem("e_list_row_ready")
        e_list_ready = sem("e_list_ready")
        e_gather_list_ready = sem("e_gather_list_ready")
        e_gathered = sem("e_gathered")
        e_weight_kept = sem("e_weight_kept")
        e_transposed = sem("e_transposed")
        e_xT_ready = sem("e_xT_ready")
        e_up_ready = sem("e_up_ready")
        e_gelu_ready = sem("e_gelu_ready")
        e_hidden_ready = sem("e_hidden_ready")
        e_down_ready = sem("e_down_ready")
        e_downT_ready = sem("e_downT_ready")
        e_output_ready = sem("e_output_ready")
        e_weighed = sem("e_weighed")
        e_scattered = sem("e_scattered")
        e_pool_turns = sem("e_pool_turns")

        onehot = sb("onehot", [128, 2, NB, 128], F16)
        list_all = sb("list_all", [128, NE, 2], I32)
        gather_list = sb("gather_list", [128, 2], I32)
        scatter_list = sb("scatter_list", [128, 2], I32)
        kept = sb("kept", [128, NE, 2])
        gathered = view(stage, 0, 2, GROW)
        xT = view(stage, 288, 256)
        gelu_e = view(stage, 544, NI, CAP)
        hidden_e = view(stage, 1568, NI, CAP)
        weighed = view(stage, 2592, 2, D)
        downT = view(stage, 2848, CAP)
        list_row = view(stage, 3104, 128)[0:2]

        with nc.Block(no_gpsimd_drain=True) as block:
            @block.sync
            def _(sp):
                with sp.Fori(0, NE // 2 - 1) as g:
                    for u in range(2):
                        sp.wait_ge(e_down_ready, g * 2 + u + 1)
                        sp.dma_start(w_slots[:, u], d["expert_w"][bass.ds(g * 2 + u + 2, 1)].rearrange(
                            "o p w i -> (o p) w i")).then_inc(expert_w_loaded[u], 16)
                sp.wait_ge(e_scattered, 32 * NE)
                sp.dma_start(x_all[:, :, :], d["sums"].rearrange("(b t) c -> t b c", b=NB)).then_inc(x_loaded, 16)

            @block.gpsimd
            def _(pool):
                pool.wait_ge(rows_stored, 16)
                pool.wait_ge(sums_stored, 16)

                def step(i, u):
                    e = i - 4
                    if live(e, NE):
                        pool.wait_ge(e_weighed, e + 1)
                        pool.sem_inc(e_pool_turns, 1)
                        for m in range(2):
                            nc.gpsimd.indirect_dma_start(
                                d["sums"], bass.IndirectOffsetOnAxis(scatter_list[:, m:m + 1], 0), weighed[:, m, :], None,
                                compute_op=ALU.add).then_inc(e_scattered, 16)
                    e = i - 1
                    if live(e, NE):
                        pool.wait_ge(e_gather_list_ready, e + 1)
                        pool.sem_inc(e_pool_turns, 1)
                        for m in range(2):
                            nc.gpsimd.indirect_dma_start(
                                gathered[:, m, :], None, d["rows"], bass.IndirectOffsetOnAxis(gather_list[:, m:m + 1], 0)
                                ).then_inc(e_gathered, 16)

                skewed(pool, NE, 4, step)

            @block.tensor
            def _(pe):
                def step(i, u):
                    e = i - 3
                    if live(e, NE):
                        pe.wait_ge(e_xT_ready, e + 1)
                        pe.wait_ge(expert_w_loaded[(u + 1) % 2], 8 * (e - (u + 1) % 2) + 16)
                        for s in range(2):
                            for which in range(2):
                                for k in range(2):
                                    c = 2 * s + k
                                    last = nc.tensor.matmul(
                                        bank[1 + s + 2 * which][:, k * 256:(k + 1) * 256],
                                        w_slots[:, (u + 1) % 2, which, c * 128:(c + 1) * 128], xT, start=True, stop=True)
                            last.then_inc(e_up_ready, 1)
                    e = i - 1
                    if live(e, NE):
                        pe.wait_ge(e_onehot_ready, e + 1)
                        for b in range(NB):
                            last = nc.tensor.matmul(bank[6][0:2, 0:128], halves[:, bass.ds(e * NB + b, 1), :]
                                                    .rearrange("p o n -> p (o n)"), onehot[:, (u + 1) % 2, b, :],
                                                    start=(b == 0), stop=(b == NB - 1))
                        last.then_inc(e_listed, 1)
                    e = i - 4
                    if live(e, NE):
                        pe.wait_ge(e_downT_ready, e + 1)
                        if live(i - 2, NE):
                            pe.wait_ge(e_gather_list_ready, i - 1)
                        if live(e - 1, NE):
                            pe.wait_ge(e_weighed, e)
                        for m in range(2):
                            last = nc.tensor.transpose(bank[7][:, m * 128:(m + 1) * 128], downT[:, m * 128:(m + 1) * 128],
                                                       ident)
                        last.then_inc(e_output_ready, 1)
                    e = i - 2
                    if live(e, NE):
                        pe.wait_ge(e_gathered, 32 * e + 32)
                        for m in range(2):
                            last = nc.tensor.transpose(bank[0][:, m * 128:(m + 1) * 128], gathered[:, m, 0:D], ident)
                        last.then_inc(e_transposed, 1)
                    e = i - 1
                    if live(e, NE):
                        pe.wait_ge(e_list_row_ready, e + 1)
                        if live(i - 4, NE):
                            pe.wait_ge(e_weighed, i - 3)
                        nc.tensor.matmul(bank[7][:, 256:258], list_row, ident[0:2, 0:2], start=True, stop=True
                                         ).then_inc(e_list_ready, 1)
                    e = i - 3
                    if live(e, NE):
                        pe.wait_ge(e_hidden_ready, 2 * e + 2)
                        for k in range(NI):
                            last = nc.tensor.matmul(bank[5][:, 0:CAP], w_slots[:, (u + 1) % 2, 2, k * 128:(k + 1) * 128],
                                                    hidden_e[:, k, :], start=(k == 0), stop=(k == NI - 1))
                        last.then_inc(e_down_ready, 1)

                skewed(pe, NE, 4, step, unroll=2)

            @block.scalar
            def _(act):
                def step(i, u):
                    e = i - 4
                    if live(e, NE):
                        act.wait_ge(e_down_ready, e + 1)
                        nc.scalar.copy(downT, bank[5][:, 0:CAP]).then_inc(e_downT_ready, 1)
                    e = i - 3
                    if live(e, NE):
                        for s in range(2):
                            act.wait_ge(e_up_ready, 2 * e + 1 + s)
                            nc.scalar.activation(gelu_e[:, 2 * s:2 * s + 2, :],
                                                 bank[1 + s][:, :].rearrange("p (k t) -> p k t", k=2), ACT.Gelu
                                                 ).then_inc(e_gelu_ready, 1)
                    e = i - 1
                    if live(e, NE):
                        act.wait_ge(e_listed, e + 1)
                        nc.scalar.copy(list_row, bank[6][0:2, 0:128]).then_inc(e_list_row_ready, 1)
                    e = i - 2
                    if live(e, NE):
                        act.wait_ge(e_transposed, e + 1)
                        nc.scalar.copy(xT, bank[0][:, 0:256]).then_inc(e_xT_ready, 1)

                skewed(act, NE, 4, step)

            @block.vector
            def _(dve):
                def hidden(e, s):
                    dve.wait_ge(e_gelu_ready, 2 * e + 1 + s)
                    nc.vector.tensor_tensor(hidden_e[:, 2 * s:2 * s + 2, :], gelu_e[:, 2 * s:2 * s + 2, :],
                                            bank[3 + s][:, :].rearrange("p (k t) -> p k t", k=2), ALU.mult
                                            ).then_inc(e_hidden_ready, 1)

                def places(i, u, part):
                    for b in range(part * NB // 2, (part + 1) * NB // 2):
                        last = nc.vector.tensor_scalar(onehot[:, u, b, :], iota1, low[:, bass.ds(i * NB + b, 1)], None,
                                                       ALU.is_equal)
                    if part:
                        last.then_inc(e_onehot_ready, 1)

                def step(i, u):
                    if live(i, NE):
                        places(i, u, 0)
                    if live(i - 3, NE):
                        hidden(i - 3, 0)
                    if live(i, NE):
                        places(i, u, 1)
                    if live(i - 3, NE):
                        hidden(i - 3, 1)
                    e = i - 2
                    if live(e, NE):
                        dve.wait_ge(e_gathered, 32 * e + 32)
                        nc.vector.tensor_copy(kept[:, e, :], gathered[:, :, bass.ds(e + D, 1)].rearrange("p m o -> p (m o)")
                                              ).then_inc(e_weight_kept, 1)
                    e = i - 4
                    if live(e, NE):
                        dve.wait_ge(e_output_ready, e + 1)
                        if live(e - 1, NE):
                            dve.wait_ge(e_scattered, 32 * e)
                        nc.vector.tensor_copy(scatter_list[:, :], list_all[:, e, :])
                        nc.vector.tensor_tensor(weighed, bank[7][:, 0:256].rearrange("p (m d) -> p m d", m=2),
                                                kept[:, e, :, None].to_broadcast([128, 2, D]), ALU.mult
                                                ).then_inc(e_weighed, 1)
                    e = i - 1
                    if live(e, NE):
                        dve.wait_ge(e_list_ready, e + 1)
                        nc.vector.tensor_copy(list_all[:, e, :], bank[7][:, 256:258])
                        nc.vector.tensor_copy(gather_list[:, :], bank[7][:, 256:258]).then_inc(e_gather_list_ready, 1)

                skewed(dve, NE, 4, step, unroll=2)
                blocks = wq4_in[:, :, :].rearrange("p m (n k) -> p (m n) k", k=WBLOCK)
                q4s3 = q4s[:, :, :].rearrange("p m (n k) -> p (m n) k", k=WBLOCK)
                link(dve, nc.vector.tensor_reduce(q4m, blocks, axis=AX.X, op=ALU.max, apply_absolute_value=True))
                link(dve, nc.vector.tensor_scalar(q4m, q4m, 1.0 / WMAX, TINY, ALU.mult, ALU.max))
                link(dve, nc.vector.reciprocal(q4i, q4m))
                link(dve, nc.vector.tensor_tensor(q4s3, blocks, q4i[:, :, None].to_broadcast([128, 36, WBLOCK]), ALU.mult))
                link(dve, nc.vector.tensor_scalar(q4s, q4s, ROUND, ROUND, ALU.add, ALU.subtract))
                nc.vector.tensor_tensor(q4s3, q4s3, q4m[:, :, None].to_broadcast([128, 36, WBLOCK]), ALU.mult
                                        ).then_inc(q4_ready, 1)

        c_bn_done = sem("c_bn_done")
        c_moments = sem("c_moments")
        c_gain_ready = sem("c_gain_ready")
        c_h_ready = sem("c_h_ready")
        c_transposed = sem("c_transposed")
        c_hT_ready = sem("c_hT_ready")
        c_queried = sem("c_queried")
        c_qT_ready = sem("c_qT_ready")
        c_q4_copied = sem("c_q4_copied")
        c_bank_clear = sem("c_bank_clear")
        c_q_now_ready = sem("c_q_now_ready")
        c_keys_ready = sem("c_keys_ready")
        c_scored = sem("c_scored")
        c_max_ready = sem("c_max_ready")
        c_shifted = sem("c_shifted")
        c_weights_ready = sem("c_weights_ready")
        c_weights_transposed = sem("c_weights_transposed")
        c_wT_ready = sem("c_wT_ready")
        c_values_ready = sem("c_values_ready")
        c_mixed = sem("c_mixed")
        c_mixed_out = sem("c_mixed_out")
        c_out_transposed = sem("c_out_transposed")
        c_inv_ready = sem("c_inv_ready")
        c_out_ready = sem("c_out_ready")
        c_x_ready = sem("c_x_ready")
        c_x_bn_done = sem("c_x_bn_done")

        masked_rstd = view(stage, 0, NB)
        masked_shift = view(stage, 16, NB)
        q_now = view(stage, 32, 128)
        out1 = view(stage, 160, H1, DH1)
        max1 = view(stage, 288, H1)
        inv1 = view(stage, 304, H1)
        keys_now = view(stage, 320, QUAD, CK)
        mixed_s = view(stage, 640, 512)
        values_now = view(stage, 1152 + 2 * H1 * CK, H1, DH1 + 1)[0:CK]
        weights1 = [view(stage, 1152, H1 * CK), view(stage, 1152 + H1 * CK, H1 * CK)]
        wT1 = sb("wT1", [CK, H1, 128])
        h1_all = rows[:, :, 0:D]
        G4 = 4 * T

        with nc.Block(no_gpsimd_drain=True) as block:
            @block.gpsimd
            def _(pool):
                def step(i, u):
                    if live(i, NB):
                        if live(i - 1, NB):
                            pool.wait_ge(c_scored, 4 * i)
                        nc.gpsimd.tensor_tensor(keys_now, keys1[:, i, None, :].to_broadcast([128, QUAD, CK]),
                                                head_of_row[:, :, None].to_broadcast([128, QUAD, CK]), ALU.mult
                                                ).then_inc(c_keys_ready, 1)
                    b = i - 2
                    if live(b, NB):
                        if live(b - 1, NB):
                            pool.wait_ge(c_mixed, b)
                        nc.gpsimd.tensor_copy(values_now, values1[:, b, :, :]).then_inc(c_values_ready, 1)

                skewed(pool, NB, 2, step)

            @block.tensor
            def _(pe):
                pe.wait_ge(q4_ready, 1)
                for m in range(3):
                    for c in range(NQ):
                        last = nc.tensor.transpose(bank[m][:, c * 128:(c + 1) * 128], q4s[:, m, c * 128:(c + 1) * 128],
                                                   ident)
                    last.then_inc(q4_transposed, 1)
                for g in range(4):
                    pe.wait_ge(c_h_ready, g + 1)
                    if g:
                        pe.wait_ge(c_q4_copied, g)
                    for j in range(4):
                        last = nc.tensor.transpose(bank[(g + 3) % 4][:, j * T:(j + 1) * T], h1_all[:, g * 4 + j, :], ident)
                    last.then_inc(c_transposed, 1)
                    if g:
                        pe.wait_ge(c_hT_ready, g)
                        nc.tensor.matmul(bank[3 + g][:, :], wq1[:, :], hT_all[:, (g - 1) * G4:g * G4], start=True, stop=True
                                         ).then_inc(c_queried, 1)
                pe.wait_ge(c_hT_ready, 4)
                nc.tensor.matmul(bank[7][:, :], wq1[:, :], hT_all[:, 3 * G4:4 * G4], start=True, stop=True
                                 ).then_inc(c_queried, 1)
                pe.wait_ge(c_bank_clear, 1)

                def step(i, u):
                    b = i - 1
                    if live(b, NB):
                        pe.wait_ge(c_q_now_ready, b + 1)
                        pe.wait_ge(c_keys_ready, b + 1)
                        for g in range(QUAD):
                            if live(b - 1, NB):
                                pe.wait_ge(c_shifted, 4 * b + g - 3)
                            r = slice(32 * g, 32 * g + 32)
                            nc.tensor.matmul(bank[g][:, 0:QUAD * CK], q_now[r, :],
                                                    keys_now[r].rearrange("p j k -> p (j k)"), start=True, stop=True,
                                                    tile_position=(32 * g, 0)).then_inc(c_scored, 1)
                    b = i - 4
                    if live(b, NB):
                        pe.wait_ge(c_mixed_out, b + 1)
                        if live(b - 1, NB):
                            pe.wait_ge(c_out_ready, b)
                        for g in range(QUAD):
                            last = nc.tensor.transpose(bank[6][:, g * 128:(g + 1) * 128], mixed_s[:, g * 128:(g + 1) * 128],
                                                       ident)
                        last.then_inc(c_out_transposed, 1)
                    b = i - 3
                    if live(b, NB):
                        pe.wait_ge(c_wT_ready, 4 * b + 4)
                        pe.wait_ge(c_values_ready, b + 1)
                        if live(b - 1, NB):
                            pe.wait_ge(c_mixed_out, b)
                        for g in range(QUAD):
                            for j in range(QUAD):
                                h = g * QUAD + j
                                last = nc.tensor.matmul(bank[7][32 * j:32 * j + DH1 + 1, g * 128:(g + 1) * 128],
                                                        values_now[:, h, :],
                                                        wT1[:, h, :], start=True, stop=True, tile_position=(0, 32 * j))
                        last.then_inc(c_mixed, 1)
                    b = i - 2
                    if live(b, NB):
                        pe.wait_ge(c_weights_ready, b + 1)
                        for g in range(QUAD):
                            if g >= 2:
                                pe.wait_ge(c_wT_ready, 4 * b + g - 1)
                            for j in range(QUAD):
                                h = g * QUAD + j
                                last = nc.tensor.transpose(bank[4 + g % 2][0:CK, j * 128:(j + 1) * 128],
                                                           weights1[u][:, h * CK:(h + 1) * CK], ident)
                            last.then_inc(c_weights_transposed, 1)

                skewed(pe, NB, 4, step, unroll=2)

            @block.scalar
            def _(act):
                batched_rstd(2, None, act, NB)
                for m in range(3):
                    act.wait_ge(q4_transposed, m + 1)
                    nc.scalar.copy(wq4[:, m, :], bank[m][:, 0:IQ]).then_inc(c_q4_copied, 1)
                for g in range(4):
                    act.wait_ge(c_transposed, g + 1)
                    nc.scalar.copy(hT_all[:, g * G4:(g + 1) * G4], bank[(g + 3) % 4][:, :]).then_inc(c_hT_ready, 1)

                def step(i, u):
                    if live(i, NB):
                        if isinstance(i, int) and i == 0:
                            act.wait_ge(c_qT_ready, 4)
                        else:
                            act.wait_ge(c_scored, 4 * i)
                        nc.scalar.copy(q_now, hT_all[:, bass.ds(i * T, T)]).then_inc(c_q_now_ready, 1)
                    b = i - 3
                    if live(b, NB):
                        act.wait_ge(c_mixed, b + 1)
                        if live(b - 1, NB):
                            act.wait_ge(c_out_transposed, b)
                        nc.scalar.copy(mixed_s, bank[7][:, :]).then_inc(c_mixed_out, 1)
                    b = i - 2
                    if live(b, NB):
                        for g in range(QUAD):
                            act.wait_ge(c_weights_transposed, 4 * b + g + 1)
                            nc.scalar.copy(wT1[:, g * QUAD:(g + 1) * QUAD, :],
                                           bank[4 + g % 2][0:CK, :].rearrange("p (j q) -> p j q", j=QUAD)
                                           ).then_inc(c_wT_ready, 1)
                    b = i - 1
                    if live(b, NB):
                        act.wait_ge(c_shifted, 4 * b + 4)
                        nc.scalar.activation(weights1[(u + 1) % 2], weights1[(u + 1) % 2], ACT.Exp
                                             ).then_inc(c_weights_ready, 1)

                skewed(act, NB, 4, step, unroll=2)

            @block.vector
            def _(dve):
                dve.wait_ge(x_loaded, 32)
                for b in range(NB):
                    nc.vector.bn_stats(bn[:, b, :], x_all[:, b, :]).then_inc(c_bn_done, 1)
                dve.wait_ge(c_bn_done, NB)
                for b in range(NB):
                    last = nc.vector.bn_aggr(moments[:, b, :], bn[:, b, :])
                last.then_inc(c_moments, 1)
                dve.wait_ge(c_moments, 1)
                batched_rstd(2, dve, None, NB)
                dve.wait_ge(shift_ready, 3)
                nc.vector.tensor_tensor(masked_rstd, rstd[:, 0:NB], mask_q[:, :], ALU.mult)
                nc.vector.tensor_tensor(masked_shift, shift[:, 0:NB], mask_q[:, :], ALU.mult).then_inc(c_gain_ready, 1)
                dve.wait_ge(c_gain_ready, 1)
                for b in range(NB):
                    h = nc.vector.tensor_scalar(h1_all[:, b, :], x_all[:, b, :], masked_rstd[:, b:b + 1],
                                                masked_shift[:, b:b + 1], ALU.mult, ALU.add)
                    if b % 4 == 3:
                        h.then_inc(c_h_ready, 1)
                for g in range(4):
                    dve.wait_ge(c_queried, g + 1)
                    nc.vector.tensor_scalar(hT_all[:, g * G4:(g + 1) * G4], bank[4 + g][:, :], DH1 ** -0.5, None, ALU.mult
                                            ).then_inc(c_qT_ready, 1)
                dve.wait_ge(c_qT_ready, 4)
                nc.vector.memset(bank[7][:, :], 0.0).then_inc(c_bank_clear, 1)

                def step(i, u):
                    b = i - 1
                    if live(b, NB):
                        if live(b - 2, NB):
                            dve.wait_ge(c_weights_transposed, 4 * b - 4)
                        for g in range(QUAD + 1):
                            if g < QUAD:
                                dve.wait_ge(c_scored, 4 * b + g + 1)
                                nc.vector.tensor_reduce(
                                    max1[:, g * QUAD:(g + 1) * QUAD], bank[g][:, 0:QUAD * CK].rearrange(
                                        "p (j k) -> p j k", j=QUAD), axis=AX.X, op=ALU.max).then_inc(c_max_ready, 1)
                            if g > 0:
                                done = g - 1
                                dve.wait_ge(c_max_ready, 4 * b + done + 1)
                                nc.vector.tensor_tensor(
                                    weights1[(u + 1) % 2][:, done * QUAD * CK:g * QUAD * CK].rearrange(
                                        "p (j k) -> p j k", j=QUAD),
                                    bank[done][:, 0:QUAD * CK].rearrange("p (j k) -> p j k", j=QUAD),
                                    max1[:, done * QUAD:g * QUAD, None].to_broadcast([128, QUAD, CK]), ALU.subtract
                                    ).then_inc(c_shifted, 1)
                    b = i - 4
                    if live(b, NB):
                        dve.wait_ge(c_out_transposed, b + 1)
                        o = bank[6][:, :].rearrange("p (h e) -> p h e", h=H1)
                        nc.vector.reciprocal(inv1, o[:, :, DH1]).then_inc(c_inv_ready, 1)
                        dve.wait_ge(c_inv_ready, b + 1)
                        nc.vector.tensor_tensor(out1, o[:, :, 0:DH1], inv1[:, :, None].to_broadcast([128, H1, DH1]),
                                                ALU.mult).then_inc(c_out_ready, 1)
                        dve.wait_ge(c_out_ready, b + 1)
                        nc.vector.tensor_tensor(x_all[:, b, :], x_all[:, b, :], out1.rearrange("p h e -> p (h e)"),
                                                ALU.add).then_inc(c_x_ready, 1)
                        dve.wait_ge(c_x_ready, b + 1)
                        nc.vector.bn_stats(bn[:, b, :], x_all[:, b, :]).then_inc(c_x_bn_done, 1)

                skewed(dve, NB, 4, step, unroll=2)
                dve.wait_ge(c_x_bn_done, NB)
                for b in range(NB):
                    last = nc.vector.bn_aggr(moments[:, b, :], bn[:, b, :])
                last.then_inc(x_moments_ready, 1)

        d_h_ready = sem("d_h_ready")
        d_h_part = sem("d_h_part")
        d_transposed = sem("d_transposed")
        d_max_ready = sem("d_max_ready")
        d_all_max = sem("d_all_max")
        d_factor_ready = sem("d_factor_ready")
        d_h_raised = sem("d_h_raised")
        d_h_ints = sem("d_h_ints")
        d_projected = sem("d_projected")
        d_copied = sem("d_copied")
        d_gate_part = sem("d_gate_part")
        d_up_part = sem("d_up_part")
        d_gate_ints = sem("d_gate_ints")
        d_sigmoid_ready = sem("d_sigmoid_ready")
        d_product_part = sem("d_product_part")
        d_up_raised = sem("d_up_raised")
        d_t_raised = sem("d_t_raised")
        d_t_ints = sem("d_t_ints")
        d_o_part = sem("d_o_part")
        d_o_raised = sem("d_o_raised")
        d_o_ints = sem("d_o_ints")
        d_down = sem("d_down")
        d_yT_ready = sem("d_yT_ready")
        d_y_transposed = sem("d_y_transposed")
        d_y_ready = sem("d_y_ready")
        y_stored = sem("y_stored")

        own_max = view(stage, 0, 8)
        all_max = view(stage, 8, 8)
        scale = view(stage, 16, 8)
        inv_scale = view(stage, 24, 8)
        factor = view(stage, 32, 8)
        unit = view(stage, 40, 8)
        round_up, round_back = view(stage, 48, 1), view(stage, 49, 1)
        part_max = view(stage, 64, 2, 12)
        gate_all = sb("gate_all", [128, NQ, NT])
        gate_flat = gate_all[:, :, :].rearrange("p c t -> p (c t)")
        up_all = qkv[:, :, :].rearrange("p b c -> p (b c)")
        up3 = up_all.rearrange("p (c t) -> p c t", c=NQ)
        sig3 = sig_all[:, :].rearrange("p (c t) -> p c t", c=NQ)
        hq = hT_all
        h_rows = rows[:, :, 0:D]
        QT = NT // 4
        PIECES = 4 * NQ
        PX, PG, PU, PT, PO = range(5)

        def quarter(q):
            return slice(q * QT, (q + 1) * QT)

        def chunk(c):
            return slice(c * NT, (c + 1) * NT)

        with nc.Block(no_gpsimd_drain=True) as block:
            @block.gpsimd
            def _(pool):
                for n in range(5):
                    pool.wait_ge(d_max_ready, n + 1)
                    nc.gpsimd.partition_all_reduce(all_max[:, n:n + 1], own_max[:, n:n + 1], 128, bass.bass_isa.ReduceOp.max
                                                   ).then_inc(d_all_max, 1)

            @block.tensor
            def _(pe):
                for q in range(4):
                    pe.wait_ge(d_h_ready, q + 1)
                    for j in range(4):
                        last = nc.tensor.transpose(bank[q][:, j * T:(j + 1) * T], h_rows[:, q * 4 + j, :], ident)
                    last.then_inc(d_transposed, 1)
                for k in range(2 * PIECES):
                    which, q, c = k // PIECES, k % PIECES // NQ, k % NQ
                    if which == 0 and c == 0:
                        pe.wait_ge(d_h_ints, q + 1)
                    if k >= 4:
                        pe.wait_ge(d_copied, k - 3)
                    nc.tensor.matmul(bank[4 + k % 4][:, :], wq4[:, which, c * 128:(c + 1) * 128], hq[:, quarter(q)],
                                     start=True, stop=True).then_inc(d_projected, 1)
                for q in range(5):
                    if q < 4:
                        pe.wait_ge(d_o_ints, q + 1)
                        if q >= 2:
                            pe.wait_ge(d_yT_ready, q - 1)
                        for c in range(NQ):
                            last = nc.tensor.matmul(bank[q % 2][:, :], wq4[:, 2, c * 128:(c + 1) * 128],
                                                    sig3[:, c, quarter(q)], start=(c == 0), stop=(c == NQ - 1))
                        last.then_inc(d_down, 1)
                    if q >= 1:
                        pe.wait_ge(d_yT_ready, q)
                        if q >= 3:
                            pe.wait_ge(d_y_ready, q - 2)
                        for j in range(4):
                            last = nc.tensor.transpose(bank[2 + (q - 1) % 2][:, j * T:(j + 1) * T],
                                                       hq[:, (q - 1) * QT + j * T:(q - 1) * QT + (j + 1) * T], ident)
                        last.then_inc(d_y_transposed, 1)

            @block.scalar
            def _(act):
                batched_rstd(3, None, act, NB)
                act.wait_ge(d_factor_ready, PX + 1)
                for q in range(4):
                    act.wait_ge(d_transposed, q + 1)
                    nc.scalar.activation(hq[:, quarter(q)], bank[q][:, :], ACT.Identity, bias=round_up,
                                         scale=factor[:, PX:PX + 1]).then_inc(d_h_raised, 1)

                def copied(k):
                    which, q, c = k // PIECES, k % PIECES // NQ, k % NQ
                    act.wait_ge(d_projected, k + 1)
                    nc.scalar.copy((gate_all, up3)[which][:, c, quarter(q)], bank[4 + k % 4][:, :]).then_inc(d_copied, 1)

                for k in range(2 * PIECES):
                    copied(k)
                    if k - PIECES in (5, 8, 11):
                        c = (k - PIECES - 5) // 3
                        act.wait_ge(d_gate_ints, c + 1)
                        nc.scalar.activation(sig_all[:, chunk(c)], gate_flat[:, chunk(c)], ACT.Sigmoid,
                                             scale=scale[:, PG:PG + 1]).then_inc(d_sigmoid_ready, 1)
                act.wait_ge(d_factor_ready, PU + 1)
                for c in range(NQ):
                    nc.scalar.activation(up_all[:, chunk(c)], up_all[:, chunk(c)], ACT.Identity, bias=round_up,
                                         scale=factor[:, PU:PU + 1]).then_inc(d_up_raised, 1)
                for c in range(NQ):
                    act.wait_ge(d_t_raised, c + 1)
                    nc.scalar.activation(sig_all[:, chunk(c)], sig_all[:, chunk(c)], ACT.Identity, bias=round_back
                                         ).then_inc(d_t_ints, 1)
                for q in range(5):
                    if q < 4:
                        act.wait_ge(d_o_raised, q + 1)
                        nc.scalar.activation(sig3[:, :, quarter(q)], sig3[:, :, quarter(q)], ACT.Identity, bias=round_back
                                             ).then_inc(d_o_ints, 1)
                    if q >= 1:
                        act.wait_ge(d_down, q)
                        nc.scalar.activation(hq[:, quarter(q - 1)], bank[(q - 1) % 2][:, :], ACT.Copy,
                                             scale=scale[:, PO:PO + 1]).then_inc(d_yT_ready, 1)

            @block.vector
            def _(dve):
                def new_scale(n, parts, unit):
                    nc.vector.tensor_reduce(own_max[:, n:n + 1], parts, axis=AX.X, op=ALU.max).then_inc(d_max_ready, 1)
                    dve.wait_ge(d_all_max, n + 1)
                    col = slice(n, n + 1)
                    if unit is None:
                        link(dve, nc.vector.tensor_scalar(scale[:, col], all_max[:, col], 1.0 / QMAX, TINY, ALU.mult, ALU.max))
                        link(dve, nc.vector.reciprocal(factor[:, col], scale[:, col]))
                    else:
                        link(dve, nc.vector.tensor_scalar(scale[:, col], all_max[:, col], unit, 1.0 / QMAX, ALU.mult, ALU.mult))
                        link(dve, nc.vector.tensor_scalar(scale[:, col], scale[:, col], TINY, None, ALU.max))
                        link(dve, nc.vector.reciprocal(inv_scale[:, col], scale[:, col]))
                        link(dve, nc.vector.tensor_tensor(factor[:, col], inv_scale[:, col], unit, ALU.mult))
                    dve.sem_inc(d_factor_ready, 1)

                def part(which, n, src, signal):
                    nc.vector.tensor_reduce(part_max[:, which, n:n + 1], src, axis=AX.X, op=ALU.max,
                                            apply_absolute_value=True).then_inc(signal, 1)

                nc.vector.memset(round_up, ROUND)
                nc.vector.memset(round_back, -ROUND)
                batched_rstd(3, dve, None, NB)
                dve.wait_ge(shift_ready, 4)
                for q in range(4):
                    for b in range(4 * q, 4 * q + 4):
                        last = nc.vector.tensor_scalar(h_rows[:, b, :], x_all[:, b, :], rstd[:, b:b + 1],
                                                       shift[:, b:b + 1], ALU.mult, ALU.add)
                    last.then_inc(d_h_ready, 1)
                for q in range(4):
                    dve.wait_ge(d_h_ready, q + 1)
                    nc.vector.tensor_reduce(part_max[:, 0, q:q + 1], h_rows[:, 4 * q:4 * q + 4, :], axis=AX.XY, op=ALU.max,
                                            apply_absolute_value=True).then_inc(d_h_part, 1)
                dve.wait_ge(d_h_part, 4)
                new_scale(PX, part_max[:, 0, 0:4], None)
                for q in range(4):
                    dve.wait_ge(d_h_raised, q + 1)
                    nc.vector.tensor_scalar(hq[:, quarter(q)], hq[:, quarter(q)], ROUND, None, ALU.subtract
                                            ).then_inc(d_h_ints, 1)
                for k in range(PIECES):
                    dve.wait_ge(d_copied, k + 1)
                    part(0, k, gate_all[:, k % NQ, quarter(k // NQ)], d_gate_part)
                dve.wait_ge(d_gate_part, PIECES)
                new_scale(PG, part_max[:, 0, :], scale[:, PX:PX + 1])
                for c in range(NQ):
                    g = gate_flat[:, chunk(c)]
                    link(dve, nc.vector.tensor_scalar(g, g, factor[:, PG:PG + 1], ROUND, ALU.mult, ALU.add))
                    nc.vector.tensor_scalar(g, g, ROUND, None, ALU.subtract).then_inc(d_gate_ints, 1)
                for k in range(PIECES):
                    dve.wait_ge(d_copied, PIECES + k + 1)
                    part(1, k, up3[:, k % NQ, quarter(k // NQ)], d_up_part)
                dve.wait_ge(d_up_part, PIECES)
                new_scale(PU, part_max[:, 1, :], scale[:, PX:PX + 1])
                for c in range(NQ):
                    s, g = sig_all[:, chunk(c)], gate_flat[:, chunk(c)]
                    dve.wait_ge(d_sigmoid_ready, c + 1)
                    link(dve, nc.vector.tensor_scalar(s, s, 65535.0 / 65536.0, 192.0, ALU.min, ALU.add))
                    link(dve, nc.vector.scalar_tensor_tensor(s, s, 192.0, g, ALU.subtract, ALU.mult))
                    part(0, c, s, d_product_part)
                dve.wait_ge(d_product_part, NQ)
                new_scale(PT, part_max[:, 0, 0:NQ], scale[:, PG:PG + 1])
                for c in range(NQ):
                    s = sig_all[:, chunk(c)]
                    nc.vector.tensor_scalar(s, s, factor[:, PT:PT + 1], ROUND, ALU.mult, ALU.add).then_inc(d_t_raised, 1)
                for c in range(NQ):
                    s, up = sig_all[:, chunk(c)], up_all[:, chunk(c)]
                    dve.wait_ge(d_up_raised, c + 1)
                    dve.wait_ge(d_t_ints, c + 1)
                    link(dve, nc.vector.scalar_tensor_tensor(s, up, ROUND, s, ALU.subtract, ALU.mult))
                    part(1, c, s, d_o_part)
                dve.wait_ge(d_o_part, NQ)
                link(dve, nc.vector.tensor_tensor(unit[:, 0:1], scale[:, PT:PT + 1], scale[:, PU:PU + 1], ALU.mult))
                new_scale(PO, part_max[:, 1, 0:NQ], unit[:, 0:1])
                for q in range(4):
                    o = sig3[:, :, quarter(q)]
                    nc.vector.tensor_scalar(o, o, factor[:, PO:PO + 1], ROUND, ALU.mult, ALU.add).then_inc(d_o_raised, 1)
                for q in range(4):
                    dve.wait_ge(d_y_transposed, q + 1)
                    x4 = x_all[:, 4 * q:4 * q + 4, :]
                    nc.vector.tensor_tensor(x4, x4, bank[2 + q % 2][:, :].rearrange("p (b d) -> p b d", b=4), ALU.add
                                            ).then_inc(d_y_ready, 1)

            @block.sync
            def _(sp):
                for g in range(4):
                    sp.wait_ge(d_y_ready, g + 1)
                    sp.dma_start(d["out"][4 * g:4 * g + 4].rearrange("b t d -> t b d"), x_all[:, 4 * g:4 * g + 4, :]
                                 ).then_inc(y_stored, 16)
                sp.wait_ge(y_stored, 64)


def kernel(**inputs):
    import ml_dtypes
    import numpy as np
    from concourse import bacc, mybir
    from concourse.bass_utils import run_bass_kernel_spmd

    a = {k: np.asarray(v) for k, v in inputs.items()}
    k = np.arange(128)
    eye = np.eye(128, dtype=np.float32)
    const = np.concatenate([
        eye,
        ((k[:, None] % 32) // DH1 == np.arange(QUAD)[None, :]).astype(np.float32),
        np.tile(np.float32([2.0 ** max(0, BITS - 3 - n) * (n < BITS - 2) for n in range(BITS)]), (128, 1)),
        (np.arange(NB)[None, :] * T + k[:, None]).astype(np.float32),
        np.tile((np.arange(NE * NB) % NB != 0).astype(np.float32), (128, 1)),
    ], axis=1)
    const16 = np.concatenate([
        (k[:, None] < k[None, :]).astype(np.float32),
        np.ones((128, 128), np.float32),
        (k[:, None] % NE == k[None, :] % NE).astype(np.float32),
        np.tile((k + 1).astype(np.float32), (128, 1)),
    ], axis=1).astype(ml_dtypes.bfloat16)
    bit_int = np.tile(np.array([2 ** max(0, BITS - 3 - n) * (n < BITS - 2) for n in range(BITS)], np.int32), (128, 1))
    columns = np.zeros((128, 8), np.float32)
    columns[:, 0], columns[:, 1] = a["L0_xattn_ln_l_g"], a["L0_xattn_ln_l_b"]
    columns[:CD, 2], columns[:CD, 3] = a["L0_xattn_ln_x_g"], a["L0_xattn_ln_x_b"]
    columns[:, 4], columns[:, 5] = np.tile(a["L0_xattn_qn_g"], H0), np.tile(a["L0_xattn_kn_g"], H0)

    def chunks(w):
        return np.ascontiguousarray(w.reshape(-1, 128, w.shape[1]).transpose(1, 0, 2))

    arrays = {
        "x": a["x"], "context": a["ctx_768"], "context_t": a["ctx_768"].transpose(2, 0, 1),
        "mask_k": a["mask_BxS2_bk0"].reshape(-1), "mask_q": a["mask_BxS_bk0"].T,
        "const": const, "const16": const16, "bit_int": bit_int, "columns": columns,
        "w_token": np.concatenate([a["L0_xattn_Wq"], a["L0_xattn_Wlkv"]]).T,
        "w_context": a["L0_xattn_Wkv"].T, "w_out": a["L0_xattn_Wo"].T, "bias_out": a["L0_xattn_bo"],
        "wq1": a["L1_xattn_Wq"].T, "wkv1": a["L1_xattn_Wkv"].T, "gate_w": a["L0_ffn_gate_w"].T,
        "shared_up": np.stack([a["L0_ffn_Sg"].T, a["L0_ffn_Su"].T], axis=1),
        "shared_down": chunks(a["L0_ffn_Sd"].T),
        "expert_w": np.stack([a["L0_ffn_Wg"].transpose(0, 2, 1), a["L0_ffn_Wu"].transpose(0, 2, 1),
                              a["L0_ffn_Wd"].transpose(0, 2, 1).reshape(NE, NI, 128, 128).transpose(0, 2, 1, 3)
                              .reshape(NE, 128, IE)], axis=2),
        "w_gate": a["L1_ffn_w_gate"], "w_up": a["L1_ffn_w_up"], "w_down": a["L1_ffn_w_down"],
    }
    nc = bacc.Bacc("TRN2", target_bir_lowering=False, num_devices=1)
    dram = {}
    for name, v in arrays.items():
        arrays[name] = v = np.ascontiguousarray(v)
        dram[name] = nc.dram_tensor(f"in_{name}", v.shape, mybir.dt.from_np(v.dtype), kind="ExternalInput").ap()
    dram["rows"] = nc.dram_tensor("rows", (NT, GROW), mybir.dt.float32).ap()
    dram["sums"] = nc.dram_tensor("sums", (NT, D), mybir.dt.float32).ap()
    dram["out"] = nc.dram_tensor("out", (NB, T, D), mybir.dt.float32, kind="ExternalOutput").ap()
    build(nc, dram)
    r = run_bass_kernel_spmd(nc, [{f"in_{name}": v for name, v in arrays.items()}], core_ids=[0])
    return r.results[0]["out"]
```

```python
from contextlib import ExitStack

import concourse.bass as bass
import concourse.mybir as mybir

F32, BF16, F16 = mybir.dt.float32, mybir.dt.bfloat16, mybir.dt.float16
I32, I16, U8 = mybir.dt.int32, mybir.dt.int16, mybir.dt.uint8
ALU = mybir.AluOpType
ACT = mybir.ActivationFunctionType
AX = mybir.AxisListType

NB, T, D = 16, 128, 128
NT = NB * T
CK, CD = 77, 96
H0, DH0 = 2, 64
KEYS0 = CK + T
H1, DH1 = 16, 8
QUAD = 4
NE, CAP, IE = 16, 256, 512
NI = IE // 128
IS = 256
IQ = 384
NQ = IQ // 128
WBLOCK = 32
GROW = D + NE
LN_EPS, RMS_EPS = 1e-5, 1e-8
MASKED = -(2.0 ** 100)
ROUND = 1.5 * 2.0 ** 23
QMAX, WMAX, TINY = 32767.0, 7.0, 1e-12
ROUNDS = 15


def live(b, n):
    return 0 <= b < n if isinstance(b, int) else True


def skewed(eng, n, lag, body, unroll=1):
    for i in range(lag):
        body(i, i % unroll)
    with eng.Fori(lag // unroll, n // unroll) as g:
        for u in range(unroll):
            body(g * unroll + u, u)
    for i in range(n, n + lag):
        body(i, i % unroll)


def build(nc, d):
    with ExitStack() as ctx:
        def sb(name, shape, dt=F32):
            return ctx.enter_context(nc.sbuf_tensor(name, shape, dt))

        def sem(name):
            return ctx.enter_context(nc.semaphore(name))

        bank = [ctx.enter_context(nc.psum_tensor(f"bank{n}", [128, 512], F32)) for n in range(8)]

        x_all = sb("x_all", [128, NB, D])
        moments = sb("moments", [128, 2 * NB, 2])
        variance = sb("variance", [128, 2 * NB])
        deviation = sb("deviation", [128, 2 * NB])
        rstd = sb("rstd", [128, 2 * NB])
        shift = sb("shift", [128, 2 * NB])
        bn = sb("bn", [128, 2 * NB, 6])
        const = sb("const", [128, d["const"].shape[1]])
        const16 = sb("const16", [128, d["const16"].shape[1]], BF16)
        ident = const[:, 0:128]
        head_of_row = const[:, 128:132]
        unit_of_round = const[:, 132:132 + ROUNDS]
        token_id = const[:, 147:163]
        first_batch = const[:, 163:419]
        before = const16[:, 0:128]
        ones16 = const16[:, 128:256]
        same_expert = const16[:, 256:384]
        iota1 = const16[:, 384:512]
        patterns = sb("patterns", [128, 3 * ROUNDS], I32)
        stage = sb("stage", [128, 4096])

        def view(tensor, start, *shape):
            n = 1
            for s in shape:
                n *= s
            flat = tensor[:, start:start + n]
            if len(shape) == 1:
                return flat
            names = "abc"[:len(shape)]
            return flat.rearrange(f"p ({' '.join(names)}) -> p {' '.join(names)}",
                                  **{k: v for k, v in zip(names, shape)})

        loads = sem("loads")
        N_LOADS = [0]

        def load(eng, dst, src):
            eng.dma_start(dst, src).then_inc(loads, 16)
            N_LOADS[0] += 1

        w_token = sb("w_token", [128, 384])
        w_context = sb("w_context", [CD, 256])
        w_out = sb("w_out", [128, 128])
        bias_out = sb("bias_out", [128, 128])
        columns = sb("columns", [128, 8])
        wq1 = sb("wq1", [128, 128])
        wkv1 = sb("wkv1", [CD, 256])
        gate_w = sb("gate_w", [128, NE])
        shared_up = sb("shared_up", [128, 2, IS])
        shared_down = sb("shared_down", [128, 2, 128])
        wq4_in = sb("wq4_in", [128, 3, IQ])
        wq4 = sb("wq4", [128, 3, IQ])
        mask_q8 = sb("mask_q8", [128, NB], U8)
        mask_q = sb("mask_q", [128, NB])
        mask_k8 = sb("mask_k8", [1, NB * CK], U8)
        mask_k = sb("mask_k", [1, NB, KEYS0], BF16)
        sig_all = sb("sig_all", [128, NQ * NT])
        context = sig_all[0:CK, NB * 256:NB * (256 + CD)].rearrange("k (b d) -> k b d", b=NB)
        context_t = sb("context_t", [CD, NB, CK])
        qkv = sb("qkv", [128, NB, 384])
        ctx_kv = sig_all[0:CK, 0:NB * 256].rearrange("k (b n) -> k b n", b=NB)
        keys1 = sb("keys1", [128, NB, CK])
        values1 = sb("values1", [CK, NB, H1, DH1 + 1])
        norms = sb("norms", [128, NB, 6])
        inv_norms = sb("inv_norms", [128, NB, 6])
        gate_all = sb("gate_all", [128, NQ, NT])
        SLOTS = 4
        w_slots = gate_all[:, :, :].rearrange("p c t -> p (c t)").rearrange("p (s w i) -> p s w i", s=SLOTS, w=3)

        memory_set = sem("memory_set")
        bn_done = sem("bn_done")
        var_ready = sem("var_ready")
        dev_ready = sem("dev_ready")
        rstd_ready = sem("rstd_ready")
        shift_ready = sem("shift_ready")
        q4_ready = sem("q4_ready")
        q4_transposed = sem("q4_transposed")
        expert_w_loaded = [sem(f"expert_w_loaded_{slot}") for slot in range(SLOTS)]
        x_loaded = sem("x_loaded")
        ctx_loaded = sem("ctx_loaded")

        vector_chain = sem("vector_chain")
        linked = [0]

        def link(dve, instruction):
            linked[0] += 1
            instruction.then_inc(vector_chain, 1)
            dve.wait_ge(vector_chain, linked[0])

        q4_work = sb("q4_work", [128, 3 * IQ + 2 * (3 * IQ // WBLOCK)])
        N_WBLOCKS = 3 * IQ // WBLOCK
        q4s = view(q4_work, 0, 3, IQ)
        q4m = view(q4_work, 3 * IQ, N_WBLOCKS)
        q4i = view(q4_work, 3 * IQ + N_WBLOCKS, N_WBLOCKS)

        def batched_rstd(k, dve, act, n):
            if dve is not None:
                if n == 2 * NB:
                    nc.vector.tensor_scalar(variance[:, 0:NB], moments[:, 0:NB, 1], 1.0 + LN_EPS, LN_EPS * LN_EPS,
                                            ALU.mult, ALU.add)
                    nc.vector.tensor_scalar(variance[:, NB:2 * NB], moments[:, NB:2 * NB, 1], LN_EPS, None,
                                            ALU.add).then_inc(var_ready, 1)
                else:
                    nc.vector.tensor_scalar(variance[:, 0:n], moments[:, 0:n, 1], LN_EPS, None,
                                            ALU.add).then_inc(var_ready, 1)
                dve.wait_ge(dev_ready, k + 1)
                nc.vector.reciprocal(rstd[:, 0:n], deviation[:, 0:n]).then_inc(rstd_ready, 1)
                dve.wait_ge(rstd_ready, k + 1)
                nc.vector.scalar_tensor_tensor(shift[:, 0:n], moments[:, 0:n, 0], -1.0, rstd[:, 0:n],
                                               ALU.mult, ALU.mult).then_inc(shift_ready, 1)
            if act is not None:
                act.wait_ge(var_ready, k + 1)
                nc.scalar.activation(deviation[:, 0:n], variance[:, 0:n], ACT.Sqrt).then_inc(dev_ready, 1)

        keys1_loaded = sem("keys1_loaded")
        keys1_projected = sem("keys1_projected")
        keys1_ready = sem("keys1_ready")
        keys1_flat = keys1[:, :, :].rearrange("p b k -> p (b k)")
        context_t_flat = context_t[:, :, :].rearrange("p b k -> p (b k)")

        with nc.Block(no_gpsimd_drain=True) as block:
            @block.sync
            def _(sp):
                sp.dma_start(x_all[:, :, :], d["x"].rearrange("b t d -> t b d")).then_inc(x_loaded, 16)
                load(sp, const[:, :], d["const"])
                load(sp, columns[:, :], d["columns"])
                load(sp, w_token[:, :], d["w_token"])
                load(sp, w_context[:, :], d["w_context"])
                load(sp, w_out[:, :], d["w_out"])
                load(sp, bias_out[:, :], d["bias_out"].rearrange("(a n) -> a n", a=1).to_broadcast([128, 128]))
                for m, name in enumerate(("w_gate", "w_up")):
                    load(sp, wq4_in[:, m, :].rearrange("p (c i) -> p c i", c=NQ),
                         d[name].rearrange("(c p) i -> p c i", p=128))
                load(sp, wq4_in[:, 2, :], d["w_down"])
                for e in range(SLOTS):
                    sp.dma_start(w_slots[:, e], d["expert_w"][e]).then_inc(expert_w_loaded[e], 16)

            @block.scalar
            def _(act):
                act.dma_start(context[:, :, :], d["context"].rearrange("b k d -> k b d")).then_inc(ctx_loaded, 16)
                act.dma_start(context_t[:, :, :], d["context_t"]).then_inc(keys1_loaded, 16)
                act.dma_start(wkv1[:, :], d["wkv1"]).then_inc(keys1_loaded, 16)
                load(act, const16[:, :], d["const16"])
                load(act, patterns[:, :], d["patterns"])
                load(act, wq1[:, :], d["wq1"])
                load(act, gate_w[:, :], d["gate_w"])
                load(act, shared_up[:, :, :], d["shared_up"])
                load(act, shared_down[:, :, :], d["shared_down"])
                load(act, mask_q8[:, :], d["mask_q"])
                load(act, mask_k8[:, :], d["mask_k"].rearrange("(a n) -> a n", a=1))
                for n in range(3):
                    act.wait_ge(keys1_projected, n + 1)
                    nc.scalar.copy(keys1_flat[:, n * 512:min(n * 512 + 512, NB * CK)],
                                   bank[n][:, 0:min(512, NB * CK - n * 512)]).then_inc(keys1_ready, 1)
                batched_rstd(0, None, act, 2 * NB)

            @block.tensor
            def _(pe):
                pe.wait_ge(keys1_loaded, 32)
                for n in range(3):
                    nc.tensor.matmul(bank[n][:, 0:min(512, NB * CK - n * 512)], wkv1[:, 0:128],
                                     context_t_flat[:, n * 512:min(n * 512 + 512, NB * CK)], start=True, stop=True
                                     ).then_inc(keys1_projected, 1)

            @block.gpsimd
            def _(pool):
                nc.gpsimd.memset(moments[:, :, :], 1.0).then_inc(memory_set, 1)
                nc.gpsimd.memset(norms[:, :, :], 1.0).then_inc(memory_set, 1)
                nc.gpsimd.memset(mask_k[:, :, CK:KEYS0], 0.0).then_inc(memory_set, 1)
                nc.gpsimd.memset(values1[:, :, :, DH1:DH1 + 1], 1.0).then_inc(memory_set, 1)

            @block.vector
            def _(dve):
                dve.wait_ge(memory_set, 4)
                dve.wait_ge(x_loaded, 16)
                for b in range(NB):
                    nc.vector.bn_stats(bn[:, b, :], x_all[:, b, :]).then_inc(bn_done, 1)
                dve.wait_ge(ctx_loaded, 16)
                for b in range(NB):
                    nc.vector.bn_stats(bn[0:CK, NB + b, :], context[:, b, :]).then_inc(bn_done, 1)
                dve.wait_ge(bn_done, 2 * NB)
                for b in range(2 * NB):
                    p = 128 if b < NB else CK
                    last = nc.vector.bn_aggr(moments[0:p, b, :], bn[0:p, b, :])
                link(dve, last)
                batched_rstd(0, dve, None, 2 * NB)
                dve.wait_ge(loads, 16 * N_LOADS[0])
                nc.vector.tensor_copy(mask_q[:, :], mask_q8[:, :])
                nc.vector.tensor_scalar(mask_k[:, :, 0:CK], mask_k8[:, :].rearrange("p (b k) -> p b k", b=NB),
                                        -1.0, -MASKED, ALU.add, ALU.mult)
                nc.vector.scalar_tensor_tensor(columns[:, 6:7], columns[:, 4:5], DH0 ** -0.5, columns[:, 5:6],
                                               ALU.mult, ALU.mult)

        a1_xn_ready = sem("a1_xn_ready")
        a1_cn_ready = sem("a1_cn_ready")
        a1_transposed = sem("a1_transposed")
        a1_lnT_ready = sem("a1_lnT_ready")
        a1_cnT_ready = sem("a1_cnT_ready")
        a1_rawT_ready = sem("a1_rawT_ready")
        a1_projected = sem("a1_projected")
        a1_qkv_ready = sem("a1_qkv_ready")
        a1_ctx_kv_ready = sem("a1_ctx_kv_ready")
        a1_values1_ready = sem("a1_values1_ready")
        a1_squares_ready = sem("a1_squares_ready")
        a1_ctx_squares_ready = sem("a1_ctx_squares_ready")
        a1_sums_ready = sem("a1_sums_ready")
        a1_norms_ready = sem("a1_norms_ready")

        xn = [view(stage, 1024 * p, 128) for p in range(2)]
        cn = [view(stage, 1024 * p + 128, CD)[0:CK] for p in range(2)]
        lnT = [view(stage, 1024 * p + 256, 128) for p in range(2)]
        cnT = [view(stage, 1024 * p + 384, CK)[0:CD] for p in range(2)]
        rawT = [view(stage, 1024 * p + 464, CK)[0:CD] for p in range(2)]
        squares = [view(stage, 1024 * p + 544, 4, DH0) for p in range(2)]
        ctx_squares = [view(stage, 1024 * p + 800, 2, DH0)[0:CK] for p in range(2)]

        with nc.Block(no_gpsimd_drain=True) as block:
            @block.gpsimd
            def _(pool):
                def step(i, u):
                    if live(i, NB):
                        pool.wait_ge(a1_xn_ready, i + 1)
                        nc.gpsimd.tensor_tensor(x_all[:, i, :], x_all[:, i, :], bias_out[:, :], ALU.add)
                    b = i - 1
                    if live(b, NB):
                        if live(b - 2, NB):
                            pool.wait_ge(a1_projected, b - 1)
                        nc.gpsimd.tensor_copy(rawT[(u + 1) % 2], context_t[:, b, :]).then_inc(a1_rawT_ready, 1)
                    b = i - 3
                    if live(b, NB):
                        if live(b - 2, NB):
                            pool.wait_ge(a1_sums_ready, b - 1)
                        pool.wait_ge(a1_qkv_ready, b + 1)
                        qk = qkv[:, b, 0:256].rearrange("p (h e) -> p h e", h=4)
                        nc.gpsimd.tensor_tensor(squares[(u + 1) % 2], qk, qk, ALU.mult).then_inc(a1_squares_ready, 1)

                skewed(pool, NB, 4, step, unroll=2)

            @block.vector
            def _(dve):
                def step(i, u):
                    if live(i, NB):
                        if live(i - 2, NB):
                            dve.wait_ge(a1_transposed, i - 1)
                        nc.vector.tensor_scalar(xn[u], x_all[:, i, :], rstd[:, bass.ds(i, 1)], shift[:, bass.ds(i, 1)],
                                                ALU.mult, ALU.add).then_inc(a1_xn_ready, 1)
                    b = i - 1
                    if live(b, NB):
                        dve.wait_ge(a1_transposed, b + 1)
                        if live(b - 2, NB):
                            dve.wait_ge(a1_projected, b - 1)
                        p = (u + 1) % 2
                        nc.vector.tensor_scalar(cnT[p], bank[2 + p][0:CD, 0:CK], columns[0:CD, 2:3], columns[0:CD, 3:4],
                                                ALU.mult, ALU.add).then_inc(a1_cnT_ready, 1)
                    b = i - 2
                    if live(b, NB):
                        dve.wait_ge(a1_projected, b + 1)
                        nc.vector.tensor_copy(ctx_kv[:, b, :], bank[6 + u][0:CK, 0:256]).then_inc(a1_ctx_kv_ready, 1)
                        nc.vector.tensor_copy(values1[:, b, :, 0:DH1], bank[6 + u][0:CK, 336:464].rearrange(
                            "p (h e) -> p h e", h=H1)).then_inc(a1_values1_ready, 1)
                    b = i - 4
                    if live(b, NB):
                        dve.wait_ge(a1_squares_ready, b + 1)
                        nc.vector.tensor_reduce(norms[:, b, 0:4], squares[u], axis=AX.X, op=ALU.add)
                        dve.wait_ge(a1_ctx_squares_ready, b + 1)
                        nc.vector.tensor_reduce(norms[0:CK, b, 4:6], ctx_squares[u], axis=AX.X,
                                                op=ALU.add).then_inc(a1_sums_ready, 1)

                skewed(dve, NB, 4, step, unroll=2)
                dve.wait_ge(a1_norms_ready, 1)
                link(dve, nc.vector.tensor_scalar(norms[:, :, :], norms[:, :, :], RMS_EPS, None, ALU.max))
                nc.vector.reciprocal(inv_norms[:, :, :], norms[:, :, :])

            @block.scalar
            def _(act):
                def step(i, u):
                    if live(i, NB):
                        if live(i - 2, NB):
                            act.wait_ge(a1_transposed, i - 1)
                        nc.scalar.activation(cn[u], context[:, i, :], ACT.Identity, bias=shift[0:CK, bass.ds(i + NB, 1)],
                                             scale=rstd[0:CK, bass.ds(i + NB, 1)]).then_inc(a1_cn_ready, 1)
                    b = i - 1
                    if live(b, NB):
                        act.wait_ge(a1_transposed, b + 1)
                        if live(b - 2, NB):
                            act.wait_ge(a1_projected, b - 1)
                        p = (u + 1) % 2
                        nc.scalar.activation(lnT[p], bank[p][:, 0:128], ACT.Identity, bias=columns[:, 1:2],
                                             scale=columns[:, 0:1]).then_inc(a1_lnT_ready, 1)
                    b = i - 2
                    if live(b, NB):
                        act.wait_ge(a1_projected, b + 1)
                        nc.scalar.copy(qkv[:, b, :], bank[4 + u][:, 0:384]).then_inc(a1_qkv_ready, 1)
                    b = i - 3
                    if live(b, NB):
                        if live(b - 2, NB):
                            act.wait_ge(a1_sums_ready, b - 1)
                        act.wait_ge(a1_ctx_kv_ready, b + 1)
                        nc.scalar.activation(ctx_squares[(u + 1) % 2], ctx_kv[:, b, 0:128].rearrange(
                            "p (h e) -> p h e", h=2), ACT.Square).then_inc(a1_ctx_squares_ready, 1)

                skewed(act, NB, 4, step, unroll=2)
                act.wait_ge(a1_sums_ready, NB)
                nc.scalar.activation(norms[:, :, :], norms[:, :, :], ACT.Sqrt, scale=1.0 / DH0
                                     ).then_inc(a1_norms_ready, 1)

            @block.tensor
            def _(pe):
                pe.wait_ge(keys1_ready, 3)

                def step(i, u):
                    b = i - 1
                    if live(b, NB):
                        p = (u + 1) % 2
                        pe.wait_ge(a1_xn_ready, b + 1)
                        nc.tensor.transpose(bank[p][:, 0:128], xn[p], ident)
                        pe.wait_ge(a1_cn_ready, b + 1)
                        nc.tensor.transpose(bank[2 + p][0:CD, 0:CK], cn[p], ident[0:CK, 0:CK]
                                            ).then_inc(a1_transposed, 1)
                    b = i - 2
                    if live(b, NB):
                        pe.wait_ge(a1_lnT_ready, b + 1)
                        if live(b - 2, NB):
                            pe.wait_ge(a1_qkv_ready, b - 1)
                            pe.wait_ge(a1_values1_ready, b - 1)
                        nc.tensor.matmul(bank[4 + u][:, 0:384], lnT[u], w_token[:, :], start=True, stop=True)
                        pe.wait_ge(a1_cnT_ready, b + 1)
                        nc.tensor.matmul(bank[6 + u][0:CK, 0:256], cnT[u], w_context[:, :], start=True, stop=True)
                        pe.wait_ge(a1_rawT_ready, b + 1)
                        nc.tensor.matmul(bank[6 + u][0:CK, 336:464], rawT[u], wkv1[:, 128:256], start=True, stop=True
                                         ).then_inc(a1_projected, 1)

                skewed(pe, NB, 4, step, unroll=2)

        a2_q_normed = sem("a2_q_normed")
        a2_k_normed = sem("a2_k_normed")
        a2_values_ready = sem("a2_values_ready")
        a2_transposed = sem("a2_transposed")
        a2_qT_ready = sem("a2_qT_ready")
        a2_kT_ready = sem("a2_kT_ready")
        a2_scored = sem("a2_scored")
        a2_max_ready = sem("a2_max_ready")
        a2_exp_ready = sem("a2_exp_ready")
        a2_weights_ready = sem("a2_weights_ready")
        a2_weights_transposed = sem("a2_weights_transposed")
        a2_ctx_wT_ready = sem("a2_ctx_wT_ready")
        a2_lat_wT_ready = sem("a2_lat_wT_ready")
        a2_mixed = sem("a2_mixed")
        a2_outT_ready = sem("a2_outT_ready")
        a2_inv_sum_ready = sem("a2_inv_sum_ready")
        a2_out_projected = sem("a2_out_projected")
        a2_x_ready = sem("a2_x_ready")
        a2_x_bn_done = sem("a2_x_bn_done")

        qk_n = [view(stage, 0 + 384 * p, 4, DH0) for p in range(2)]
        ck_n = [view(stage, 256 + 384 * p, 2, DH0)[0:CK] for p in range(2)]
        weights = [view(stage, 768 + H0 * KEYS0 * p, H0, KEYS0) for p in range(2)]
        lat_values = [view(stage, 1664 + 256 * p, 128) for p in range(2)]
        ctx_values = [view(stage, 1792 + 256 * p, 128)[0:CK] for p in range(2)]
        qT = view(stage, 2176, 128)
        kT = view(stage, 2304, KEYS0)
        ctx_wT = view(stage, 2560, H0, 128)[0:CK]
        lat_wT = view(stage, 2816, H0, 128)
        outT = view(stage, 3072, 128)
        neg_max = view(stage, 3200, H0)
        weight_sum = view(stage, 3232, NB, H0)
        inv_sum = view(stage, 3264, NB, H0)
        score = [bank[2], bank[3]]

        with nc.Block(no_gpsimd_drain=True) as block:
            @block.gpsimd
            def _(pool):
                def step(i, u):
                    if live(i, NB):
                        if live(i - 2, NB):
                            pool.wait_ge(a2_transposed, i - 1)
                        nc.gpsimd.tensor_tensor(qk_n[u], qkv[:, i, 0:256].rearrange("p (h e) -> p h e", h=4),
                                                inv_norms[:, i, 0:4, None].to_broadcast([128, 4, DH0]), ALU.mult
                                                ).then_inc(a2_q_normed, 1)
                        nc.gpsimd.tensor_tensor(ck_n[u], ctx_kv[:, i, 0:128].rearrange("p (h e) -> p h e", h=2),
                                                inv_norms[0:CK, i, 4:6, None].to_broadcast([CK, 2, DH0]), ALU.mult
                                                ).then_inc(a2_k_normed, 1)
                    b = i - 3
                    if live(b, NB):
                        if live(b - 2, NB):
                            pool.wait_ge(a2_mixed, b - 1)
                        nc.gpsimd.tensor_copy(lat_values[(u + 1) % 2], qkv[:, b, 256:384])
                        nc.gpsimd.tensor_copy(ctx_values[(u + 1) % 2], ctx_kv[:, b, 128:256]).then_inc(a2_values_ready, 1)

                skewed(pool, NB, 4, step, unroll=2)

            @block.tensor
            def _(pe):
                def step(i, u):
                    other = (u + 1) % 2
                    b = i - 2
                    if live(b, NB):
                        pe.wait_ge(a2_qT_ready, b + 1)
                        pe.wait_ge(a2_kT_ready, b + 1)
                        if live(b - 1, NB):
                            pe.wait_ge(a2_exp_ready, b)
                        for h in range(H0):
                            rows = slice(h * DH0, (h + 1) * DH0)
                            nc.tensor.matmul(score[h][:, 0:KEYS0], qT[rows, :], kT[rows, :], start=True, stop=False)
                            last = nc.tensor.matmul(score[h][:, 0:KEYS0], ones16[0:1, :], mask_k[:, b, :],
                                                    start=False, stop=True)
                        last.then_inc(a2_scored, 1)
                    b = i - 5
                    if live(b, NB):
                        pe.wait_ge(a2_outT_ready, b + 1)
                        if live(b - 1, NB):
                            pe.wait_ge(a2_x_ready, b)
                        nc.tensor.matmul(bank[7][:, 0:128], outT, w_out[:, :], start=True, stop=True
                                         ).then_inc(a2_out_projected, 1)
                    b = i - 1
                    if live(b, NB):
                        pe.wait_ge(a2_q_normed, b + 1)
                        pe.wait_ge(a2_k_normed, b + 1)
                        qk_flat = qk_n[other].rearrange("p h e -> p (h e)")
                        ck_flat = ck_n[other].rearrange("p h e -> p (h e)")
                        nc.tensor.transpose(bank[0][:, 0:128], qk_flat[:, 0:128], ident)
                        nc.tensor.transpose(bank[1][:, 0:CK], ck_flat, ident[0:CK, 0:CK])
                        nc.tensor.transpose(bank[1][:, CK:KEYS0], qk_flat[:, 128:256], ident
                                            ).then_inc(a2_transposed, 1)
                    b = i - 4
                    if live(b, NB):
                        pe.wait_ge(a2_ctx_wT_ready, b + 1)
                        pe.wait_ge(a2_lat_wT_ready, b + 1)
                        pe.wait_ge(a2_values_ready, b + 1)
                        for h in range(H0):
                            rows = slice(h * DH0, (h + 1) * DH0)
                            nc.tensor.matmul(bank[6][rows, 0:128], ctx_values[u][:, rows], ctx_wT[:, h, :],
                                             start=True, stop=False, tile_position=(0, h * DH0))
                            last = nc.tensor.matmul(bank[6][rows, 0:128], lat_values[u][:, rows], lat_wT[:, h, :],
                                                    start=False, stop=True, tile_position=(0, h * DH0))
                        last.then_inc(a2_mixed, 1)
                    b = i - 3
                    if live(b, NB):
                        pe.wait_ge(a2_weights_ready, b + 1)
                        for h in range(H0):
                            nc.tensor.transpose(bank[4][0:CK, h * 128:(h + 1) * 128], weights[other][:, h, 0:CK], ident)
                            last = nc.tensor.transpose(bank[5][:, h * 128:(h + 1) * 128], weights[other][:, h, CK:KEYS0],
                                                       ident)
                        last.then_inc(a2_weights_transposed, 1)

                skewed(pe, NB, 6, step, unroll=2)

            @block.scalar
            def _(act):
                def step(i, u):
                    b = i - 2
                    if live(b, NB):
                        act.wait_ge(a2_max_ready, b + 1)
                        for h in range(H0):
                            last = nc.scalar.activation(weights[u][:, h, :], score[h][:, 0:KEYS0], ACT.Exp,
                                                        bias=neg_max[:, h:h + 1],
                                                        accum_out=weight_sum[:, bass.ds(b, 1), h:h + 1].rearrange(
                                                            "p o h -> p (o h)"))
                        last.then_inc(a2_exp_ready, 1)
                    b = i - 1
                    if live(b, NB):
                        act.wait_ge(a2_transposed, b + 1)
                        nc.scalar.activation(qT, bank[0][:, 0:128], ACT.Copy, scale=columns[:, 6:7]
                                             ).then_inc(a2_qT_ready, 1)
                    b = i - 4
                    if live(b, NB):
                        act.wait_ge(a2_mixed, b + 1)
                        nc.scalar.copy(outT, bank[6][:, 0:128]).then_inc(a2_outT_ready, 1)
                    b = i - 2
                    if live(b, NB):
                        act.wait_ge(a2_inv_sum_ready, b + 1)
                        for h in range(H0):
                            last = nc.scalar.activation(weights[u][:, h, :], weights[u][:, h, :], ACT.Copy,
                                                        scale=inv_sum[:, bass.ds(b, 1), h:h + 1].rearrange(
                                                            "p o h -> p (o h)"))
                        last.then_inc(a2_weights_ready, 1)
                    b = i - 3
                    if live(b, NB):
                        act.wait_ge(a2_weights_transposed, b + 1)
                        nc.scalar.copy(ctx_wT, bank[4][0:CK, 0:256].rearrange("p (h q) -> p h q", h=H0)
                                       ).then_inc(a2_ctx_wT_ready, 1)

                skewed(act, NB, 6, step, unroll=2)
                batched_rstd(1, None, act, NB)

            @block.vector
            def _(dve):
                def step(i, u):
                    b = i - 2
                    if live(b, NB):
                        dve.wait_ge(a2_scored, b + 1)
                        for h in range(H0):
                            last = nc.vector.tensor_reduce(neg_max[:, h:h + 1], score[h][:, 0:KEYS0], axis=AX.X,
                                                           op=ALU.max, negate=True)
                        last.then_inc(a2_max_ready, 1)

                    if live(i - 1, NB):
                        dve.wait_ge(a2_transposed, i)
                        nc.vector.tensor_copy(kT, bank[1][:, 0:KEYS0]).then_inc(a2_kT_ready, 1)
                    b = i - 5
                    if live(b, NB):
                        dve.wait_ge(a2_out_projected, b + 1)
                        nc.vector.tensor_tensor(x_all[:, b, :], bank[7][:, 0:128], x_all[:, b, :], ALU.add
                                                ).then_inc(a2_x_ready, 1)
                    if live(i - 2, NB):
                        dve.wait_ge(a2_exp_ready, i - 1)
                        nc.vector.reciprocal(inv_sum[:, i - 2, :], weight_sum[:, i - 2, :]).then_inc(a2_inv_sum_ready, 1)
                    if live(b, NB):
                        dve.wait_ge(a2_x_ready, b + 1)
                        nc.vector.bn_stats(bn[:, b, :], x_all[:, b, :]).then_inc(a2_x_bn_done, 1)
                    b = i - 3
                    if live(b, NB):
                        dve.wait_ge(a2_weights_transposed, b + 1)
                        nc.vector.tensor_copy(lat_wT, bank[5][:, 0:256].rearrange("p (h q) -> p h q", h=H0)
                                              ).then_inc(a2_lat_wT_ready, 1)

                skewed(dve, NB, 6, step, unroll=2)
                dve.wait_ge(a2_x_bn_done, NB)
                for b in range(NB):
                    last = nc.vector.bn_aggr(moments[:, b, :], bn[:, b, :])
                link(dve, last)
                batched_rstd(1, dve, None, NB)

        b1_transposed = sem("b1_transposed")
        b1_hT_ready = sem("b1_hT_ready")
        b1_logits_ready = sem("b1_logits_ready")
        b1_shifted = sem("b1_shifted")
        b1_exp_ready = sem("b1_exp_ready")
        b1_scores_ready = sem("b1_scores_ready")

        rows = sb("rows_all", [128, NB, GROW])
        h_rows = rows[:, :, 0:D]
        hT_all = sb("hT_all", [128, NT])
        scores = sb("scores", [128, NB, NE])
        sm_max = view(stage, 256, NB)
        sm_sum = view(stage, 272, NB)
        QT = NT // 4

        def quarter(q):
            return slice(q * QT, (q + 1) * QT)

        h_by_vector = sem("h_by_vector")
        h_by_scalar = sem("h_by_scalar")

        def normed(eng, gain, shift):
            for q in range(4):
                if (q < 2) != (eng is nc.vector):
                    continue
                for b in range(4 * q, 4 * q + 4):
                    if eng is nc.vector:
                        last = nc.vector.tensor_scalar(h_rows[:, b, :], x_all[:, b, :], gain[:, b:b + 1],
                                                       shift[:, b:b + 1], ALU.mult, ALU.add)
                    else:
                        last = nc.scalar.activation(h_rows[:, b, :], x_all[:, b, :], ACT.Identity,
                                                    bias=shift[:, b:b + 1], scale=gain[:, b:b + 1])
                last.then_inc(h_by_vector if q < 2 else h_by_scalar, 1)

        def wait_normed(eng, phase, q):
            eng.wait_ge(h_by_vector if q < 2 else h_by_scalar, 2 * phase + q % 2 + 1)

        def transposed_rows(q, out, signal):
            for j in range(4):
                last = nc.tensor.transpose(out[:, j * T:(j + 1) * T], h_rows[:, q * 4 + j, :], ident)
            last.then_inc(signal, 1)

        with nc.Block(no_gpsimd_drain=True) as block:
            @block.scalar
            def _(act):
                act.wait_ge(shift_ready, 2)
                normed(nc.scalar, rstd, shift)
                for q in range(4):
                    act.wait_ge(b1_transposed, q + 1)
                    nc.scalar.copy(hT_all[:, quarter(q)], bank[q][:, :]).then_inc(b1_hT_ready, 1)
                act.wait_ge(b1_shifted, 1)
                nc.scalar.activation(scores[:, :, :], scores[:, :, :], ACT.Exp).then_inc(b1_exp_ready, 1)

            @block.tensor
            def _(pe):
                for q in range(5):
                    if q < 4:
                        wait_normed(pe, 0, q)
                        transposed_rows(q, bank[q], b1_transposed)
                    if q > 0:
                        pe.wait_ge(b1_hT_ready, q)
                        for b in range(4 * q - 4, 4 * q):
                            last = nc.tensor.matmul(bank[7][:, b * NE:(b + 1) * NE], hT_all[:, b * T:(b + 1) * T],
                                                    gate_w[:, :], start=True, stop=True)
                last.then_inc(b1_logits_ready, 1)

            @block.vector
            def _(dve):
                dve.wait_ge(shift_ready, 2)
                normed(nc.vector, rstd, shift)
                dve.wait_ge(b1_logits_ready, 1)
                logits = bank[7][:, 0:NB * NE].rearrange("p (b e) -> p b e", b=NB)
                link(dve, nc.vector.tensor_reduce(sm_max, logits, axis=AX.X, op=ALU.max))
                nc.vector.tensor_tensor(scores[:, :, :], logits, sm_max[:, :, None].to_broadcast([128, NB, NE]),
                                        ALU.subtract).then_inc(b1_shifted, 1)
                dve.wait_ge(b1_exp_ready, 1)
                link(dve, nc.vector.tensor_reduce(sm_sum, scores[:, :, :], axis=AX.X, op=ALU.add))
                link(dve, nc.vector.reciprocal(sm_max, sm_sum))
                nc.vector.tensor_tensor(scores[:, :, :], scores[:, :, :],
                                        sm_max[:, :, None].to_broadcast([128, NB, NE]), ALU.mult
                                        ).then_inc(b1_scores_ready, 1)
                dve.wait_ge(b1_scores_ready, 1)
                nc.vector.tensor_copy(rows[:, :, D:GROW], scores[:, :, :])

        rows_stored = sem("rows_stored")
        sums_stored = sem("sums_stored")
        b2_scoresT = sem("b2_scoresT")
        b2_scoresT_ready = sem("b2_scoresT_ready")
        b2_trial_ready = sem("b2_trial_ready")
        b2_counted = sem("b2_counted")
        b2_total_ready = sem("b2_total_ready")
        b2_hits_ready = sem("b2_hits_ready")
        b2_value_ready = sem("b2_value_ready")
        b2_found_ready = sem("b2_found_ready")
        b2_gate_ready = sem("b2_gate_ready")
        b2_up_ready = sem("b2_up_ready")
        b2_gelu_ready = sem("b2_gelu_ready")
        b2_hidden_ready = sem("b2_hidden_ready")
        b2_shared_ready = sem("b2_shared_ready")
        b2_added = sem("b2_added")
        b3_wide_ready = sem("b3_wide_ready")
        b3_threshold_ready = sem("b3_threshold_ready")
        b3_above_ready = sem("b3_above_ready")
        b3_from_ready = sem("b3_from_ready")
        b3_scanned = sem("b3_scanned")
        b3_earlier_ready = sem("b3_earlier_ready")
        b3_above_counted = sem("b3_above_counted")
        b3_equal_ranked = sem("b3_equal_ranked")
        b3_in_need = sem("b3_in_need")
        b3_taken_ranked = sem("b3_taken_ranked")

        PAIRS = NB // 2
        scoresT = view(stage, 0, NB * T // 8)
        trial = view(stage, 2000, 3).bitcast(I32)
        found = view(stage, 2004, 1).bitcast(I32)
        value = view(stage, 2006, 1).bitcast(I32)
        hits = view(stage, 2008, 1)
        hit3 = view(stage, 2010, 3)
        count16 = sb("count16", [128, 4], BF16)
        junk16 = sb("junk16", [128, 3, 256], BF16)
        gelu_s = view(stage, 260, 2, 256)
        hidden_s = view(stage, 772, 2, 256)
        wide = view(stage, 1284, 128)
        sel16 = sb("sel16", [128, 6, NE * NB], BF16)
        above, equal, earlier, taken = (sel16[:, n, :] for n in range(4))
        from16, in_need = sel16[:, 4, :], sel16[:, 5, :]
        need = view(stage, 1412, NE)
        scan = view(stage, 1430, NE * NB)
        place = view(stage, 1686, NE * NB)
        low = sb("low", [128, NE * NB])
        half = sb("half", [128, 2, NE * NB])
        halves = sb("halves", [128, NE * NB, 2], F16)

        def ranks(pe, bits, earlier_bits, out):
            nc.tensor.matmul(out, before, bits, start=True, stop=False)
            return nc.tensor.matmul(out, ones16, earlier_bits, start=False, stop=True)

        with nc.Block(no_gpsimd_drain=True) as block:
            @block.sync
            def _(sp):
                sp.dma_start(d["rows"].rearrange("(b t) c -> t b c", b=NB), rows[:, :, :]).then_inc(rows_stored, 16)
                sp.wait_ge(b2_added, PAIRS)
                sp.dma_start(d["sums"].rearrange("(b t) c -> t b c", b=NB), x_all[:, :, :]).then_inc(sums_stored, 16)

            @block.tensor
            def _(pe):
                scores_flat = scores[:, :, :].rearrange("p b e -> p (b e)")
                for n in range(2):
                    last = nc.tensor.transpose(bank[6][:, n * 128:(n + 1) * 128], scores_flat[:, n * 128:(n + 1) * 128],
                                               ident)
                last.then_inc(b2_scoresT, 1)

                def down(c, m):
                    for k in range(2):
                        last = nc.tensor.matmul(bank[5][:, m * 128:(m + 1) * 128], hidden_s[:, k, m * 128:(m + 1) * 128],
                                                shared_down[:, k, :], start=(k == 0), stop=(k == 1))
                    return last

                def up(c, which, k):
                    bk = bank[1 + 2 * which]
                    return nc.tensor.matmul(bk[:, k * 256:(k + 1) * 256],
                                            shared_up[:, which, k * 128:(k + 1) * 128],
                                            hT_all[:, bass.ds(c * 256, 256)], start=True, stop=True)

                def total(n):
                    pe.wait_ge(b2_counted, n + 1)
                    nc.tensor.matmul(bank[6][:, 0:3], same_expert, count16[:, 0:3], start=True, stop=True
                                     ).then_inc(b2_total_ready, 1)

                def gates(c):
                    if live(c - 1, PAIRS):
                        pe.wait_ge(b2_gelu_ready, c)
                    up(c, 0, 0)
                    up(c, 0, 1).then_inc(b2_gate_ready, 1)

                def ups(c):
                    up(c, 1, 0)
                    up(c, 1, 1).then_inc(b2_up_ready, 1)

                def downs(c):
                    pe.wait_ge(b2_hidden_ready, c + 1)
                    if live(c - 1, PAIRS):
                        pe.wait_ge(b2_added, c)
                    down(c, 0)
                    down(c, 1).then_inc(b2_shared_ready, 1)

                def step(c):
                    total(2 * c)
                    gates(c)
                    if live(c - 1, PAIRS):
                        downs(c - 1)
                    total(2 * c + 1)
                    ups(c)

                step(0)
                with pe.Fori(1, PAIRS - 1) as c:
                    step(c)
                total(ROUNDS - 1)
                gates(PAIRS - 1)
                pe.wait_ge(b3_wide_ready, 1)
                nc.tensor.transpose(bank[0][:, 0:128], wide, ident).then_inc(b3_threshold_ready, 1)
                downs(PAIRS - 2)
                ups(PAIRS - 1)
                pe.wait_ge(b3_above_ready, 1)
                nc.tensor.matmul(bank[7][:, 0:256], ones16, above, start=True, stop=True).then_inc(b3_above_counted, 1)
                downs(PAIRS - 1)
                pe.wait_ge(b3_earlier_ready, 1)
                ranks(pe, equal, earlier, bank[2][:, 0:256]).then_inc(b3_equal_ranked, 1)
                pe.wait_ge(b3_earlier_ready, 2)
                ranks(pe, taken, earlier, bank[3][:, 0:256]).then_inc(b3_taken_ranked, 1)

            @block.scalar
            def _(act):
                def step(c, u):
                    act.wait_ge(b2_gate_ready, c + 1)
                    if live(c - 1, PAIRS):
                        act.wait_ge(b2_hidden_ready, c)
                    nc.scalar.activation(gelu_s, bank[1][:, 0:512].rearrange("p (k t) -> p k t", k=2), ACT.Gelu
                                         ).then_inc(b2_gelu_ready, 1)

                step(0, 0)
                with act.Fori(1, PAIRS) as c:
                    step(c, 0)

            @block.vector
            def _(dve):
                dve.wait_ge(b2_scoresT, 1)
                nc.vector.tensor_copy(scoresT, bank[6][:, 0:256]).then_inc(b2_scoresT_ready, 1)
                nc.vector.memset(found, 0).then_inc(b2_found_ready, 1)
                nc.vector.tensor_copy(trial, patterns[:, 0:3]).then_inc(b2_trial_ready, 1)
                dve.wait_ge(b2_scoresT_ready, 1)

                def bits(n, next_round, between):
                    dve.wait_ge(b2_trial_ready, n + 1)
                    for j in range(3):
                        last = nc.vector.tensor_scalar(junk16[:, j, :], scoresT, trial[:, j:j + 1].bitcast(F32), None,
                                                       ALU.is_ge, ALU.add, accum_out=count16[:, j:j + 1])
                    last.then_inc(b2_counted, 1)
                    if not isinstance(n, int) or n > 0:
                        nc.vector.tensor_tensor(found, found, value, ALU.bitwise_or).then_inc(b2_found_ready, 1)
                    if between is not None:
                        between()
                    dve.wait_ge(b2_total_ready, n + 1)
                    nc.vector.tensor_scalar(hit3, bank[6][:, 0:3], float(CAP), None, ALU.is_ge, ALU.add,
                                            accum_out=hits).then_inc(b2_hits_ready, 1)
                    dve.wait_ge(b2_hits_ready, n + 1)
                    dve.wait_ge(b2_found_ready, n + 1)
                    nc.vector.tensor_scalar(value, hits, unit_of_round[:, bass.ds(n, 1)], None, ALU.mult
                                            ).then_inc(b2_value_ready, 1)
                    dve.wait_ge(b2_value_ready, n + 1)
                    if next_round:
                        nc.vector.scalar_tensor_tensor(trial, patterns[:, bass.ds(n * 3 + 3, 3)], value,
                                                       found.to_broadcast([128, 3]), ALU.bitwise_or, ALU.bitwise_or
                                                       ).then_inc(b2_trial_ready, 1)

                def hidden(c):
                    dve.wait_ge(b2_up_ready, c + 1)
                    dve.wait_ge(b2_gelu_ready, c + 1)
                    if live(c - 1, PAIRS):
                        dve.wait_ge(b2_shared_ready, c)
                    nc.vector.tensor_tensor(hidden_s, gelu_s, bank[3][:, 0:512].rearrange("p (k t) -> p k t", k=2),
                                            ALU.mult).then_inc(b2_hidden_ready, 1)

                def add(c):
                    dve.wait_ge(b2_shared_ready, c + 1)
                    xs = x_all[:, bass.ds(c * 2, 2), :]
                    nc.vector.tensor_tensor(xs, bank[5][:, 0:256].rearrange("p (b d) -> p b d", b=2), xs, ALU.add
                                            ).then_inc(b2_added, 1)

                def step(c):
                    first = isinstance(c, int) and c == 0
                    bits(2 * c, True, None if first else lambda: hidden(c - 1))
                    bits(2 * c + 1, True, None if first else lambda: add(c - 1))

                step(0)
                with dve.Fori(1, PAIRS - 1) as c:
                    step(c)
                bits(ROUNDS - 1, False, lambda: hidden(PAIRS - 2))
                nc.vector.tensor_tensor(found, found, value, ALU.bitwise_or).then_inc(b2_found_ready, 1)
                dve.wait_ge(b2_found_ready, ROUNDS + 1)
                nc.vector.tensor_copy(wide, found.bitcast(F32).to_broadcast([128, 128])).then_inc(b3_wide_ready, 1)
                dve.wait_ge(b3_threshold_ready, 1)

                def compared(out, op, signal):
                    for n in range(2):
                        last = nc.vector.tensor_tensor(
                            out.rearrange("p (e n j) -> p n j e", n=2, j=8)[:, n],
                            scores[:, n * 8:(n + 1) * 8, :], bank[0][:, 0:128].rearrange("p (j e) -> p j e", j=8), op)
                    last.then_inc(signal, 1)

                compared(above, ALU.is_gt, b3_above_ready)
                compared(from16, ALU.is_ge, b3_from_ready)
                add(PAIRS - 2)
                hidden(PAIRS - 1)
                dve.wait_ge(b3_from_ready, 1)
                link(dve, nc.vector.tensor_tensor(equal, from16, above, ALU.subtract))

                def earlier_of(bits, n):
                    if n:
                        dve.wait_ge(b3_equal_ranked, n)
                    nc.vector.tensor_tensor_scan(scan, first_batch, bits, 0.0, ALU.mult, ALU.add
                                                 ).then_inc(b3_scanned, 1)
                    dve.wait_ge(b3_scanned, n + 1)
                    nc.vector.tensor_tensor(earlier, scan, bits, ALU.subtract).then_inc(b3_earlier_ready, 1)

                earlier_of(equal, 0)
                add(PAIRS - 1)
                dve.wait_ge(b3_above_counted, 1)
                link(dve, nc.vector.tensor_reduce(need, bank[7][:, 0:256].rearrange("p (e b) -> p e b", b=NB), axis=AX.X,
                                        op=ALU.add))
                link(dve, nc.vector.tensor_scalar(need, need, -1.0, float(CAP), ALU.mult, ALU.add))
                dve.wait_ge(b3_equal_ranked, 1)
                nc.vector.tensor_tensor(in_need.rearrange("p (e b) -> p e b", b=NB),
                                        bank[2][:, 0:256].rearrange("p (e b) -> p e b", b=NB),
                                        need[:, :, None].to_broadcast([128, NE, NB]), ALU.is_lt
                                        ).then_inc(b3_in_need, 1)
                dve.wait_ge(b3_in_need, 1)
                link(dve, nc.vector.tensor_tensor(in_need, in_need, equal, ALU.mult))
                link(dve, nc.vector.tensor_tensor(taken, in_need, above, ALU.add))
                earlier_of(taken, 1)
                dve.wait_ge(b3_taken_ranked, 1)
                link(dve, nc.vector.scalar_tensor_tensor(place, bank[3][:, 0:256], 1.0, taken, ALU.add, ALU.mult))
                nc.vector.tensor_scalar(half[:, 1, :], place, 128.5, None, ALU.is_gt)
                link(dve, nc.vector.tensor_scalar(half[:, 0, :], place, 128.5, None, ALU.is_lt))
                nc.vector.scalar_tensor_tensor(low[:, :], half[:, 1, :], -128.0, place, ALU.mult, ALU.add)
                for n in range(2):
                    last = nc.vector.tensor_tensor(
                        halves[:, :, n].rearrange("p (e b) -> p e b", b=NB),
                        half[:, n, :].rearrange("p (e b) -> p e b", b=NB),
                        token_id[:, None, :].to_broadcast([128, NE, NB]), ALU.mult)

        e_onehot_ready = sem("e_onehot_ready")
        e_listed = sem("e_listed")
        e_list_row_ready = sem("e_list_row_ready")
        e_list_ready = sem("e_list_ready")
        e_gather_list_ready = sem("e_gather_list_ready")
        e_gathered = sem("e_gathered")
        e_transposed = sem("e_transposed")
        e_xT_ready = sem("e_xT_ready")
        e_up_ready = sem("e_up_ready")
        e_gelu_ready = sem("e_gelu_ready")
        e_hidden_ready = sem("e_hidden_ready")
        e_down_ready = sem("e_down_ready")
        e_weighed = sem("e_weighed")
        e_scattered = sem("e_scattered")
        x_reloaded = [sem(f"x_reloaded_{q}") for q in range(4)]
        e_pool_turns = sem("e_pool_turns")

        onehot = sb("onehot", [128, 2, NB, 128], F16)
        list_all = sb("list_all", [128, NE, 2], I32)
        gather_list = sb("gather_list", [128, 2], I32)
        scatter_list = sb("scatter_list", [128, 2, 2], I32)
        kept = sb("kept", [128, NE, 2])
        gathered = [view(stage, 0, 2, GROW), view(stage, 3232, 2, GROW)]
        xT = view(stage, 288, 256)
        gelu_e = view(stage, 544, NI, CAP)
        hidden_e = view(stage, 1568, NI, CAP)
        weighed = [view(stage, 2592 + 256 * p, 2, D) for p in range(2)]
        list_row = view(stage, 3104, 128)[0:2]
        DOWN_BANK = (5, 7)

        with nc.Block(no_gpsimd_drain=True) as block:
            @block.sync
            def _(sp):
                with sp.Fori(0, NE // SLOTS - 1) as g:
                    for slot in range(SLOTS):
                        sp.wait_ge(e_down_ready, g * SLOTS + slot + 1)
                        sp.dma_start(w_slots[:, slot], d["expert_w"][bass.ds(g * SLOTS + slot + SLOTS, 1)].rearrange(
                            "o p w i -> (o p) w i")).then_inc(expert_w_loaded[slot], 16)
                sp.wait_ge(e_scattered, 32 * NE)
                for q in range(4):
                    sp.dma_start(x_all[:, 4 * q:4 * q + 4, :], d["sums"][q * QT:(q + 1) * QT].rearrange(
                        "(b t) c -> t b c", b=4)).then_inc(x_reloaded[q], 16)

            @block.gpsimd
            def _(pool):
                pool.wait_ge(rows_stored, 16)
                pool.wait_ge(sums_stored, 16)

                def step(i, u):
                    e = i - 1
                    if live(e, NE):
                        pool.wait_ge(e_gather_list_ready, e + 1)
                        pool.sem_inc(e_pool_turns, 1)
                        for m in range(2):
                            nc.gpsimd.indirect_dma_start(
                                gathered[(u + 1) % 2][:, m, :], None, d["rows"],
                                bass.IndirectOffsetOnAxis(gather_list[:, m:m + 1], 0)).then_inc(e_gathered, 16)
                    e = i - 4
                    if live(e, NE):
                        pool.wait_ge(e_weighed, e + 1)
                        if live(e - 1, NE):
                            pool.wait_ge(e_scattered, 32 * e)
                        pool.sem_inc(e_pool_turns, 1)
                        for m in range(2):
                            nc.gpsimd.indirect_dma_start(
                                d["sums"], bass.IndirectOffsetOnAxis(scatter_list[:, u, m:m + 1], 0),
                                weighed[u][:, m, :], None, compute_op=ALU.add).then_inc(e_scattered, 16)

                skewed(pool, NE, 4, step, unroll=2)

            @block.tensor
            def _(pe):
                def step(i, u):
                    def down(ks):
                        for k in ks:
                            if k % 2 == 0:
                                pe.wait_ge(e_hidden_ready, 2 * (i - 3) + 1 + k // 2)
                            for m in range(2):
                                last = nc.tensor.matmul(bank[DOWN_BANK[m]][:, 0:D],
                                                        hidden_e[:, k, m * 128:(m + 1) * 128],
                                                        w_slots[:, (u - 3) % SLOTS, 2, k * 128:(k + 1) * 128],
                                                        start=(k == 0), stop=(k == NI - 1))
                        return last

                    e = i - 3
                    if live(e, NE):
                        pe.wait_ge(e_xT_ready, e + 1)
                        slot = (u - 3) % SLOTS
                        pe.wait_ge(expert_w_loaded[slot], 16 // SLOTS * (e - slot) + 16)
                        for s in range(2):
                            for which in range(2):
                                for k in range(2):
                                    c = 2 * s + k
                                    last = nc.tensor.matmul(
                                        bank[1 + s + 2 * which][:, k * 256:(k + 1) * 256],
                                        w_slots[:, slot, which, c * 128:(c + 1) * 128], xT, start=True, stop=True)
                            last.then_inc(e_up_ready, 1)
                    e = i - 1
                    if live(e, NE):
                        pe.wait_ge(e_onehot_ready, e + 1)
                        if live(e - 1, NE):
                            pe.wait_ge(e_gather_list_ready, e)
                        for b in range(NB):
                            last = nc.tensor.matmul(bank[6][0:2, 0:128], halves[:, bass.ds(e * NB + b, 1), :]
                                                    .rearrange("p o n -> p (o n)"), onehot[:, (u + 1) % 2, b, :],
                                                    start=(b == 0), stop=(b == NB - 1))
                        last.then_inc(e_listed, 1)
                    if live(i - 3, NE):
                        if live(i - 4, NE):
                            pe.wait_ge(e_weighed, i - 3)
                        down((0, 1))
                    e = i - 1
                    if live(e, NE):
                        pe.wait_ge(e_list_row_ready, e + 1)
                        nc.tensor.matmul(bank[6][:, 256:258], list_row, ident[0:2, 0:2], start=True, stop=True
                                         ).then_inc(e_list_ready, 1)
                    e = i - 2
                    if live(e, NE):
                        pe.wait_ge(e_gathered, 32 * e + 32)
                        for m in range(2):
                            last = nc.tensor.transpose(bank[0][:, m * 128:(m + 1) * 128], gathered[u % 2][:, m, 0:D], ident)
                        last.then_inc(e_transposed, 1)
                    if live(i - 3, NE):
                        down((2, 3)).then_inc(e_down_ready, 1)

                skewed(pe, NE, 4, step, unroll=SLOTS)

            @block.scalar
            def _(act):
                def step(i, u):
                    e = i - 3
                    if live(e, NE):
                        for s in range(2):
                            act.wait_ge(e_up_ready, 2 * e + 1 + s)
                            nc.scalar.activation(gelu_e[:, 2 * s:2 * s + 2, :],
                                                 bank[1 + s][:, :].rearrange("p (k t) -> p k t", k=2), ACT.Gelu
                                                 ).then_inc(e_gelu_ready, 1)
                    e = i - 1
                    if live(e, NE):
                        act.wait_ge(e_listed, e + 1)
                        nc.scalar.copy(list_row, bank[6][0:2, 0:128]).then_inc(e_list_row_ready, 1)
                    e = i - 2
                    if live(e, NE):
                        act.wait_ge(e_transposed, e + 1)
                        nc.scalar.copy(xT, bank[0][:, 0:256]).then_inc(e_xT_ready, 1)

                skewed(act, NE, 4, step)

            @block.vector
            def _(dve):
                def hidden(e, s):
                    dve.wait_ge(e_gelu_ready, 2 * e + 1 + s)
                    nc.vector.tensor_tensor(hidden_e[:, 2 * s:2 * s + 2, :], gelu_e[:, 2 * s:2 * s + 2, :],
                                            bank[3 + s][:, :].rearrange("p (k t) -> p k t", k=2), ALU.mult
                                            ).then_inc(e_hidden_ready, 1)

                def places(i, u, part):
                    for b in range(part * NB // 2, (part + 1) * NB // 2):
                        last = nc.vector.tensor_scalar(onehot[:, u, b, :], iota1, low[:, bass.ds(i * NB + b, 1)], None,
                                                       ALU.is_equal)
                    if part:
                        last.then_inc(e_onehot_ready, 1)

                def step(i, u):
                    e = i - 4
                    if live(e, NE):
                        dve.wait_ge(e_down_ready, e + 1)
                        if live(e - 2, NE):
                            dve.wait_ge(e_scattered, 32 * e - 32)
                        nc.vector.tensor_copy(scatter_list[:, u, :], list_all[:, e, :])
                        for m in range(2):
                            last = nc.vector.tensor_scalar(weighed[u][:, m, :], bank[DOWN_BANK[m]][:, 0:D],
                                                           kept[:, e, m:m + 1], None, ALU.mult)
                        last.then_inc(e_weighed, 1)
                    if live(i, NE):
                        places(i, u, 0)
                    if live(i - 3, NE):
                        hidden(i - 3, 0)
                    if live(i, NE):
                        places(i, u, 1)
                    if live(i - 3, NE):
                        hidden(i - 3, 1)
                    e = i - 2
                    if live(e, NE):
                        dve.wait_ge(e_gathered, 32 * e + 32)
                        nc.vector.tensor_copy(kept[:, e, :], gathered[u][:, :, bass.ds(e + D, 1)].rearrange("p m o -> p (m o)"))
                    e = i - 1
                    if live(e, NE):
                        dve.wait_ge(e_list_ready, e + 1)
                        nc.vector.tensor_copy(list_all[:, e, :], bank[6][:, 256:258])
                        nc.vector.tensor_copy(gather_list[:, :], bank[6][:, 256:258]).then_inc(e_gather_list_ready, 1)

                skewed(dve, NE, 6, step, unroll=2)
                blocks = wq4_in[:, :, :].rearrange("p m (n k) -> p (m n) k", k=WBLOCK)
                q4s3 = q4s[:, :, :].rearrange("p m (n k) -> p (m n) k", k=WBLOCK)
                link(dve, nc.vector.tensor_reduce(q4m, blocks, axis=AX.X, op=ALU.max, apply_absolute_value=True))
                link(dve, nc.vector.tensor_scalar(q4m, q4m, 1.0 / WMAX, TINY, ALU.mult, ALU.max))
                link(dve, nc.vector.reciprocal(q4i, q4m))
                link(dve, nc.vector.tensor_tensor(q4s3, blocks, q4i[:, :, None].to_broadcast([128, N_WBLOCKS, WBLOCK]),
                                                  ALU.mult))
                link(dve, nc.vector.tensor_scalar(q4s, q4s, ROUND, ROUND, ALU.add, ALU.subtract))
                nc.vector.tensor_tensor(q4s3, q4s3, q4m[:, :, None].to_broadcast([128, N_WBLOCKS, WBLOCK]), ALU.mult
                                        ).then_inc(q4_ready, 1)

        c_bn_done = sem("c_bn_done")
        c_moments = sem("c_moments")
        c_gain_ready = sem("c_gain_ready")
        c_transposed = sem("c_transposed")
        c_hT_by_vector = sem("c_hT_by_vector")
        c_hT_by_scalar = sem("c_hT_by_scalar")
        c_queried = sem("c_queried")
        c_qT_ready = sem("c_qT_ready")
        c_q4_copied = sem("c_q4_copied")
        c_bank_clear = sem("c_bank_clear")
        c_q_now_ready = sem("c_q_now_ready")
        c_keys_ready = sem("c_keys_ready")
        c_scored = sem("c_scored")
        c_max_ready = sem("c_max_ready")
        c_shifted = sem("c_shifted")
        c_weights_ready = sem("c_weights_ready")
        c_weights_transposed = sem("c_weights_transposed")
        c_wT_ready = sem("c_wT_ready")
        c_values_ready = sem("c_values_ready")
        c_mixed = sem("c_mixed")
        c_mixed_out = sem("c_mixed_out")
        c_out_transposed = sem("c_out_transposed")
        c_inv_ready = sem("c_inv_ready")
        c_out_ready = sem("c_out_ready")
        c_x_ready = sem("c_x_ready")
        c_x_bn_done = sem("c_x_bn_done")

        masked_rstd = view(stage, 0, NB)
        masked_shift = view(stage, 16, NB)
        q_now = view(stage, 32, 128)
        out1 = view(stage, 160, H1, DH1)
        max1 = view(stage, 288, H1)
        inv1 = view(stage, 304, H1)
        keys_now = view(stage, 320, QUAD, CK)
        mixed_s = view(stage, 640, 512)
        values_now = view(stage, 1152 + 2 * H1 * CK, H1, DH1 + 1)[0:CK]
        weights1 = [view(stage, 1152, H1 * CK), view(stage, 1152 + H1 * CK, H1 * CK)]
        wT1 = sb("wT1", [CK, H1, 128])
        wT_bank = [bank[4], bank[5], bank[6], bank[4]]

        with nc.Block(no_gpsimd_drain=True) as block:
            @block.gpsimd
            def _(pool):
                def step(i, u):
                    if live(i, NB):
                        if live(i - 1, NB):
                            pool.wait_ge(c_scored, 4 * i)
                        nc.gpsimd.tensor_tensor(keys_now, keys1[:, i, None, :].to_broadcast([128, QUAD, CK]),
                                                head_of_row[:, :, None].to_broadcast([128, QUAD, CK]), ALU.mult
                                                ).then_inc(c_keys_ready, 1)
                    b = i - 2
                    if live(b, NB):
                        if live(b - 1, NB):
                            pool.wait_ge(c_mixed, b)
                        nc.gpsimd.tensor_copy(values_now, values1[:, b, :, :]).then_inc(c_values_ready, 1)

                skewed(pool, NB, 2, step)

            @block.tensor
            def _(pe):
                pe.wait_ge(q4_ready, 1)
                for m in range(3):
                    for c in range(NQ):
                        last = nc.tensor.transpose(bank[m][:, c * 128:(c + 1) * 128], q4s[:, m, c * 128:(c + 1) * 128],
                                                   ident)
                    last.then_inc(q4_transposed, 1)
                def query(g):
                    pe.wait_ge(c_hT_by_vector if g < 2 else c_hT_by_scalar, g % 2 + 1)
                    nc.tensor.matmul(bank[4 + g][:, :], wq1[:, :], hT_all[:, quarter(g)], start=True, stop=True
                                     ).then_inc(c_queried, 1)

                for g in range(4):
                    wait_normed(pe, 1, g)
                    if g:
                        pe.wait_ge(c_q4_copied, g)
                    transposed_rows(g, bank[(g + 3) % 4], c_transposed)
                    if g:
                        query(g - 1)
                query(3)

                def step(i, u):
                    b = i - 1
                    if live(b, NB):
                        pe.wait_ge(c_q_now_ready, b + 1)
                        pe.wait_ge(c_keys_ready, b + 1)
                        for g in range(QUAD):
                            if live(b - 1, NB):
                                pe.wait_ge(c_shifted, 4 * b + g - 3)
                            r = slice(32 * g, 32 * g + 32)
                            nc.tensor.matmul(bank[g][:, 0:QUAD * CK], q_now[r, :],
                                             keys_now[r].rearrange("p j k -> p (j k)"), start=True, stop=True,
                                             tile_position=(32 * g, 0)).then_inc(c_scored, 1)
                    b = i - 4
                    if live(b, NB):
                        pe.wait_ge(c_mixed_out, b + 1)
                        if live(i - 3, NB):
                            pe.wait_ge(c_wT_ready, 4 * i - 9)
                        if live(b - 1, NB):
                            pe.wait_ge(c_out_ready, b)
                        for g in range(QUAD):
                            last = nc.tensor.transpose(bank[6][:, g * 128:(g + 1) * 128], mixed_s[:, g * 128:(g + 1) * 128],
                                                       ident)
                        last.then_inc(c_out_transposed, 1)
                    b = i - 3
                    if live(b, NB):
                        pe.wait_ge(c_wT_ready, 4 * b + 4)
                        pe.wait_ge(c_values_ready, b + 1)
                        if live(b - 1, NB):
                            pe.wait_ge(c_mixed_out, b)
                        for g in range(QUAD):
                            for j in range(QUAD):
                                h = g * QUAD + j
                                last = nc.tensor.matmul(bank[7][32 * j:32 * j + DH1 + 1, g * 128:(g + 1) * 128],
                                                        values_now[:, h, :],
                                                        wT1[:, h, :], start=True, stop=True, tile_position=(0, 32 * j))
                        last.then_inc(c_mixed, 1)
                    b = i - 2
                    if live(b, NB):
                        pe.wait_ge(c_weights_ready, b + 1)
                        if isinstance(b, int) and b == 0:
                            pe.wait_ge(c_bank_clear, 1)
                        for g in range(QUAD):
                            if g == 2 and live(i - 4, NB):
                                pe.wait_ge(c_out_ready, i - 3)
                            if g == 3:
                                pe.wait_ge(c_wT_ready, 4 * b + 1)
                            for j in range(QUAD):
                                h = g * QUAD + j
                                last = nc.tensor.transpose(wT_bank[g][0:CK, j * 128:(j + 1) * 128],
                                                           weights1[u % 2][:, h * CK:(h + 1) * CK], ident)
                            last.then_inc(c_weights_transposed, 1)

                skewed(pe, NB, 4, step, unroll=4)

            @block.scalar
            def _(act):
                for m in range(3):
                    act.wait_ge(q4_transposed, m + 1)
                    nc.scalar.copy(wq4[:, m, :], bank[m][:, 0:IQ]).then_inc(c_q4_copied, 1)
                batched_rstd(2, None, act, NB)
                act.wait_ge(c_gain_ready, 1)
                normed(nc.scalar, masked_rstd, masked_shift)
                for g in (2, 3):
                    act.wait_ge(c_transposed, g + 1)
                    nc.scalar.copy(hT_all[:, quarter(g)], bank[(g + 3) % 4][:, :]).then_inc(c_hT_by_scalar, 1)

                def step(i, u):
                    if live(i, NB):
                        if isinstance(i, int) and i == 0:
                            act.wait_ge(c_qT_ready, 1)
                        else:
                            act.wait_ge(c_scored, 4 * i)
                        nc.scalar.copy(q_now, hT_all[:, bass.ds(i * T, T)]).then_inc(c_q_now_ready, 1)
                    b = i - 2
                    if live(b, NB):
                        for g in range(QUAD):
                            act.wait_ge(c_weights_transposed, 4 * b + g + 1)
                            nc.scalar.copy(wT1[:, g * QUAD:(g + 1) * QUAD, :],
                                           wT_bank[g][0:CK, :].rearrange("p (j q) -> p j q", j=QUAD)
                                           ).then_inc(c_wT_ready, 1)
                    b = i - 3
                    if live(b, NB):
                        act.wait_ge(c_mixed, b + 1)
                        if live(b - 1, NB):
                            act.wait_ge(c_out_transposed, b)
                        nc.scalar.copy(mixed_s, bank[7][:, :]).then_inc(c_mixed_out, 1)
                    b = i - 1
                    if live(b, NB):
                        act.wait_ge(c_shifted, 4 * b + 4)
                        nc.scalar.activation(weights1[(u + 1) % 2], weights1[(u + 1) % 2], ACT.Exp
                                             ).then_inc(c_weights_ready, 1)

                skewed(act, NB, 4, step, unroll=2)
                batched_rstd(3, None, act, NB)

            @block.vector
            def _(dve):
                for q in range(4):
                    dve.wait_ge(x_reloaded[q], 16)
                    for b in range(4 * q, 4 * q + 4):
                        nc.vector.bn_stats(bn[:, b, :], x_all[:, b, :]).then_inc(c_bn_done, 1)
                    if q:
                        dve.wait_ge(c_bn_done, 4 * q)
                        for b in range(4 * q - 4, 4 * q):
                            nc.vector.bn_aggr(moments[:, b, :], bn[:, b, :])
                dve.wait_ge(c_bn_done, NB)
                for b in range(NB - 4, NB):
                    last = nc.vector.bn_aggr(moments[:, b, :], bn[:, b, :])
                last.then_inc(c_moments, 1)
                dve.wait_ge(c_moments, 1)
                batched_rstd(2, dve, None, NB)
                dve.wait_ge(shift_ready, 3)
                nc.vector.tensor_tensor(masked_rstd, rstd[:, 0:NB], mask_q[:, :], ALU.mult)
                nc.vector.tensor_tensor(masked_shift, shift[:, 0:NB], mask_q[:, :], ALU.mult).then_inc(c_gain_ready, 1)
                dve.wait_ge(c_gain_ready, 1)
                normed(nc.vector, masked_rstd, masked_shift)
                for g in (0, 1):
                    dve.wait_ge(c_transposed, g + 1)
                    nc.vector.tensor_copy(hT_all[:, quarter(g)], bank[(g + 3) % 4][:, :]).then_inc(c_hT_by_vector, 1)
                for g in range(4):
                    dve.wait_ge(c_queried, g + 1)
                    nc.vector.tensor_scalar(hT_all[:, quarter(g)], bank[4 + g][:, :], DH1 ** -0.5, None, ALU.mult
                                            ).then_inc(c_qT_ready, 1)

                def step(i, u):
                    b = i - 1
                    if live(b, NB):
                        if live(b - 2, NB):
                            dve.wait_ge(c_weights_transposed, 4 * b - 4)
                    def largest(g):
                        if live(b, NB):
                            dve.wait_ge(c_scored, 4 * b + g + 1)
                            nc.vector.tensor_reduce(
                                max1[:, g * QUAD:(g + 1) * QUAD], bank[g][:, 0:QUAD * CK].rearrange(
                                    "p (j k) -> p j k", j=QUAD), axis=AX.X, op=ALU.max).then_inc(c_max_ready, 1)

                    def shifted(g):
                        if live(b, NB):
                            dve.wait_ge(c_max_ready, 4 * b + g + 1)
                            nc.vector.tensor_tensor(
                                weights1[(u + 1) % 2][:, g * QUAD * CK:(g + 1) * QUAD * CK].rearrange(
                                    "p (j k) -> p j k", j=QUAD),
                                bank[g][:, 0:QUAD * CK].rearrange("p (j k) -> p j k", j=QUAD),
                                max1[:, g * QUAD:(g + 1) * QUAD, None].to_broadcast([128, QUAD, CK]), ALU.subtract
                                ).then_inc(c_shifted, 1)

                    done = i - 4
                    o = bank[6][:, :].rearrange("p (h e) -> p h e", h=H1)
                    largest(0)
                    largest(1)
                    shifted(0)
                    largest(2)
                    shifted(1)
                    largest(3)
                    if live(done, NB):
                        dve.wait_ge(c_out_transposed, done + 1)
                        nc.vector.reciprocal(inv1, o[:, :, DH1]).then_inc(c_inv_ready, 1)
                    shifted(2)
                    if live(done, NB):
                        dve.wait_ge(c_inv_ready, done + 1)
                        nc.vector.tensor_tensor(out1, o[:, :, 0:DH1], inv1[:, :, None].to_broadcast([128, H1, DH1]),
                                                ALU.mult).then_inc(c_out_ready, 1)
                    shifted(3)
                    if live(done, NB):
                        dve.wait_ge(c_out_ready, done + 1)
                        nc.vector.tensor_tensor(x_all[:, done, :], x_all[:, done, :], out1.rearrange("p h e -> p (h e)"),
                                                ALU.add).then_inc(c_x_ready, 1)
                        dve.wait_ge(c_x_ready, done + 1)
                        nc.vector.bn_stats(bn[:, done, :], x_all[:, done, :]).then_inc(c_x_bn_done, 1)

                    if isinstance(i, int) and i == 1:
                        dve.wait_ge(c_qT_ready, 4)
                        nc.vector.memset(bank[7][:, :], 0.0).then_inc(c_bank_clear, 1)

                skewed(dve, NB, 4, step, unroll=2)
                dve.wait_ge(c_x_bn_done, NB)
                for b in range(NB):
                    last = nc.vector.bn_aggr(moments[:, b, :], bn[:, b, :])
                link(dve, last)
                batched_rstd(3, dve, None, NB)

        d_h_part = sem("d_h_part")
        d_transposed = sem("d_transposed")
        d_max_ready = sem("d_max_ready")
        d_all_max = sem("d_all_max")
        d_factor_ready = sem("d_factor_ready")
        d_h_raised = sem("d_h_raised")
        d_h_ints = sem("d_h_ints")
        d_projected = sem("d_projected")
        d_copied = sem("d_copied")
        d_gate_part = sem("d_gate_part")
        d_up_part = sem("d_up_part")
        d_gate_ints = sem("d_gate_ints")
        d_sigmoid_ready = sem("d_sigmoid_ready")
        d_sigmoid_raised = sem("d_sigmoid_raised")
        d_sigmoid_shifted = sem("d_sigmoid_shifted")
        d_pool_float = sem("d_pool_float")
        d_pool_product = sem("d_pool_product")
        d_product_part = sem("d_product_part")
        d_up_ints = sem("d_up_ints")
        d_t_ints = sem("d_t_ints")
        d_o_part = sem("d_o_part")
        d_o_raised = sem("d_o_raised")
        d_o_ints = sem("d_o_ints")
        d_down = sem("d_down")
        d_y_ready = sem("d_y_ready")
        y_stored = sem("y_stored")

        own_max = view(stage, 0, 8)
        all_max = view(stage, 8, 8)
        scale = view(stage, 16, 8)
        inv_scale = view(stage, 24, 8)
        factor = view(stage, 32, 8)
        unit = view(stage, 40, 8)
        round_up, round_back = view(stage, 48, 1), view(stage, 49, 1)
        raise_sig, lower_sig = view(stage, 50, 1), view(stage, 51, 1)
        part_max = view(stage, 64, 2, 12)
        gate_flat = gate_all[:, :, :].rearrange("p c t -> p (c t)")
        up_all = qkv[:, :, :].rearrange("p b c -> p (b c)")
        up3 = up_all.rearrange("p (c t) -> p c t", c=NQ)
        gate_ints = view(stage, 1024, NQ * NT // 2).bitcast(I16)
        up_ints, t_ints = (gate_flat[:, n * NQ * NT // 2:(n + 1) * NQ * NT // 2].bitcast(I16) for n in range(2))
        sig3 = sig_all[:, :].rearrange("p (c t) -> p c t", c=NQ)
        hq = hT_all
        PIECES = 4 * NQ
        PX, PG, PU, PT, PO = range(5)

        def chunk(c):
            return slice(c * NT, (c + 1) * NT)

        last_chunk = chunk(NQ - 1)
        sig_last = sig_all[:, last_chunk]

        with nc.Block(no_gpsimd_drain=True) as block:
            @block.gpsimd
            def _(pool):
                for n in range(5):
                    if n == PT:
                        pool.wait_ge(d_gate_ints, NQ)
                        nc.gpsimd.tensor_copy(gate_flat[:, last_chunk], gate_ints[:, last_chunk]).then_inc(d_pool_float, 1)
                        pool.wait_ge(d_pool_float, 1)
                        pool.wait_ge(d_sigmoid_shifted, 2)
                        nc.gpsimd.tensor_tensor(sig_last, sig_last, gate_flat[:, last_chunk], ALU.mult
                                                ).then_inc(d_pool_product, 1)
                    if n == PO:
                        pool.wait_ge(d_up_ints, NQ + 1)
                        pool.wait_ge(d_t_ints, 2)
                        nc.gpsimd.tensor_tensor(sig_last, sig_last, up_all[:, last_chunk], ALU.mult
                                                ).then_inc(d_pool_product, 1)
                    pool.wait_ge(d_max_ready, n + 1)
                    nc.gpsimd.partition_all_reduce(all_max[:, n:n + 1], own_max[:, n:n + 1], 128, bass.bass_isa.ReduceOp.max
                                                   ).then_inc(d_all_max, 1)

            @block.tensor
            def _(pe):
                for q in range(4):
                    wait_normed(pe, 2, q)
                    transposed_rows(q, bank[q], d_transposed)
                for k in range(2 * PIECES):
                    which, q, c = k // PIECES, k % PIECES // NQ, k % NQ
                    if which == 0 and c == 0:
                        pe.wait_ge(d_h_ints, q + 1)
                    if k >= 4:
                        pe.wait_ge(d_copied, k - 3)
                    nc.tensor.matmul(bank[4 + k % 4][:, :], wq4[:, which, c * 128:(c + 1) * 128], hq[:, quarter(q)],
                                     start=True, stop=True).then_inc(d_projected, 1)
                for q in range(4):
                    pe.wait_ge(d_o_ints, q + 1)
                    for j in range(4):
                        for c in range(NQ):
                            last = nc.tensor.matmul(bank[q][:, j * T:(j + 1) * T],
                                                    sig3[:, c, q * QT + j * T:q * QT + (j + 1) * T],
                                                    wq4[:, 2, c * 128:(c + 1) * 128], start=(c == 0), stop=(c == NQ - 1))
                    last.then_inc(d_down, 1)

            @block.scalar
            def _(act):
                act.wait_ge(shift_ready, 4)
                normed(nc.scalar, rstd, shift)
                act.wait_ge(d_factor_ready, PX + 1)
                for q in range(4):
                    act.wait_ge(d_transposed, q + 1)
                    nc.scalar.activation(hq[:, quarter(q)], bank[q][:, :], ACT.Identity, bias=round_up,
                                         scale=factor[:, PX:PX + 1]).then_inc(d_h_raised, 1)

                def copied(k):
                    which, q, c = k // PIECES, k % PIECES // NQ, k % NQ
                    act.wait_ge(d_projected, k + 1)
                    nc.scalar.copy((gate_all, up3)[which][:, c, quarter(q)], bank[4 + k % 4][:, :]).then_inc(d_copied, 1)

                for k in range(2 * PIECES):
                    copied(k)
                    if k - PIECES in (4, 8, 11):
                        c = {4: 0, 8: 1, 11: 2}[k - PIECES]
                        act.wait_ge(d_gate_ints, c + 1)
                        nc.scalar.activation(sig_all[:, chunk(c)], gate_ints[:, chunk(c)], ACT.Sigmoid,
                                             scale=scale[:, PG:PG + 1]).then_inc(d_sigmoid_ready, 1)
                s1, s2 = sig_all[:, chunk(1)], sig_all[:, chunk(2)]
                act.wait_ge(d_sigmoid_ready, 2)
                nc.scalar.activation(s1, s1, ACT.Identity, bias=raise_sig).then_inc(d_sigmoid_shifted, 1)
                act.wait_ge(d_sigmoid_raised, 1)
                nc.scalar.activation(s2, s2, ACT.Identity, bias=lower_sig).then_inc(d_sigmoid_shifted, 1)
                act.wait_ge(d_sigmoid_shifted, 1)
                nc.scalar.activation(s1, s1, ACT.Identity, bias=lower_sig).then_inc(d_sigmoid_shifted, 1)
                act.wait_ge(d_factor_ready, PU + 1)
                for c in range(NQ):
                    nc.scalar.activation(up_ints[:, chunk(c)], up_all[:, chunk(c)], ACT.Copy,
                                         scale=factor[:, PU:PU + 1]).then_inc(d_up_ints, 1)
                act.wait_ge(d_up_ints, NQ)
                nc.scalar.copy(up_all[:, last_chunk], up_ints[:, last_chunk]).then_inc(d_up_ints, 1)
                act.wait_ge(d_factor_ready, PT + 1)
                for c in (2, 1):
                    nc.scalar.activation(t_ints[:, chunk(c)], sig_all[:, chunk(c)], ACT.Copy,
                                         scale=factor[:, PT:PT + 1]).then_inc(d_t_ints, 1)
                    if c == 2:
                        act.wait_ge(d_t_ints, 1)
                        nc.scalar.copy(sig_last, t_ints[:, last_chunk]).then_inc(d_t_ints, 1)
                for q in range(4):
                    act.wait_ge(d_o_raised, q + 1)
                    nc.scalar.activation(sig3[:, :, quarter(q)], sig3[:, :, quarter(q)], ACT.Identity, bias=round_back
                                         ).then_inc(d_o_ints, 1)

            @block.vector
            def _(dve):
                def new_scale(n, parts, unit, meanwhile=None):
                    nc.vector.tensor_reduce(own_max[:, n:n + 1], parts, axis=AX.X, op=ALU.max).then_inc(d_max_ready, 1)
                    if meanwhile is not None:
                        meanwhile()
                    dve.wait_ge(d_all_max, n + 1)
                    col = slice(n, n + 1)
                    if unit is None:
                        link(dve, nc.vector.tensor_scalar(scale[:, col], all_max[:, col], 1.0 / QMAX, TINY,
                                                          ALU.mult, ALU.max))
                        link(dve, nc.vector.reciprocal(factor[:, col], scale[:, col]))
                    else:
                        link(dve, nc.vector.tensor_scalar(scale[:, col], all_max[:, col], unit, 1.0 / QMAX,
                                                          ALU.mult, ALU.mult))
                        link(dve, nc.vector.tensor_scalar(scale[:, col], scale[:, col], TINY, None, ALU.max))
                        link(dve, nc.vector.reciprocal(inv_scale[:, col], scale[:, col]))
                        link(dve, nc.vector.tensor_tensor(factor[:, col], inv_scale[:, col], unit, ALU.mult))
                    dve.sem_inc(d_factor_ready, 1)

                def part(which, n, src, signal):
                    nc.vector.tensor_reduce(part_max[:, which, n:n + 1], src, axis=AX.X, op=ALU.max,
                                            apply_absolute_value=True).then_inc(signal, 1)

                nc.vector.memset(round_up, ROUND)
                nc.vector.memset(round_back, -ROUND)
                nc.vector.memset(raise_sig, 192.0)
                nc.vector.memset(lower_sig, -192.0)
                dve.wait_ge(shift_ready, 4)
                normed(nc.vector, rstd, shift)
                for q in range(4):
                    wait_normed(dve, 2, q)
                    nc.vector.tensor_reduce(part_max[:, 0, q:q + 1], h_rows[:, 4 * q:4 * q + 4, :], axis=AX.XY, op=ALU.max,
                                            apply_absolute_value=True).then_inc(d_h_part, 1)
                dve.wait_ge(d_h_part, 4)
                new_scale(PX, part_max[:, 0, 0:4], None)
                for q in range(4):
                    dve.wait_ge(d_h_raised, q + 1)
                    nc.vector.tensor_scalar(hq[:, quarter(q)], hq[:, quarter(q)], ROUND, None, ALU.subtract
                                            ).then_inc(d_h_ints, 1)
                for k in range(PIECES):
                    dve.wait_ge(d_copied, k + 1)
                    part(0, k, gate_all[:, k % NQ, quarter(k // NQ)], d_gate_part)
                dve.wait_ge(d_gate_part, PIECES)
                new_scale(PG, part_max[:, 0, :], scale[:, PX:PX + 1])
                for c in range(NQ):
                    nc.vector.tensor_scalar(gate_ints[:, chunk(c)], gate_flat[:, chunk(c)], factor[:, PG:PG + 1], None,
                                            ALU.mult).then_inc(d_gate_ints, 1)
                for k in range(PIECES):
                    dve.wait_ge(d_copied, PIECES + k + 1)
                    part(1, k, up3[:, k % NQ, quarter(k // NQ)], d_up_part)
                dve.wait_ge(d_up_part, PIECES)

                def raised(c):
                    dve.wait_ge(d_sigmoid_ready, c + 1)
                    nc.vector.tensor_scalar(sig_all[:, chunk(c)], sig_all[:, chunk(c)], 65535.0 / 65536.0, 192.0,
                                            ALU.min, ALU.add).then_inc(d_sigmoid_raised, 1)

                def both_raised():
                    raised(2)
                    raised(0)

                new_scale(PU, part_max[:, 1, :], scale[:, PX:PX + 1], both_raised)
                for c in range(NQ):
                    s, g = sig_all[:, chunk(c)], gate_ints[:, chunk(c)]
                    if c == 0:
                        dve.wait_ge(d_sigmoid_raised, 2)
                        link(dve, nc.vector.scalar_tensor_tensor(s, s, 192.0, g, ALU.subtract, ALU.mult))
                    elif c == 1:
                        dve.wait_ge(d_sigmoid_shifted, 3)
                        link(dve, nc.vector.scalar_tensor_tensor(s, s, 65535.0 / 65536.0, g, ALU.min, ALU.mult))
                    else:
                        dve.wait_ge(d_pool_product, 1)
                    part(0, c, s, d_product_part)
                dve.wait_ge(d_product_part, NQ)
                new_scale(PT, part_max[:, 0, 0:NQ], scale[:, PG:PG + 1])
                link(dve, nc.vector.tensor_scalar(t_ints[:, chunk(0)], sig_all[:, chunk(0)], factor[:, PT:PT + 1], None,
                                                  ALU.mult))
                for c in range(NQ):
                    s = sig_all[:, chunk(c)]
                    if c < 2:
                        dve.wait_ge(d_up_ints, c + 1)
                        if c == 1:
                            dve.wait_ge(d_t_ints, 3)
                        link(dve, nc.vector.tensor_tensor(s, up_ints[:, chunk(c)], t_ints[:, chunk(c)], ALU.mult))
                    else:
                        dve.wait_ge(d_pool_product, 2)
                    part(1, c, s, d_o_part)
                dve.wait_ge(d_o_part, NQ)
                link(dve, nc.vector.tensor_tensor(unit[:, 0:1], scale[:, PT:PT + 1], scale[:, PU:PU + 1], ALU.mult))
                new_scale(PO, part_max[:, 1, 0:NQ], unit[:, 0:1])
                for q in range(4):
                    o = sig3[:, :, quarter(q)]
                    nc.vector.tensor_scalar(o, o, factor[:, PO:PO + 1], ROUND, ALU.mult, ALU.add).then_inc(d_o_raised, 1)
                for q in range(4):
                    dve.wait_ge(d_down, q + 1)
                    x4 = x_all[:, 4 * q:4 * q + 4, :]
                    nc.vector.scalar_tensor_tensor(x4, bank[q][:, :].rearrange("p (b d) -> p b d", b=4),
                                                   scale[:, PO:PO + 1], x4, ALU.mult, ALU.add).then_inc(d_y_ready, 1)

            @block.sync
            def _(sp):
                for g in range(4):
                    sp.wait_ge(d_y_ready, g + 1)
                    sp.dma_start(d["out"][4 * g:4 * g + 4].rearrange("b t d -> t b d"), x_all[:, 4 * g:4 * g + 4, :]
                                 ).then_inc(y_stored, 16)
                sp.wait_ge(y_stored, 64)


def kernel(**inputs):
    import ml_dtypes
    import numpy as np
    from concourse import bacc, mybir
    from concourse.bass_utils import run_bass_kernel_spmd

    a = {k: np.asarray(v) for k, v in inputs.items()}
    k = np.arange(128)
    eye = np.eye(128, dtype=np.float32)
    units = np.array([4 ** (ROUNDS - 1 - n) for n in range(ROUNDS)], np.int32)
    const = np.concatenate([
        eye,
        ((k[:, None] % 32) // DH1 == np.arange(QUAD)[None, :]).astype(np.float32),
        np.tile(units.astype(np.float32), (128, 1)),
        (np.arange(NB)[None, :] * T + k[:, None]).astype(np.float32),
        np.tile((np.arange(NE * NB) % NB != 0).astype(np.float32), (128, 1)),
    ], axis=1)
    const16 = np.concatenate([
        (k[:, None] < k[None, :]).astype(np.float32),
        np.ones((128, 128), np.float32),
        (k[:, None] % NE == k[None, :] % NE).astype(np.float32),
        np.tile((k + 1).astype(np.float32), (128, 1)),
    ], axis=1).astype(ml_dtypes.bfloat16)
    patterns = np.tile((units[:, None] * np.arange(1, 4, dtype=np.int32)[None, :]).reshape(1, -1), (128, 1))
    columns = np.zeros((128, 8), np.float32)
    columns[:, 0], columns[:, 1] = a["L0_xattn_ln_l_g"], a["L0_xattn_ln_l_b"]
    columns[:CD, 2], columns[:CD, 3] = a["L0_xattn_ln_x_g"], a["L0_xattn_ln_x_b"]
    columns[:, 4], columns[:, 5] = np.tile(a["L0_xattn_qn_g"], H0), np.tile(a["L0_xattn_kn_g"], H0)

    def chunks(w):
        return np.ascontiguousarray(w.reshape(-1, 128, w.shape[1]).transpose(1, 0, 2))

    arrays = {
        "x": a["x"], "context": a["ctx_768"], "context_t": a["ctx_768"].transpose(2, 0, 1),
        "mask_k": a["mask_BxS2_bk0"].reshape(-1), "mask_q": a["mask_BxS_bk0"].T,
        "const": const, "const16": const16, "patterns": patterns, "columns": columns,
        "w_token": np.concatenate([a["L0_xattn_Wq"], a["L0_xattn_Wlkv"]]).T,
        "w_context": a["L0_xattn_Wkv"].T, "w_out": a["L0_xattn_Wo"].T, "bias_out": a["L0_xattn_bo"],
        "wq1": a["L1_xattn_Wq"].T, "wkv1": a["L1_xattn_Wkv"].T, "gate_w": a["L0_ffn_gate_w"].T,
        "shared_up": np.stack([a["L0_ffn_Sg"].T, a["L0_ffn_Su"].T], axis=1),
        "shared_down": chunks(a["L0_ffn_Sd"].T),
        "expert_w": np.stack([a["L0_ffn_Wg"].transpose(0, 2, 1), a["L0_ffn_Wu"].transpose(0, 2, 1),
                              a["L0_ffn_Wd"].transpose(0, 2, 1).reshape(NE, NI, 128, 128).transpose(0, 2, 1, 3)
                              .reshape(NE, 128, IE)], axis=2),
        "w_gate": a["L1_ffn_w_gate"], "w_up": a["L1_ffn_w_up"], "w_down": a["L1_ffn_w_down"],
    }
    nc = bacc.Bacc("TRN2", target_bir_lowering=False, num_devices=1)
    dram = {}
    for name, v in arrays.items():
        arrays[name] = v = np.ascontiguousarray(v)
        dram[name] = nc.dram_tensor(f"in_{name}", v.shape, mybir.dt.from_np(v.dtype), kind="ExternalInput").ap()
    dram["rows"] = nc.dram_tensor("rows", (NT, GROW), mybir.dt.float32).ap()
    dram["sums"] = nc.dram_tensor("sums", (NT, D), mybir.dt.float32).ap()
    dram["out"] = nc.dram_tensor("out", (NB, T, D), mybir.dt.float32, kind="ExternalOutput").ap()
    build(nc, dram)
    r = run_bass_kernel_spmd(nc, [{f"in_{name}": v for name, v in arrays.items()}], core_ids=[0])
    return r.results[0]["out"]
```
